# Optimizing a Trainium2 kernel written in Bass

```python
import numpy as np
import jax
import jax.numpy as jnp

def _softmax(x, axis=-1):
    return jax.nn.softmax(x, axis=axis)

def _gelu(x):
    return jax.nn.gelu(x, approximate=True)

def _silu(x):
    return jax.nn.silu(x)

def _sigmoid(x):
    return jax.nn.sigmoid(x)

def _layernorm(x, axis=-1, eps=1e-05):
    m = jnp.mean(x, axis=axis, keepdims=True)
    v = jnp.var(x, axis=axis, keepdims=True)
    return (x - m) / jnp.sqrt(v + eps)

def _scatter_add(tgt, idx, src, axis=0):
    return tgt.at[idx].add(src)

def _segment_sum(src, seg, n):
    return jax.ops.segment_sum(src, seg, n)
kernel_name = 'mk_flamingo_gated_d1_seqx_r4_b8ffee'

def setup_inputs(seed: int=0):
    np.random.seed(seed)
    _w = jnp.asarray

    def _rec_inputs():
        import jax
        import jax.numpy as jnp
        _rk = jax.random.key(seed)
        x = -0.0003929 + 0.9999 * jax.random.normal(jax.random.fold_in(_rk, 1), (16, 128, 1024), jnp.float32)
        _lenS = 128 - jax.random.randint(jax.random.fold_in(_rk, 7), (16,), 0, max(1, 128 // 4) + 1, jnp.int32)
        _lenS2 = 128 - jax.random.randint(jax.random.fold_in(_rk, 8), (16,), 0, max(1, 128 // 4) + 1, jnp.int32)
        _ctx_4096P = jax.random.normal(jax.random.fold_in(_rk, 11), (16, 16, 1024), jnp.float32)
        _ctx_4096c = jax.random.dirichlet(jax.random.fold_in(_rk, 511), 0.3 * jnp.ones((16,), jnp.float32), (16, 128))
        _ctx_4096t = jnp.einsum('bsk,bkd->bsd', _ctx_4096c, _ctx_4096P)
        _ctx_4096t = _ctx_4096t * jax.lax.rsqrt(jnp.mean(jnp.square(_ctx_4096t)) + 1e-12) * 0.953939
        ctx_4096 = 2.81802e-05 + 1.00001 * (_ctx_4096t + 0.3 * jax.random.normal(jax.random.fold_in(_rk, 611), (16, 128, 1024), jnp.float32))
        _g = jax.random.normal(jax.random.fold_in(_rk, 9001), (2, 1), jnp.float32)
        _g = jnp.sign(_g) * jnp.maximum(jnp.abs(_g), 1.0) + (_g == 0) * 1.0
        g_xattn = _g[0]
        g_ffn = _g[1]
        return (x, ctx_4096, g_xattn, g_ffn)
    x, ctx_4096, g_xattn, g_ffn = _rec_inputs()

    def _L0_xattn_setup():
        import jax, jax.numpy as jnp
        import numpy as np
        EPS = 1e-08

        def _cosine_sim(a, b):
            na = jnp.maximum(jnp.sqrt(jnp.sum(a * a, axis=1)), EPS)
            nb = jnp.maximum(jnp.sqrt(jnp.sum(b * b, axis=1)), EPS)
            return jnp.sum(a * b, axis=1) / (na * nb)
        key = jax.random.key(seed)
        k1, k2, k3 = jax.random.split(key, 3)
        B, C, T, O, K = (8, 128, 1024, 128, 3)
        feature = jax.random.normal(k1, (B, C, T), dtype=jnp.float32)
        embedding = jax.random.normal(k2, (B, C, T), dtype=jnp.float32)
        weight = jax.random.normal(k3, (O, C, K), dtype=jnp.float32) * 0.05
        return {'feature': feature, 'embedding': embedding, 'weight': weight}
    _L0_xattn_all = _L0_xattn_setup()
    _L0_xattn_in = {k: v for k, v in _L0_xattn_all.items() if k in ('weight',)}
    del _L0_xattn_all

    def _L0_ffn_setup():
        import jax, jax.numpy as jnp
        import numpy as np
        HID, INT, LAT, NE, K = (1024, 2048, 512, 8, 2)
        LN_EPS = 1e-05

        def _layernorm(x, gamma, beta):
            mu = jnp.mean(x, axis=-1, keepdims=True)
            var = jnp.var(x, axis=-1, keepdims=True)
            return (x - mu) * jax.lax.rsqrt(var + LN_EPS) * gamma + beta
        key = jax.random.key(seed)
        ks = jax.random.split(key, 8)
        s = lambda d: 1.0 / np.sqrt(d)
        return {'hidden_states': jax.random.normal(ks[0], (4, 512, HID), jnp.float32), 'gate_w': jax.random.normal(ks[1], (HID, NE), jnp.float32) * s(HID), 'up_w': jax.random.normal(ks[2], (HID, INT), jnp.float32) * s(HID), 'down_w': jax.random.normal(ks[3], (INT, HID), jnp.float32) * s(INT), 'fc1_w': jax.random.normal(ks[4], (HID, LAT), jnp.float32) * s(HID), 'fc2_w': jax.random.normal(ks[5], (LAT, HID), jnp.float32) * s(LAT), 'expert_w': jax.random.normal(ks[6], (LAT, LAT), jnp.float32), 'ln_gamma': jnp.ones((HID,), jnp.float32), 'ln_beta': jnp.zeros((HID,), jnp.float32)}
    _L0_ffn_all = _L0_ffn_setup()
    _L0_ffn_in = {k: v for k, v in _L0_ffn_all.items() if k in ('gate_w', 'up_w', 'down_w', 'fc1_w', 'fc2_w', 'expert_w', 'ln_gamma', 'ln_beta')}
    del _L0_ffn_all
    return {'x': x, 'ctx_4096': ctx_4096, 'g_xattn': g_xattn, 'g_ffn': g_ffn, 'L0_xattn_weight': _L0_xattn_in['weight'], 'L0_ffn_gate_w': _L0_ffn_in['gate_w'], 'L0_ffn_up_w': _L0_ffn_in['up_w'], 'L0_ffn_down_w': _L0_ffn_in['down_w'], 'L0_ffn_fc1_w': _L0_ffn_in['fc1_w'], 'L0_ffn_fc2_w': _L0_ffn_in['fc2_w'], 'L0_ffn_expert_w': _L0_ffn_in['expert_w'], 'L0_ffn_ln_gamma': _L0_ffn_in['ln_gamma'], 'L0_ffn_ln_beta': _L0_ffn_in['ln_beta']}

def reference(x, ctx_4096, g_xattn, g_ffn, L0_xattn_weight, L0_ffn_gate_w, L0_ffn_up_w, L0_ffn_down_w, L0_ffn_fc1_w, L0_ffn_fc2_w, L0_ffn_expert_w, L0_ffn_ln_gamma, L0_ffn_ln_beta):
    import jax
    import jax.numpy as jnp

    def _L0_xattn_ref(feature, embedding, weight):
        import jax, jax.numpy as jnp
        import numpy as np
        EPS = 1e-08

        def _cosine_sim(a, b):
            na = jnp.maximum(jnp.sqrt(jnp.sum(a * a, axis=1)), EPS)
            nb = jnp.maximum(jnp.sqrt(jnp.sum(b * b, axis=1)), EPS)
            return jnp.sum(a * b, axis=1) / (na * nb)
        B, C, T = feature.shape
        O = weight.shape[0]
        K = 3
        emb_l = jnp.pad(embedding[:, :, :-1], ((0, 0), (0, 0), (1, 0)))
        emb_r = jnp.pad(embedding[:, :, 1:], ((0, 0), (0, 0), (0, 1)))
        sim = jnp.stack([_cosine_sim(embedding, emb_l), _cosine_sim(embedding, embedding), _cosine_sim(embedding, emb_r)], axis=1)
        att = jnp.repeat(sim, C, axis=1)
        f_pad = jnp.pad(feature, ((0, 0), (0, 0), (1, 1)))
        inp_unf = jnp.stack([f_pad[:, :, k:k + T] for k in range(K)], axis=2)
        inp_unf = inp_unf.reshape(B, C * K, T)
        w_flat = weight.reshape(O, C * K)
        out = jnp.einsum('bit,oi->bot', inp_unf * att, w_flat)
        return out

    def _L0_ffn_ref(hidden_states, gate_w, up_w, down_w, fc1_w, fc2_w, expert_w, ln_gamma, ln_beta):
        import jax, jax.numpy as jnp
        import numpy as np
        HID, INT, LAT, NE, K = (1024, 2048, 512, 8, 2)
        LN_EPS = 1e-05

        def _layernorm(x, gamma, beta):
            mu = jnp.mean(x, axis=-1, keepdims=True)
            var = jnp.var(x, axis=-1, keepdims=True)
            return (x - mu) * jax.lax.rsqrt(var + LN_EPS) * gamma + beta
        logits = jnp.einsum('bsh,he->bse', hidden_states, gate_w)
        routing_weights, selected_experts = jax.lax.top_k(logits, K)
        h = jax.nn.relu(jnp.einsum('bsh,hi->bsi', hidden_states, up_w)) ** 2
        shared_out = jnp.einsum('bsi,ih->bsh', h, down_w)
        x_latent = jnp.einsum('bsh,hl->bsl', hidden_states, fc1_w)
        expert_out = jnp.einsum('bsl,lm->bsm', x_latent, expert_w)
        moe_out = expert_out * jnp.sum(routing_weights, axis=-1, keepdims=True)
        routed_out = jnp.einsum('bsl,lh->bsh', moe_out, fc2_w)
        return _layernorm(shared_out + routed_out, ln_gamma, ln_beta)
    x = x + jnp.tanh(g_xattn[0]) * _L0_xattn_ref(_layernorm(x, axis=-1), ctx_4096, L0_xattn_weight)
    x = x + jnp.tanh(g_ffn[0]) * _L0_ffn_ref(_layernorm(x, axis=-1), L0_ffn_gate_w, L0_ffn_up_w, L0_ffn_down_w, L0_ffn_fc1_w, L0_ffn_fc2_w, L0_ffn_expert_w, L0_ffn_ln_gamma, L0_ffn_ln_beta)
    return x

_drawn_inputs = setup_inputs


def setup_inputs(seed=0):
    import zlib

    import numpy as np

    out = dict(_drawn_inputs(seed))
    spreads = {'L0_ffn_ln_gamma': (1.0, 0.2), 'L0_ffn_ln_beta': (0.0, 0.1)}
    factors = {}
    for name, (base, spread) in spreads.items():
        noise = np.random.default_rng([zlib.crc32(name.encode()), seed]).standard_normal(out[name].shape)
        drawn = base * np.exp(spread * noise) if base else spread * noise
        out[name] = jnp.asarray(drawn.astype(out[name].dtype))
    for name, factor in factors.items():
        out[name] = (out[name] * factor).astype(out[name].dtype)
    return out
```

```python
from contextlib import ExitStack

import concourse.bass as bass
from concourse import mybir

ALU = mybir.AluOpType
ACT = mybir.ActivationFunctionType
AX = mybir.AxisListType
F32 = mybir.dt.float32
F16 = mybir.dt.float16
BF16 = mybir.dt.bfloat16
I32 = mybir.dt.int32
RMAX = bass.bass_isa.ReduceOp.max

P = 128
LN_EPS = 1e-5
COS_EPS = 1e-8
LOG_ACT = 10
LOG_W = 14
LAT_SHIFT = -20
HID_SHIFT = -45
W2_SHIFT = 4
WX, WG, WE, WF2, WF1, WDN, WUP = range(7)


def flamingo_block(nc, x, ctx, g_xattn, g_ffn, w_xattn, w_gate, w_up, w_down, w_fc1, w_fc2,
                   w_expert, ln_gamma, ln_beta, out):
    B, C, T = x.shape
    INT = w_up.shape[1]
    LAT = w_fc1.shape[1]
    NE = w_gate.shape[1]
    KB = T // P
    IT = INT // P
    LT = LAT // P
    BB = 4
    NB = B // BB
    TOK = BB * C
    UT = LT + IT
    HALF = T // 2
    G = 3
    NR = 4
    CH = T // 32

    with ExitStack() as es:
        def sb(name, shape, dt):
            return es.enter_context(nc.sbuf_tensor(name, shape, dt))

        def ps(name, shape):
            return es.enter_context(nc.psum_tensor(name, shape, F32))

        def sem(name):
            return es.enter_context(nc.semaphore(name))

        pair_dram = nc.dram_tensor("pair_scratch", (UT, P, 2 * KB * P), F16, kind="Internal").ap()
        side_dram = nc.dram_tensor("side_scratch", (B * T + 2,), F32, kind="Internal").ap()
        self_dram = nc.dram_tensor("self_scratch", (B * T,), F32, kind="Internal").ap()

        big = sb("big", [P, IT * T], F32)
        up_raw = big[:, :].rearrange("p (k i) -> p k i", k=KB)
        dn_raw = big[:, :].rearrange("p (c h) -> p c h", c=IT)
        dn = big[:, :].bitcast(F16).rearrange("p (c s h) -> p c s h", c=IT, s=2)
        LO, HI = 0, 1
        w2 = sb("w2", [P, LT, 2, T], F16)
        gate = sb("gate", [P, KB, 2 * NE], F16)
        wx = sb("wx", [P, G, 2, P], F16)
        xT = sb("xT", [P, KB, 2, TOK], F16)
        hid = sb("hid", [P, IT * 2 * TOK // 2], F32)
        hT = hid[:, :].bitcast(F16).rearrange("p (i s t) -> p i s t", i=IT, s=2)
        fc1_raw = hid[:, 0:KB * LAT].rearrange("p (k l) -> p k l", k=KB)
        fc2_raw = hid[:, KB * LAT:KB * LAT + LT * T].rearrange("p (m h) -> p m h", m=LT)
        staging = hid[:, KB * LAT:].bitcast(F16).rearrange("p (b s k i) -> p b s k i", b=NR, s=2, k=KB)
        latb = sb("latb", [P, LT * TOK], F32)
        lat = latb[:, :].bitcast(F16).rearrange("p (l s t) -> p l s t", l=LT, s=2)
        e_raw = latb[:, :].rearrange("p (l m) -> p l m", l=LT)
        ring_f = sb("ring", [P, NR, 1024], F32)
        ring = ring_f[:, :, :].bitcast(F16).rearrange("p r (s k i) -> p r s k i", s=2, k=KB)
        U = ring_f[:, 0:G, :].bitcast(F16).rearrange("p g (s t) -> p g s t", s=2)
        wx_raw = ring_f[:, 3, 0:G * P]
        gate_raw = ring_f[:, 3, G * P:G * P + KB * NE].rearrange("p (k e) -> p k e", k=KB)
        squares = ring_f[:, 3, :].bitcast(BF16)
        home = sb("home", [P, BB, T], F32)
        ET = home[:, 2:4, :].rearrange("p a (b l) -> p (a b) l", b=2)
        work = sb("work", [P, 2, T], F32)
        dn_hi_tmp = work[:, 1, :].bitcast(F16).rearrange("p (b h) -> p b h", b=2)
        scr = sb("scr", [P, T], F32)
        sides = sb("sides", [P, T + 2], F32)
        fp = sides[:, :].bitcast(F16).rearrange("p (s t) -> p s t", s=2)
        fp_flat = sides[:, :].bitcast(F16)
        sim_side = sb("sim_side", [P, T + 2], F32)
        hbuf = sim_side[:, 0:1024].rearrange("p (b t) -> p b t", b=2)
        y = sb("y", [P, T], F32)
        gam = sb("gam", [P, T], F32)
        bet = sb("bet", [P, T], F32)
        ident = sb("ident", [P, P], F32)
        fold = sb("fold", [P, 32], F32)
        ones_b = sb("ones_b", [P, P], BF16)
        part = sb("part", [P, 2, BB * CH + 1], F32)
        sums = sb("sums", [P, 72], F32)
        nrm = sb("nrm", [P, 36], F32)
        nt = sb("nt", [P, 2, 36], F32)
        simo = sb("simo", [P, 2, 32], F32)
        g_col = sb("g_col", [P, 2], F32)
        th = sb("th", [P, 2], F32)
        amx = sb("amx", [P, 8], F32)
        dmax = sb("dmax", [P, IT], F32)
        amr = sb("amr", [P, 8], F32)
        wexp = sb("wexp", [P, 8], I32)
        wsc = sb("wsc", [P, 8], F32)
        wp = sb("wp", [P, 8], F32)
        coef = sb("coef", [P, 8], F32)
        c_x, c_s, c_r, s_w2 = (coef[:, k:k + 1] for k in range(4))
        st = sb("st", [P, 3, 2, 6], F32)
        mv = sb("mv", [P, 3, 2], F32)
        sd = sb("sd", [P, 3, 4], F32)
        rs = sb("rs", [P, 3, 2], F32)
        LX, L1, LY = range(3)
        lg = sb("lg", [P, BB, NE], F32)
        top = sb("top", [P, BB, 8], F32)
        rw = sb("rw", [P, BB], F32)
        zeros = sb("zeros", [P, 2], F32)

        psS = ps("psS", [P, T])
        psR = ps("psR", [P, T])
        psP = ps("psP", [P, G, HALF])
        psM = ps("psM", [P, 512])
        up_bank = [psS[:, 0:512], psS[:, 512:1024], psR[:, 0:512], psR[:, 512:1024]]

        const_rdy = sem("const_rdy")
        small_in = sem("small_in")
        e_in, f2_in, f1_in, gb_in = sem("e_in"), sem("f2_in"), sem("f1_in"), sem("gb_in")
        upraw_in = [sem(f"upraw_in{k}") for k in range(KB)]
        dnraw_in = [sem(f"dnraw_in{k}") for k in range(4)]
        x_in = [sem(f"x_in{k}") for k in range(2)]
        ctx_in = sem("ctx_in")
        u_in = sem("u_in")
        sim_in = sem("sim_in")
        ring_in = [sem(f"ring_in{k}") for k in range(NR)]
        stg_out = [sem(f"stg_out{k}") for k in range(NR)]
        simrow_out, edge_out = sem("simrow_out"), sem("edge_out")
        out_done = sem("out_done")
        tanh_rdy = sem("tanh_rdy")
        amax_rdy, amax_all = sem("amax_rdy"), sem("amax_all")
        scale_rdy = sem("scale_rdy")
        gb_rdy = sem("gb_rdy")
        wxT_done, wx_hi, wx_rdy = sem("wxT_done"), sem("wx_hi"), sem("wx_rdy")
        gate_hi, gate_w_rdy = sem("gate_hi"), sem("gate_w_rdy")
        eT_done, eT_rdy = sem("eT_done"), sem("eT_rdy")
        w2_done, w2_hi, w2_rdy = sem("w2_done"), sem("w2_hi"), sem("w2_rdy")
        sq_rdy, sq_used = sem("sq_rdy"), sem("sq_used")
        stg_hi, stg_rdy = sem("stg_hi"), sem("stg_rdy")
        dn_hi, dn_lo, dn_rdy = sem("dn_hi"), sem("dn_lo"), sem("dn_rdy")
        prod1, prod0 = sem("prod1"), sem("prod0")
        prod_used = sem("prod_used")
        part_rdy = sem("part_rdy")
        pads_rdy = sem("pads_rdy")
        sums_done, s0_rdy, nrm_rdy, simo_rdy = sem("sums_done"), sem("s0_rdy"), sem("nrm_rdy"), sem("simo_rdy")
        var_rdy = [sem(f"var_rdy{k}") for k in range(3)]
        std_rdy = [sem(f"std_rdy{k}") for k in range(3)]
        rs_rdy = [sem(f"rs_rdy{k}") for k in range(3)]
        f_hi, f_rdy = sem("f_hi"), sem("f_rdy")
        p_done, comb = sem("p_done"), sem("comb")
        xn_rdy, tr_done, xt_hi, xt_rdy = sem("xn_rdy"), sem("tr_done"), sem("xt_hi"), sem("xt_rdy")
        home_rdy = sem("home_rdy")
        up_done, up_evac = sem("up_done"), sem("up_evac")
        relu_rdy, sq_hid, h_hi, h_rdy = sem("relu_rdy"), sem("sq_hid"), sem("h_hi"), sem("h_rdy")
        l_hi, l_rdy = sem("l_hi"), sem("l_rdy")
        gate_done, rw_rdy = sem("gate_done"), sem("rw_rdy")
        s_done, r_done, s_evac, r_evac = sem("s_done"), sem("r_done"), sem("s_evac"), sem("r_evac")
        y_nrm, y_fin = sem("y_nrm"), sem("y_fin")

        SIM_T = 2
        SUMS_T = 16
        LNX_T = 18
        AMAX_T, DSPLIT_T = 6, 12
        AMAX_N, DSPLIT_N = 3, 2

        block = es.enter_context(nc.Block())

        @block.sync
        def _(sp):
            def ahead(value):
                return value if isinstance(value, int) else sp.snap(sp.to_reg(value))

            def load_x(m, j, slot):
                sp.dma_start(work[:, slot, :], x[bass.ds(BB * m + j, 1)].rearrange("o p t -> p (o t)"))\
                    .then_inc(x_in[slot], 16)

            def load_ctx(m, j):
                q = BB * m + j
                if j > 0:
                    sp.wait_ge(prod_used, 2 * q)
                sp.dma_start(scr[:, :], ctx[bass.ds(q, 1)].rearrange("o p t -> p (o t)"))\
                    .then_inc(ctx_in, 16)

            def store_sims(m):
                sp.wait_ge(simo_rdy, m + 1)
                first = BB * T * m
                sp.dma_start(side_dram[bass.ds(first + 2, BB * T)].rearrange("(c t) -> c t", t=32), simo[:, 0, :])\
                    .then_inc(simrow_out, 16)
                sp.dma_start(self_dram[bass.ds(first, BB * T)].rearrange("(c t) -> c t", t=32), simo[:, 1, :])\
                    .then_inc(simrow_out, 16)

            def unfold(m, j, first=False):
                q = BB * m + j
                f_count, pad_count = ahead(q + 1), ahead(m + 1)
                used = ahead(2 * q if j > 0 else UT * m)
                sp.wait_ge(f_rdy, f_count)
                sp.wait_ge(pads_rdy, pad_count)
                if j > 0:
                    sp.wait_ge(p_done, used)
                elif not first:
                    sp.wait_ge(up_done, used)
                for g in range(G):
                    for k in range(G):
                        p0 = (k - P * g) % G
                        c0 = (P * g + p0) // G
                        num = (P - p0 + G - 1) // G
                        sp.dma_start(U[p0:p0 + G * (num - 1) + 1:G, g, :, :],
                                     fp[c0:c0 + num, :, k:k + T]).then_inc(u_in, 16)

            def load_sims(m, j, first=False):
                q = BB * m + j
                rows, combined, hidden = ahead(32 * (m + 1)), ahead(q), ahead(IT * m)
                stored = ahead(16 * (q - BB))
                sp.wait_ge(simrow_out, rows)
                if j > 0:
                    sp.wait_ge(rs_rdy[L1], combined)
                elif not first:
                    sp.wait_ge(h_rdy, hidden)
                if not first and not (isinstance(q, int) and q == BB):
                    sp.wait_ge(out_done, stored)
                side = side_dram[bass.ds(q * T + 1, T + 1)].rearrange("(a t) -> a t", a=1)
                same = self_dram[bass.ds(q * T, T)].rearrange("(a t) -> a t", a=1)
                sp.dma_start(sim_side[:, 0:T + 1], side.broadcast_to([P, T + 1]))\
                    .then_inc(sim_in, 16)
                sp.dma_start(y[:, :], same.broadcast_to([P, T])).then_inc(sim_in, 16)

            def up_half(n, phase_a, first=False):
                m = n + 1
                for t in range(UT):
                    if t == 0:
                        sp.wait_ge(p_done, 2 * BB * m)
                        if first:
                            sp.wait_ge(sq_used, KB)
                    if t >= NR:
                        sp.wait_ge(up_done, UT * n + t - NR + 1)
                    if first:
                        sp.wait_ge(stg_out[t % NR], 16 * (t // NR + 1))
                    sp.dma_start(ring_f[:, t % NR, :].bitcast(F16), pair_dram[t])\
                        .then_inc(ring_in[t % NR], 16)
                    if first and t == NR - 1:
                        sp.wait_ge(stg_rdy, UT)
                        src = w_down.rearrange("(c p) h -> p c h", p=P)
                        for k in range(4):
                            sp.dma_start(dn_raw[:, 4 * k:4 * k + 4, :], src[:, 4 * k:4 * k + 4, :])\
                                .then_inc(dnraw_in[k], 16)
                    if phase_a:
                        if t == NR - 1:
                            sp.wait_ge(tr_done, 2 * BB * m)
                            load_ctx(m, 0)
                            sp.wait_ge(home_rdy, BB * m - 1)
                            load_x(m, 0, 0)
                            if not first:
                                sp.wait_ge(home_rdy, BB * m)
                                load_x(m, 1, 1)
                        for j in range(1, BB):
                            if t == 4 * j + 5:
                                load_ctx(m, j)
                if phase_a:
                    store_sims(m)
                    if first:
                        sp.wait_ge(dn_rdy, IT)
                        sp.wait_ge(home_rdy, BB * m)
                        load_x(m, 1, 1)

            def phase_a_loads(m, j, first=False):
                unfold(m, j, first)
                load_sims(m, j, first)
                if 1 <= j < BB - 1:
                    sp.wait_ge(home_rdy, BB * m + j)
                    load_x(m, j + 1, (j + 1) % 2)

            load_ctx(0, 0)
            sp.dma_start(wx_raw, w_xattn.rearrange("o c k -> o (c k)")).then_inc(small_in, 16)
            sp.dma_start(gate_raw, w_gate.rearrange("(k p) e -> p k e", p=P)).then_inc(small_in, 16)
            sp.dma_start(g_col[:, 0:1], g_xattn.rearrange("(a b) -> a b", a=1).broadcast_to([P, 1]))\
                .then_inc(small_in, 16)
            sp.dma_start(g_col[:, 1:2], g_ffn.rearrange("(a b) -> a b", a=1).broadcast_to([P, 1]))\
                .then_inc(small_in, 16)
            sp.wait_ge(const_rdy, 1)
            sp.dma_start(side_dram[0:2].rearrange("(a t) -> a t", a=1), zeros[0:1, :]).then_inc(edge_out, 16)
            load_x(0, 0, 0)
            load_x(0, 1, 1)
            for j in range(1, BB):
                load_ctx(0, j)
            store_sims(0)
            sp.wait_ge(edge_out, 16)
            for j in range(BB):
                phase_a_loads(0, j, first=True)
            up_half(0, True, first=True)
            for j in range(BB):
                phase_a_loads(1, j)
            with sp.Fori(1, NB - 1) as n:
                up_half(n, True)
                for j in range(BB):
                    phase_a_loads(n + 1, j)
            up_half(NB - 1, False)
            sp.wait_ge(out_done, 16 * B)

        @block.gpsimd
        def _(pool):
            def products(m, j):
                q = BB * m + j
                pool.wait_ge(ctx_in, 16 * (q + 1))
                if j > 0:
                    pool.wait_ge(prod_used, 2 * q - 1)
                elif not (isinstance(m, int) and m == 0):
                    pool.wait_ge(u_in, 16 * G * G * BB * m)
                pool.tensor_tensor(sides[:, 0:T - 1], scr[:, 0:T - 1], scr[:, 1:T], ALU.mult)
                pool.memset(sides[:, T - 1:T], 0.0)
                pool.drain().then_inc(prod1, 1)
                pool.tensor_tensor(scr[:, :], scr[:, :], scr[:, :], ALU.mult).then_inc(prod0, 1)

            def pads(m):
                pool.wait_ge(part_rdy, m + 1)
                for c0, c1 in ((0, 1), (T + 1, T + 3), (2 * T + 3, 2 * T + 4)):
                    pool.tensor_tensor(fp_flat[:, c0:c1], zeros[:, 0:c1 - c0], zeros[:, 0:c1 - c0], ALU.add)
                pool.drain().then_inc(pads_rdy, 1)

            def finish(n, j):
                pool.wait_ge(y_nrm, BB * n + j + 1)
                pool.tensor_tensor(y[:, :], y[:, :], gam[:, :], ALU.mult)
                pool.drain()
                pool.tensor_tensor(y[:, :], y[:, :], home[:, j, :], ALU.add)
                pool.drain().then_inc(y_fin, 1)

            def keep(m, j):
                pool.wait_ge(rs_rdy[L1], BB * m + j + 1)
                pool.wait_ge(xn_rdy, BB * m + j + 1)
                pool.tensor_tensor(home[:, j, :], work[:, j % 2, :], bet[:, :], ALU.add)\
                    .then_inc(home_rdy, 1)

            def split_down(c0, c1):
                for c in range(c0, c1):
                    pool.wait_ge(dn_lo, c + 1)
                    pool.tensor_copy(dn[:, c, HI, :], dn_hi_tmp[:, c % 2, :]).then_inc(dn_rdy, 1)

            pool.memset(zeros[:, :], 0.0)
            pool.memset(ident[:, :], 0.0)
            pool.memset(ones_b[:, :], 1.0)
            pool.memset(fold[:, :], 0.0)
            pool.memset(part[:, :, BB * CH:], 1.0)
            pool.drain()
            pool.affine_select(out=ident[:, :], in_=ident[:, :], compare_op=ALU.not_equal, fill=1.0,
                               base=0, pattern=[[-1, P]], channel_multiplier=1)
            for k in range(4):
                pool.affine_select(out=fold[:, :], in_=fold[:, :], compare_op=ALU.not_equal, fill=1.0,
                                   base=-32 * k, pattern=[[-1, 32]], channel_multiplier=1)
                pool.drain()
            pool.drain().then_inc(const_rdy, 1)
            products(0, 0)
            pool.wait_ge(amax_rdy, 1)
            pool.partition_all_reduce(amr[:, WX:WG + 1], amx[:, WX:WG + 1], P, RMAX).then_inc(amax_all, 1)
            for j in range(1, BB):
                products(0, j)
            pads(0)
            pool.wait_ge(amax_rdy, 2)
            pool.partition_all_reduce(amr[:, WE:WF1 + 1], amx[:, WE:WF1 + 1], P, RMAX).then_inc(amax_all, 1)
            pool.wait_ge(gb_rdy, 1)
            for j in range(BB):
                if j == 2:
                    pool.wait_ge(w2_done, LT)
                keep(0, j)

            def up_half(n, first=False):
                for j in range(BB):
                    products(n + 1, j)
                    if first and j == 2:
                        pool.wait_ge(amax_rdy, 3)
                        pool.partition_all_reduce(amr[:, WDN:WDN + 1], amx[:, WDN:WDN + 1], P, RMAX)\
                            .then_inc(amax_all, 1)
                        split_down(0, DSPLIT_N * (SIM_T + 4 * (BB - 1) - DSPLIT_T))
                if first:
                    split_down(DSPLIT_N * (SIM_T + 4 * (BB - 1) - DSPLIT_T), IT)
                pads(n + 1)

            def down_half(n, phase_a):
                for j in range(BB):
                    finish(n, j)
                    if phase_a:
                        keep(n + 1, j)

            up_half(0, first=True)
            down_half(0, True)
            with pool.Fori(1, NB - 1) as n:
                up_half(n)
                down_half(n, True)
            down_half(NB - 1, False)

        @block.scalar
        def _(act):
            def std(k, q):
                act.wait_ge(var_rdy[k], q + 1)
                act.activation(sd[:, k, 1:2], sd[:, k, 0:1], ACT.Sqrt).then_inc(std_rdy[k], 1)

            def norms(m):
                act.wait_ge(s0_rdy, m + 1)
                act.activation(nrm[:, 0:33], sums[:, 0:33], ACT.Sqrt).then_inc(nrm_rdy, 1)

            def f_pairs(m, j):
                q = BB * m + j
                act.wait_ge(rs_rdy[LX], q + 1)
                act.wait_ge(part_rdy, m + 1)
                if j > 0:
                    act.wait_ge(tr_done, 2 * q)
                    act.wait_ge(u_in, 16 * G * G * q)
                act.activation(scr[:, :], work[:, j % 2, :], ACT.Identity, bias=rs[:, LX, 1:2],
                               scale=rs[:, LX, 0:1])
                act.drain()
                act.activation(fp[:, 0, 1:T + 1], scr[:, :], ACT.Copy).then_inc(f_hi, 1)

            def x1_normal(m, j):
                q = BB * m + j
                act.wait_ge(rs_rdy[L1], q + 1)
                act.activation(scr[:, :], work[:, j % 2, :], ACT.Identity, bias=rs[:, L1, 1:2],
                               scale=rs[:, L1, 0:1]).then_inc(xn_rdy, 1)

            def xt_his(m, j):
                for h in range(2):
                    act.wait_ge(tr_done, 2 * (BB * m + j) + h + 1)
                    act.activation(xT[:, 4 * h:4 * h + 4, 0, P * j:P * j + P],
                                   psP[:, h, :].rearrange("p (k t) -> p k t", k=4), ACT.Copy)\
                        .then_inc(xt_hi, 1)

            def finish(n, j):
                q = BB * n + j
                std(LY, q)
                act.wait_ge(rs_rdy[LY], q + 1)
                act.activation(y[:, :], y[:, :], ACT.Identity, bias=rs[:, LY, 1:2],
                               scale=rs[:, LY, 0:1]).then_inc(y_nrm, 1)
                act.wait_ge(y_fin, q + 1)
                act.dma_start(out[bass.ds(q, 1)].rearrange("o p t -> p (o t)"), y[:, :])\
                    .then_inc(out_done, 16)

            def take_s(n, j, phase_a):
                act.wait_ge(s_done, BB * n + j + 1)
                if not (isinstance(n, int) and BB * n + j == 0):
                    act.wait_ge(out_done, 16 * (BB * n + j))
                act.activation(y[:, :], psS[:, :], ACT.Copy, scale=c_s).then_inc(s_evac, 1)

            def up_half(n, phase_a, first=False):
                m = n + 1
                for t in range(UT):
                    act.wait_ge(up_done, UT * n + t + 1)
                    bank = up_bank[t % NR]
                    if t < LT:
                        act.activation(lat[:, t, 0, :], bank, ACT.Copy, scale=2.0 ** LAT_SHIFT)\
                            .then_inc(l_hi, 1)
                    else:
                        i = IT * n + t - LT
                        buf = hbuf[:, t % 2, :]
                        if t >= LT + 2:
                            act.wait_ge(h_rdy, i - 1)
                        act.activation(buf, bank, ACT.Relu, scale=2.0 ** HID_SHIFT).then_inc(relu_rdy, 1)
                        act.wait_ge(sq_hid, i + 1)
                        act.activation(hT[:, t - LT, 0, :], buf, ACT.Copy).then_inc(h_hi, 1)
                    if phase_a and t == SUMS_T + 1:
                        norms(m)
                    if phase_a and t == LNX_T:
                        std(LX, BB * m)
                    if first and t >= DSPLIT_T:
                        for c in range(DSPLIT_N * (t - DSPLIT_T), DSPLIT_N * (t - DSPLIT_T) + DSPLIT_N):
                            down_hi(c)

            def down_hi(c):
                act.wait_ge(scale_rdy, 4)
                if c >= 2:
                    act.wait_ge(dn_rdy, c - 1)
                else:
                    act.wait_ge(home_rdy, BB)
                act.activation(dn_hi_tmp[:, c % 2, :], dn_raw[:, c, :], ACT.Copy,
                               scale=wsc[:, WDN:WDN + 1]).then_inc(dn_hi, 1)

            def down_half(n, phase_a):
                m = n + 1
                for j in range(BB):
                    if phase_a:
                        f_pairs(m, j)
                    if j > 0:
                        finish(n, j - 1)
                    if phase_a:
                        std(L1, BB * m + j)
                        x1_normal(m, j)
                        if j < BB - 1:
                            std(LX, BB * m + j + 1)
                    take_s(n, j, phase_a)
                    if phase_a:
                        xt_his(m, j)
                finish(n, BB - 1)

            act.dma_start(e_raw, w_expert.rearrange("(l p) m -> p l m", p=P)).then_inc(e_in, 16)
            act.dma_start(fc2_raw, w_fc2.rearrange("(m p) h -> p m h", p=P)).then_inc(f2_in, 16)
            act.dma_start(fc1_raw, w_fc1.rearrange("(k p) l -> p k l", p=P)).then_inc(f1_in, 16)
            act.dma_start(gam[:, :], ln_gamma.rearrange("(a h) -> a h", a=1).broadcast_to([P, T]))\
                .then_inc(gb_in, 16)
            act.dma_start(bet[:, :], ln_beta.rearrange("(a h) -> a h", a=1).broadcast_to([P, T]))\
                .then_inc(gb_in, 16)
            for k in range(KB):
                act.dma_start(up_raw[:, k, :], w_up[k * P:(k + 1) * P, :]).then_inc(upraw_in[k], 16)
            act.wait_ge(small_in, 64)
            act.activation(th[:, :], g_col[:, :], ACT.Tanh).then_inc(tanh_rdy, 1)
            act.wait_ge(scale_rdy, 1)
            act.wait_ge(wxT_done, 1)
            act.activation(wx[:, :, 0, :], psM[:, 0:G * P].rearrange("p (g o) -> p g o", g=G), ACT.Copy,
                           scale=wsc[:, WX:WX + 1]).then_inc(wx_hi, 1)
            act.activation(gate[:, :, 0:NE], gate_raw, ACT.Copy, scale=wsc[:, WG:WG + 1])\
                .then_inc(gate_hi, 1)
            norms(0)
            for k in range(LT):
                act.wait_ge(eT_done, k + 1)
                act.activation(ET[:, k, :], up_bank[k], ACT.Copy).then_inc(eT_rdy, 1)

            def w2_his(l):
                act.wait_ge(scale_rdy, 2)
                act.wait_ge(w2_done, l + 1)
                act.activation(w2[:, l, 0, :], (psS if l % 2 == 0 else psR)[:, :], ACT.Copy, scale=s_w2)\
                    .then_inc(w2_hi, 1)

            def up_squares(k):
                act.wait_ge(upraw_in[k], 16)
                if k > 0:
                    act.wait_ge(sq_used, k)
                else:
                    act.wait_ge(gate_w_rdy, 1)
                    act.wait_ge(wxT_done, 1)
                act.activation(squares, up_raw[:, k, :], ACT.Square).then_inc(sq_rdy, 1)

            std(LX, 0)
            for j in range(BB):
                f_pairs(0, j)
                if j < 2:
                    w2_his(2 * j)
                    w2_his(2 * j + 1)
                std(L1, j)
                x1_normal(0, j)
                if j < BB - 1:
                    std(LX, j + 1)
                xt_his(0, j)
                if j >= 2:
                    for k in range(4 * (j - 2), 4 * (j - 2) + 4):
                        up_squares(k)
            for t in range(UT):
                act.wait_ge(scale_rdy, 3 if t >= LT else 2)
                if t >= NR:
                    act.wait_ge(stg_out[t % NR], 16 * (t // NR))
                else:
                    act.wait_ge(w2_done, LT)
                raw = fc1_raw[:, :, P * t:P * t + P] if t < LT else up_raw[:, :, P * (t - LT):P * (t - LT) + P]
                k = WF1 if t < LT else WUP
                act.activation(staging[:, t % NR, 0, :, :], raw, ACT.Copy, scale=wsc[:, k:k + 1])\
                    .then_inc(stg_hi, 1)
                if t >= 1:
                    act.wait_ge(stg_rdy, t)
                    act.dma_start(pair_dram[t - 1], staging[:, (t - 1) % NR].rearrange("p s k i -> p (s k i)"))\
                        .then_inc(stg_out[(t - 1) % NR], 16)
            act.wait_ge(stg_rdy, UT)
            act.dma_start(pair_dram[UT - 1], staging[:, (UT - 1) % NR].rearrange("p s k i -> p (s k i)"))\
                .then_inc(stg_out[(UT - 1) % NR], 16)
            for k in range(NR):
                act.wait_ge(stg_out[k], 16 * (UT // NR))

            up_half(0, True, first=True)
            down_half(0, True)
            with act.Fori(1, NB - 1) as n:
                up_half(n, True)
                down_half(n, True)
            up_half(NB - 1, False)
            down_half(NB - 1, False)

        @block.vector
        def _(dve):
            def stats(k, src):
                for h in range(2):
                    dve.bn_stats(st[:, k, h, :], src[:, HALF * h:HALF * h + HALF])
                dve.drain()
                dve.bn_aggr(mv[:, k, :], st[:, k, :, :].rearrange("p h s -> p (h s)"))
                dve.drain()
                dve.tensor_scalar(sd[:, k, 0:1], mv[:, k, 1:2], LN_EPS, None, ALU.add)\
                    .then_inc(var_rdy[k], 1)

            def scale_bias(k, q, scale):
                dve.wait_ge(std_rdy[k], q + 1)
                dve.reciprocal(sd[:, k, 2:3], sd[:, k, 1:2])
                dve.drain()
                dve.tensor_scalar(sd[:, k, 3:4], sd[:, k, 2:3], sd[:, k, 2:3], sd[:, k, 0:1], ALU.mult, ALU.mult)
                dve.drain()
                dve.tensor_scalar(sd[:, k, 3:4], sd[:, k, 3:4], -0.5, 1.5, ALU.mult, ALU.add)
                dve.drain()
                dve.scalar_tensor_tensor(out=rs[:, k, 0:1], in0=sd[:, k, 2:3], scalar=scale,
                                         in1=sd[:, k, 3:4], op0=ALU.mult, op1=ALU.mult)
                dve.drain()
                dve.scalar_tensor_tensor(out=rs[:, k, 1:2], in0=mv[:, k, 0:1], scalar=-1.0,
                                         in1=rs[:, k, 0:1], op0=ALU.mult, op1=ALU.mult)
                dve.drain().then_inc(rs_rdy[k], 1)

            def sum_products(m, j, which):
                q = BB * m + j
                if which == 1:
                    dve.wait_ge(prod1, q + 1)
                    if j == 0 and not (isinstance(m, int) and m <= 1):
                        dve.wait_ge(out_done, 16 * BB * (m - 1))
                    dve.transpose(y[:, :], sides[:, 0:T]).then_inc(prod_used, 1)
                else:
                    dve.wait_ge(prod0, q + 1)
                    dve.transpose(y[:, :], scr[:, :]).then_inc(prod_used, 1)
                dve.drain()
                dve.tensor_reduce(part[:, which, CH * j:CH * j + CH],
                                  y[:, :].rearrange("p (c a) -> p c a", a=32), AX.X, ALU.add)
                if which == 0 and j == BB - 1:
                    dve.drain().then_inc(part_rdy, 1)
                else:
                    dve.drain()

            def cosines(m):
                dve.wait_ge(sums_done, m + 1)
                dve.tensor_copy(sums[:, 0:65], psM[:, 0:65])
                dve.drain().then_inc(s0_rdy, 1)
                dve.wait_ge(nrm_rdy, m + 1)
                a, b, c = nrm[:, 0:33], nt[:, 0, 0:33], nt[:, 1, 0:33]
                dve.tensor_scalar(a, a, COS_EPS, None, ALU.max)
                dve.drain()
                dve.reciprocal(b, a)
                dve.drain()
                dve.tensor_tensor(c, sums[:, 0:33], b, ALU.mult)
                dve.drain()
                dve.tensor_tensor(a, a, c, ALU.add)
                dve.drain()
                dve.tensor_scalar(a, a, 0.5, COS_EPS, ALU.mult, ALU.max)
                dve.drain()
                dve.tensor_tensor(nt[:, 0, 0:32], nrm[:, 0:32], nrm[:, 1:33], ALU.mult)
                dve.tensor_tensor(nt[:, 1, 0:32], nrm[:, 0:32], nrm[:, 0:32], ALU.mult)
                dve.drain()
                dve.reciprocal(nt[:, :, 0:32], nt[:, :, 0:32])
                dve.drain()
                if not (isinstance(m, int) and m == 0):
                    dve.wait_ge(simrow_out, 32 * m)
                dve.tensor_tensor(simo[:, 0, :], sums[:, 33:65], nt[:, 0, 0:32], ALU.mult)
                dve.tensor_tensor(simo[:, 1, :], sums[:, 0:32], nt[:, 1, 0:32], ALU.mult)
                dve.drain().then_inc(simo_rdy, 1)

            def f_los(m, j):
                dve.wait_ge(f_hi, BB * m + j + 1)
                dve.tensor_tensor(fp[:, 1, 1:T + 1], scr[:, :], fp[:, 0, 1:T + 1], ALU.subtract)\
                    .then_inc(f_rdy, 1)

            def combine(m, j):
                q = BB * m + j
                xr = work[:, j % 2, :]
                dve.wait_ge(sim_in, 32 * (q + 1))
                for h in range(2):
                    t0 = HALF * h
                    dve.wait_ge(p_done, 2 * q + h + 1)
                    xh = xr[:, t0:t0 + HALF]
                    a, b = scr[:, 0:HALF], scr[:, HALF:T]
                    dve.scalar_tensor_tensor(out=a, in0=psP[:, 0, :], scalar=c_x,
                                             in1=sim_side[:, t0:t0 + HALF], op0=ALU.mult, op1=ALU.mult)
                    dve.scalar_tensor_tensor(out=b, in0=psP[:, 1, :], scalar=c_x,
                                             in1=y[:, t0:t0 + HALF], op0=ALU.mult, op1=ALU.mult)
                    dve.drain()
                    dve.tensor_tensor(a, a, b, ALU.add)
                    dve.drain()
                    dve.scalar_tensor_tensor(out=b, in0=psP[:, 2, :], scalar=c_x,
                                             in1=sim_side[:, t0 + 1:t0 + HALF + 1], op0=ALU.mult, op1=ALU.mult)\
                        .then_inc(comb, 1)
                    dve.tensor_tensor(xh, xh, a, ALU.add)
                    dve.drain()
                    dve.tensor_tensor(xh, xh, b, ALU.add)
                    dve.drain()
                stats(L1, xr)
                scale_bias(L1, q, 2.0 ** LOG_ACT)

            def x_stats(m, j):
                q = BB * m + j
                if isinstance(m, int):
                    loads = 2 * m + j // 2 + 1
                else:
                    loads = m * 2 + (j // 2 + 1)
                dve.wait_ge(x_in[j % 2], loads * 16)
                stats(LX, work[:, j % 2, :])
                scale_bias(LX, q, 2.0 ** LOG_ACT)

            def xt_los(m, j):
                for h in range(2):
                    dve.wait_ge(xt_hi, 2 * (BB * m + j) + h + 1)
                    dst = xT[:, 4 * h:4 * h + 4, :, P * j:P * j + P]
                    dve.tensor_tensor(dst[:, :, 1, :], psP[:, h, :].rearrange("p (k t) -> p k t", k=4),
                                      dst[:, :, 0, :], ALU.subtract)
                dve.drain().then_inc(xt_rdy, 1)

            def pow2(lo, hi, src, mult, add):
                dve.tensor_scalar(src, src, 2.0 ** -80, None, ALU.max)
                dve.drain()
                dve.tensor_scalar(wexp[:, lo:hi], src.bitcast(I32), mult, add, ALU.mult, ALU.add)
                dve.drain()
                dve.tensor_scalar(wsc[:, lo:hi].bitcast(I32), wexp[:, lo:hi], -2.0 ** 23,
                                  (254 + LOG_W) * 2.0 ** 23, ALU.mult, ALU.add)
                dve.tensor_scalar(wp[:, lo:hi].bitcast(I32), wexp[:, lo:hi], 2.0 ** 23, None, ALU.mult)
                dve.drain()

            def take_r(n, j):
                q = BB * n + j
                dve.wait_ge(r_done, q + 1)
                dve.wait_ge(s_evac, q + 1)
                dve.scalar_tensor_tensor(out=y[:, :], in0=psR[:, :], scalar=rw[:, j:j + 1], in1=y[:, :],
                                         op0=ALU.mult, op1=ALU.add).then_inc(r_evac, 1)

            def y_stats(n, j):
                dve.drain()
                stats(LY, y)
                scale_bias(LY, BB * n + j, 1.0)

            def routing(n):
                dve.wait_ge(gate_done, n + 1)
                lgp = psM[:, 128:128 + BB * 2 * NE].rearrange("p (j s e) -> p j s e", j=BB, s=2)
                dve.tensor_copy(lg[:, :, :], lgp[:, :, 0, :])
                dve.drain()
                dve.tensor_tensor(lg[:, :, :], lg[:, :, :], lgp[:, :, 1, :], ALU.add)
                dve.drain().then_inc(rw_rdy, 1)
                for j in range(BB):
                    dve.max(top[:, j, :], lg[:, j, :])
                dve.drain()
                dve.tensor_tensor(rw[:, :], top[:, :, 0], top[:, :, 1], ALU.add)
                dve.drain()
                dve.tensor_scalar(rw[:, :], rw[:, :], c_r, None, ALU.mult)
                dve.drain()

            def down_max(c):
                if c % 4 == 0:
                    dve.wait_ge(dnraw_in[c // 4], 16)
                dve.tensor_reduce(dmax[:, c:c + 1], dn_raw[:, c, :], AX.X, ALU.max, apply_absolute_value=True)

            def down_lo(c):
                dve.wait_ge(dn_hi, c + 1)
                dve.scalar_tensor_tensor(out=dn[:, c, LO, :], in0=dn_raw[:, c, :], scalar=wsc[:, WDN:WDN + 1],
                                         in1=dn_hi_tmp[:, c % 2, :], op0=ALU.mult, op1=ALU.subtract)\
                    .then_inc(dn_lo, 1)

            def up_half(n, phase_a, first=False):
                m = n + 1
                for t in range(UT):
                    bank = up_bank[t % NR]
                    if t < LT:
                        dve.wait_ge(l_hi, LT * n + t + 1)
                        dve.scalar_tensor_tensor(out=lat[:, t, 1, :], in0=bank, scalar=2.0 ** LAT_SHIFT,
                                                 in1=lat[:, t, 0, :], op0=ALU.mult, op1=ALU.subtract)\
                            .then_inc(up_evac, 1)
                    else:
                        i = IT * n + t - LT
                        dve.wait_ge(relu_rdy, i + 1)
                        dve.scalar_tensor_tensor(out=hbuf[:, t % 2, :], in0=bank, scalar=0.0,
                                                 in1=hbuf[:, t % 2, :], op0=ALU.max, op1=ALU.mult)
                        dve.drain().then_inc(up_evac, 1)
                        dve.drain().then_inc(sq_hid, 1)
                    if phase_a and t >= SIM_T and (t - SIM_T) % 4 == 0 and (t - SIM_T) // 4 < BB:
                        sum_products(m, (t - SIM_T) // 4, 1)
                    if phase_a and t >= SIM_T and (t - SIM_T) % 4 == 1 and (t - SIM_T) // 4 < BB:
                        sum_products(m, (t - SIM_T) // 4, 0)
                    if t >= LT:
                        dve.wait_ge(h_hi, i + 1)
                        dve.tensor_tensor(hT[:, t - LT, 1, :], hbuf[:, t % 2, :], hT[:, t - LT, 0, :],
                                          ALU.subtract).then_inc(h_rdy, 1)
                    if phase_a and t == SUMS_T + 1:
                        cosines(m)
                    if phase_a and t == LNX_T:
                        x_stats(m, 0)
                    if first and AMAX_T <= t < DSPLIT_T:
                        for c in range(AMAX_N * (t - AMAX_T), min(IT, AMAX_N * (t - AMAX_T) + AMAX_N)):
                            down_max(c)
                        if t == DSPLIT_T - 1:
                            dve.drain()
                            dve.tensor_reduce(amx[:, WDN:WDN + 1], dmax[:, :], AX.X, ALU.max)
                            dve.drain().then_inc(amax_rdy, 1)
                            dve.wait_ge(amax_all, 3)
                            pow2(WDN, WDN + 1, amr[:, WDN:WDN + 1], 2.0 ** -23, 0.0)
                            dve.drain().then_inc(scale_rdy, 1)
                            dve.tensor_scalar(coef[:, 4:5], wp[:, WUP:WUP + 1], wp[:, WUP:WUP + 1],
                                              wp[:, WDN:WDN + 1], ALU.mult, ALU.mult)
                            dve.drain()
                            dve.tensor_scalar(c_s, coef[:, 4:5], 2.0 ** -17, None, ALU.mult)
                            dve.drain().then_inc(scale_rdy, 1)
                    if first and t >= DSPLIT_T:
                        for c in range(DSPLIT_N * (t - DSPLIT_T), DSPLIT_N * (t - DSPLIT_T) + DSPLIT_N):
                            down_lo(c)
                routing(n)

            def down_half(n, phase_a):
                m = n + 1
                for j in range(BB):
                    if phase_a:
                        f_los(m, j)
                    if j > 0:
                        y_stats(n, j - 1)
                    if phase_a:
                        combine(m, j)
                        if j < BB - 1:
                            x_stats(m, j + 1)
                    take_r(n, j)
                    if phase_a:
                        xt_los(m, j)
                y_stats(n, BB - 1)

            dve.wait_ge(small_in, 64)
            dve.tensor_reduce(amx[:, WX:WX + 1], wx_raw, AX.X, ALU.max, apply_absolute_value=True)
            dve.tensor_reduce(amx[:, WG:WG + 1], gate_raw, AX.XY, ALU.max, apply_absolute_value=True)
            dve.drain().then_inc(amax_rdy, 1)
            dve.wait_ge(const_rdy, 1)
            sum_products(0, 0, 1)
            sum_products(0, 0, 0)
            dve.wait_ge(amax_all, 1)
            pow2(WX, WG + 1, amr[:, WX:WG + 1], 2.0 ** -23, 0.0)
            dve.drain().then_inc(scale_rdy, 1)
            dve.wait_ge(tanh_rdy, 1)
            dve.tensor_scalar(c_x, wp[:, WX:WX + 1], th[:, 0:1], 2.0 ** -(LOG_ACT + LOG_W), ALU.mult, ALU.mult)
            dve.wait_ge(wx_hi, 1)
            dve.scalar_tensor_tensor(out=wx[:, :, 1, :], in0=psM[:, 0:G * P].rearrange("p (g o) -> p g o", g=G),
                                     scalar=wsc[:, WX:WX + 1], in1=wx[:, :, 0, :], op0=ALU.mult,
                                     op1=ALU.subtract).then_inc(wx_rdy, 1)
            dve.wait_ge(gate_hi, 1)
            dve.scalar_tensor_tensor(out=gate[:, :, NE:2 * NE], in0=gate_raw, scalar=wsc[:, WG:WG + 1],
                                     in1=gate[:, :, 0:NE], op0=ALU.mult, op1=ALU.subtract)\
                .then_inc(gate_w_rdy, 1)
            for j in range(1, BB):
                sum_products(0, j, 1)
                sum_products(0, j, 0)
            cosines(0)
            dve.wait_ge(e_in, 16)
            dve.tensor_reduce(amx[:, WE:WE + 1], e_raw, AX.XY, ALU.max, apply_absolute_value=True)
            dve.wait_ge(f2_in, 16)
            dve.tensor_reduce(amx[:, WF2:WF2 + 1], fc2_raw, AX.XY, ALU.max, apply_absolute_value=True)
            dve.wait_ge(f1_in, 16)
            dve.tensor_reduce(amx[:, WF1:WF1 + 1], fc1_raw, AX.XY, ALU.max, apply_absolute_value=True)
            dve.drain().then_inc(amax_rdy, 1)
            dve.wait_ge(gb_in, 32)
            dve.tensor_scalar(gam[:, :], gam[:, :], th[:, 1:2], None, ALU.mult)
            dve.tensor_scalar(bet[:, :], bet[:, :], th[:, 1:2], None, ALU.mult)
            dve.drain().then_inc(gb_rdy, 1)
            dve.wait_ge(amax_all, 2)
            pow2(WE, WF1 + 1, amr[:, WE:WF1 + 1], 2.0 ** -23, 0.0)
            dve.tensor_scalar(s_w2, wsc[:, WE:WE + 1], wsc[:, WF2:WF2 + 1], 2.0 ** (W2_SHIFT - 2 * LOG_W),
                              ALU.mult, ALU.mult)
            dve.tensor_scalar(coef[:, 5:6], wp[:, WE:WE + 1], wp[:, WF2:WF2 + 1], wp[:, WF1:WF1 + 1],
                              ALU.mult, ALU.mult)
            dve.drain()
            dve.tensor_scalar(c_r, coef[:, 5:6], wp[:, WG:WG + 1],
                              2.0 ** -(2 * LOG_ACT + 2 * LOG_W + LAT_SHIFT + W2_SHIFT), ALU.mult, ALU.mult)
            dve.drain().then_inc(scale_rdy, 1)

            def w2_los(l):
                dve.wait_ge(w2_hi, l + 1)
                dve.scalar_tensor_tensor(out=w2[:, l, 1, :], in0=(psS if l % 2 == 0 else psR)[:, :],
                                         scalar=s_w2, in1=w2[:, l, 0, :], op0=ALU.mult,
                                         op1=ALU.subtract).then_inc(w2_rdy, 1)

            x_stats(0, 0)
            for j in range(BB):
                f_los(0, j)
                if j < 2:
                    w2_los(2 * j)
                    w2_los(2 * j + 1)
                combine(0, j)
                if j < BB - 1:
                    x_stats(0, j + 1)
                xt_los(0, j)
            dve.wait_ge(sq_used, KB)
            dve.tensor_reduce(amx[:, 6:7], psS[:, :], AX.X, ALU.max)
            dve.tensor_reduce(amx[:, 7:8], psR[:, :], AX.X, ALU.max)
            dve.drain()
            dve.tensor_tensor(amr[:, WUP:WUP + 1], amx[:, 6:7], amx[:, 7:8], ALU.max)
            dve.drain()
            pow2(WUP, WUP + 1, amr[:, WUP:WUP + 1], 2.0 ** -24, 63.5)
            dve.drain().then_inc(scale_rdy, 1)
            for t in range(UT):
                raw = fc1_raw[:, :, P * t:P * t + P] if t < LT else up_raw[:, :, P * (t - LT):P * (t - LT) + P]
                k = WF1 if t < LT else WUP
                dve.wait_ge(stg_hi, t + 1)
                dve.scalar_tensor_tensor(out=staging[:, t % NR, 1, :, :], in0=raw, scalar=wsc[:, k:k + 1],
                                         in1=staging[:, t % NR, 0, :, :], op0=ALU.mult,
                                         op1=ALU.subtract).then_inc(stg_rdy, 1)
            up_half(0, True, first=True)
            down_half(0, True)
            with dve.Fori(1, NB - 1) as n:
                up_half(n, True)
                down_half(n, True)
            up_half(NB - 1, False)
            down_half(NB - 1, False)

        @block.tensor
        def _(pe):
            def quadrant_sums(m):
                pe.wait_ge(part_rdy, m + 1)
                n = BB * CH
                pe.matmul(psM[:, 0:32], part[:, 0, 0:n], fold[:, :], start=True, stop=True)
                pe.matmul(psM[:, 32:33], part[:, 0, 1:n + 1], fold[:, 0:1], start=True, stop=True)
                pe.matmul(psM[:, 33:65], part[:, 1, 0:n], fold[:, :], start=True, stop=True)\
                    .then_inc(sums_done, 1)

            def xattn(m, j, h):
                q = BB * m + j
                if h == 0:
                    pe.wait_ge(u_in, 16 * G * G * (q + 1))
                    if not (isinstance(m, int) and q == 0):
                        pe.wait_ge(xt_rdy, q)
                else:
                    pe.wait_ge(comb, 2 * q + 1)
                t0 = HALF * h
                for g in range(G):
                    for n, (a, b) in enumerate(((0, 0), (0, 1), (1, 0))):
                        mm = pe.matmul(psP[:, g, :], wx[:, g, a, :], U[:, g, b, t0:t0 + HALF],
                                       start=(n == 0), stop=(n == 2))
                mm.then_inc(p_done, 1)

            def turn(m, j):
                pe.wait_ge(xn_rdy, BB * m + j + 1)
                for h in range(2):
                    for k in range(4):
                        mm = pe.transpose(psP[:, h, P * k:P * k + P],
                                          scr[:, P * (4 * h + k):P * (4 * h + k) + P], ident[:, :])
                    mm.then_inc(tr_done, 1)

            def up_half(n, phase_a):
                m = n + 1
                pe.wait_ge(xt_rdy, BB * m)
                for t in range(UT):
                    pe.wait_ge(ring_in[t % NR], 16 * (n * (UT // NR) + t // NR + 1))
                    if t >= NR:
                        pe.wait_ge(up_evac, UT * n + t - NR + 1)
                    elif not (isinstance(n, int) and n == 0):
                        pe.wait_ge(s_evac if t < 2 else r_evac, BB * n)
                    for k in range(KB):
                        for a, b in ((0, 0), (0, 1), (1, 0)):
                            mm = pe.matmul(up_bank[t % NR], ring[:, t % NR, a, k, :], xT[:, k, b, :],
                                           start=(k == 0 and a == 0 and b == 0),
                                           stop=(k == KB - 1 and a == 1))
                    mm.then_inc(up_done, 1)
                    if phase_a and t == SUMS_T:
                        if not (isinstance(n, int) and n == 0):
                            pe.wait_ge(rw_rdy, n)
                        quadrant_sums(m)
                if phase_a:
                    pe.wait_ge(simo_rdy, m + 1)
                for j in range(BB):
                    c0 = 128 + 2 * NE * j
                    for k in range(KB):
                        pe.matmul(psM[:, c0:c0 + 2 * NE], xT[:, k, 0, P * j:P * j + P], gate[:, k, :],
                                  start=(k == 0), stop=False, skip_group_check=True)
                        mm = pe.matmul(psM[:, c0:c0 + NE], xT[:, k, 1, P * j:P * j + P], gate[:, k, 0:NE],
                                       start=False, stop=(k == KB - 1), skip_group_check=True)
                mm.then_inc(gate_done, 1)

            def shared(j, i0, i1):
                for i in range(i0, i1):
                    for a, b in ((0, HI), (0, LO), (1, HI)):
                        for h in range(2):
                            mm = pe.matmul(psS[:, HALF * h:HALF * h + HALF], hT[:, i, a, P * j:P * j + P],
                                           dn[:, i, b, HALF * h:HALF * h + HALF],
                                           start=(i == 0 and a == 0 and b == HI),
                                           stop=(i == IT - 1 and a == 1))
                return mm

            def routed(j):
                for l in range(LT):
                    for a, b in ((0, 0), (0, 1), (1, 0)):
                        for h in range(2):
                            mm = pe.matmul(psR[:, HALF * h:HALF * h + HALF], lat[:, l, a, P * j:P * j + P],
                                           w2[:, l, b, HALF * h:HALF * h + HALF],
                                           start=(l == 0 and a == 0 and b == 0),
                                           stop=(l == LT - 1 and a == 1))
                return mm

            def down_half(n, phase_a, first=False):
                m = n + 1
                for j in range(BB):
                    q = BB * n + j
                    if j == 0:
                        pe.wait_ge(up_evac, UT * (n + 1))
                        pe.wait_ge(h_rdy, IT * (n + 1))
                        if first:
                            pe.wait_ge(dn_rdy, IT)
                    else:
                        pe.wait_ge(s_evac, q)
                    shared(j, 0, 8)
                    if phase_a:
                        xattn(m, j, 0)
                    shared(j, 8, 12)
                    if phase_a:
                        xattn(m, j, 1)
                    shared(j, 12, IT).then_inc(s_done, 1)
                    if j > 0:
                        pe.wait_ge(r_evac, q)
                    routed(j).then_inc(r_done, 1)
                    if phase_a:
                        turn(m, j)

            pe.wait_ge(const_rdy, 1)
            pe.wait_ge(small_in, 64)
            for g in range(G):
                mm = pe.transpose(psM[:, P * g:P * g + P], wx_raw[:, P * g:P * g + P], ident[:, :])
            mm.then_inc(wxT_done, 1)
            pe.wait_ge(e_in, 16)
            for k in range(LT):
                for l in range(LT):
                    mm = pe.transpose(up_bank[k][:, P * l:P * l + P], e_raw[:, l, P * k:P * k + P], ident[:, :])
                mm.then_inc(eT_done, 1)
            pe.wait_ge(wx_rdy, 1)
            quadrant_sums(0)

            def expert_fc2(l):
                pe.wait_ge(eT_rdy, LT)
                pe.wait_ge(f2_in, 16)
                if l >= 2:
                    pe.wait_ge(w2_rdy, l - 1)
                acc = psS if l % 2 == 0 else psR
                for k in range(LT):
                    for h in range(2):
                        mm = pe.matmul(acc[:, HALF * h:HALF * h + HALF], ET[:, k, P * l:P * l + P],
                                       fc2_raw[:, k, HALF * h:HALF * h + HALF],
                                       start=(k == 0), stop=(k == LT - 1))
                mm.then_inc(w2_done, 1)

            def column_norms(k):
                pe.wait_ge(sq_rdy, k + 1)
                if k == 0:
                    pe.wait_ge(w2_rdy, LT)
                for b in range(4):
                    mm = pe.matmul(up_bank[b], ones_b[:, :], squares[:, 512 * b:512 * b + 512],
                                   start=(k == 0), stop=(k == KB - 1), skip_group_check=True)
                mm.then_inc(sq_used, 1)

            for j in range(BB):
                if j < 2:
                    expert_fc2(2 * j)
                    expert_fc2(2 * j + 1)
                xattn(0, j, 0)
                xattn(0, j, 1)
                turn(0, j)
                if j >= 2:
                    for k in range(4 * (j - 2), 4 * (j - 2) + 4):
                        column_norms(k)
            pe.wait_ge(gate_w_rdy, 1)
            up_half(0, True)
            down_half(0, True, first=True)
            with pe.Fori(1, NB - 1) as n:
                up_half(n, True)
                down_half(n, True)
            up_half(NB - 1, False)
            down_half(NB - 1, False)


_INS = ["x", "ctx_4096", "g_xattn", "g_ffn", "L0_xattn_weight", "L0_ffn_gate_w", "L0_ffn_up_w",
        "L0_ffn_down_w", "L0_ffn_fc1_w", "L0_ffn_fc2_w", "L0_ffn_expert_w", "L0_ffn_ln_gamma",
        "L0_ffn_ln_beta"]


def kernel(**inputs):
    import numpy as np
    import concourse.bacc as bacc
    from concourse.bass_utils import run_bass_kernel_spmd as run

    nc = bacc.Bacc("TRN2", target_bir_lowering=False, num_devices=1)
    arrays, args = {}, []
    for name in _INS:
        a = np.ascontiguousarray(inputs[name])
        arrays[f"in_{name}"] = a
        args.append(nc.dram_tensor(f"in_{name}", a.shape, mybir.dt.from_np(a.dtype), kind="ExternalInput").ap())
    out = nc.dram_tensor("out_rows", tuple(inputs["x"].shape), F32, kind="ExternalOutput").ap()
    flamingo_block(nc, *args, out)
    r = run(nc, [arrays], core_ids=[0])
    return r.results[0]["out_rows"]
```

```python
from contextlib import ExitStack

import concourse.bass as bass
from concourse import mybir

ALU = mybir.AluOpType
ACT = mybir.ActivationFunctionType
AX = mybir.AxisListType
F32 = mybir.dt.float32
F16 = mybir.dt.float16
BF16 = mybir.dt.bfloat16
I32 = mybir.dt.int32
RMAX = bass.bass_isa.ReduceOp.max
RADD = bass.bass_isa.ReduceOp.add

P = 128
LN_EPS = 1e-5
COS_EPS = 1e-8
LOG_ACT = 10
LOG_W = 14
LAT_SHIFT = -15
HID_SHIFT = -45
WX, WG, WF1, WUP, W2E, WDN = range(6)
LO, HI = 0, 1


def flamingo_block(nc, x, ctx, g_xattn, g_ffn, w_xattn, w_gate, w_up, w_down, w_fc1, w_fc2,
                   w_expert, ln_gamma, ln_beta, out):
    B, C, T = x.shape
    INT = w_up.shape[1]
    LAT = w_fc1.shape[1]
    NE = w_gate.shape[1]
    KB = T // P
    IT = INT // P
    LT = LAT // P
    BB = 4
    NB = B // BB
    TOK = BB * C
    UT = LT + IT
    HALF = T // 2
    G = 3
    NR = 4
    CH = T // 32
    UIN = 16 * G * G

    with ExitStack() as es:
        def sb(name, shape, dt):
            return es.enter_context(nc.sbuf_tensor(name, shape, dt))

        def ps(name, shape):
            return es.enter_context(nc.psum_tensor(name, shape, F32))

        def sem(name):
            return es.enter_context(nc.semaphore(name))

        pair_dram = nc.dram_tensor("pair_scratch", (UT, P, 2 * KB * P), F16, kind="Internal").ap()
        side_dram = nc.dram_tensor("side_scratch", (B * T + 2,), F32, kind="Internal").ap()
        self_dram = nc.dram_tensor("self_scratch", (B * T,), F32, kind="Internal").ap()

        big = sb("big", [P, IT * T], F32)
        up_raw = big[:, :].rearrange("p (k i) -> p k i", k=KB)
        dn_raw = big[:, :].rearrange("p (c h) -> p c h", c=IT)
        dn = big[:, :].bitcast(F16).rearrange("p (c s h) -> p c s h", c=IT, s=2)
        fc2_raw = big[:, 0:LT * T].rearrange("p (m h) -> p m h", m=LT)
        fc1_raw = big[:, (KB - 2) * INT:].rearrange("p (k l) -> p k l", k=KB)
        w2_raw = sb("w2", [P, LT, T], F32)
        w2 = w2_raw[:, :, :].bitcast(F16).rearrange("p l (s h) -> p l s h", s=2)
        gate = sb("gate", [P, KB, 2 * NE], F16)
        wx = sb("wx", [P, G, 2, P], F16)
        xT_f = sb("xT", [P, KB * TOK], F32)
        xT = xT_f[:, :].bitcast(F16).rearrange("p (k s t) -> p k s t", k=KB, s=2)
        ctx_first = xT_f[:, :].rearrange("p (j t) -> p j t", j=BB)
        hid = sb("hid", [P, IT * TOK], F32)
        hT = hid[:, :].bitcast(F16).rearrange("p (i s t) -> p i s t", i=IT, s=2)
        x_tail = hid[:, 0:2 * T].rearrange("p (b t) -> p b t", b=2)
        half_hid = IT * TOK // 2
        staging = hid[:, half_hid:].bitcast(F16).rearrange("p (b s k i) -> p b s k i", b=NR, s=2, k=KB)
        lgb = sb("lgb", [P, LT * TOK + 2 * T], F32)
        lat = lgb[:, 0:LT * TOK].bitcast(F16).rearrange("p (l s t) -> p l s t", l=LT, s=2)
        e_raw = lgb[:, 0:LT * TOK].rearrange("p (l m) -> p l m", l=LT)
        gam = lgb[:, LT * TOK:LT * TOK + T]
        bet = lgb[:, LT * TOK + T:]
        ring_f = sb("ring", [P, NR, T], F32)
        ring = ring_f[:, :, :].bitcast(F16).rearrange("p r (s k i) -> p r s k i", s=2, k=KB)
        wx_raw = ring_f[:, 3, 0:G * P]
        gate_raw = ring_f[:, 3, G * P:G * P + KB * NE].rearrange("p (k e) -> p k e", k=KB)
        home = sb("home", [P, BB, T], F32)
        fc1_staging = home[:, 0:2, :].bitcast(F16).rearrange("p b (s k i) -> p b s k i", s=2, k=KB)
        ET = home[:, 2:4, :].rearrange("p a (b l) -> p (a b) l", b=2)
        work = sb("work", [P, 2, T], F32)
        hi_tmp = work[:, 1, :].bitcast(F16).rearrange("p (b h) -> p b h", b=2)
        y = sb("y", [P, T], F32)
        scr_a = sb("scr", [P, T], F32)
        sides_a = sb("sides", [P, T + 2], F32)
        side_a = sb("sim_side", [P, T + 2], F32)
        squares = [y[:, :].bitcast(BF16), sides_a[:, 0:T].bitcast(BF16)]
        hbuf = side_a[:, 0:1024].rearrange("p (b t) -> p b t", b=2)

        def as_pairs(buf):
            return buf.bitcast(F16).rearrange("p (s t) -> p s t", s=2)

        spare = [hid[:, 2 * T + (T + 2) * k:2 * T + (T + 2) * (k + 1)] for k in range(5)]
        scr = [scr_a[:, :], spare[3][:, 0:T]]
        fp = [as_pairs(b) for b in (sides_a[:, :], spare[2], spare[0], spare[1])]
        fp_flat = [b.bitcast(F16) for b in (sides_a[:, :], spare[2], spare[0], spare[1])]
        U = [ring_f[:, 0:G, :].bitcast(F16).rearrange("p g (s t) -> p g s t", s=2),
             lgb[:, 0:G * T].bitcast(F16).rearrange("p (g s t) -> p g s t", g=G, s=2)]
        sim_side = [side_a[:, :], spare[4]]
        sim_self = [ring_f[:, 3, :], bet]
        x_buf = [work[:, 0, :], work[:, 1, :], x_tail[:, 0, :], x_tail[:, 1, :]]
        prod_first = [w2_raw[:, 2, :], w2_raw[:, 3, :]]
        ident = sb("ident", [P, P], F32)
        fold = sb("fold", [P, 32], F32)
        ones_b = sb("ones_b", [P, P], BF16)
        part = sb("part", [P, 2, BB * CH + 1], F32)
        sums = sb("sums", [P, 72], F32)
        nrm = sb("nrm", [P, 36], F32)
        nt = sb("nt", [P, 2, 36], F32)
        simo = sb("simo", [P, 2, 32], F32)
        g_col = sb("g_col", [P, 2], F32)
        th = sb("th", [P, 2], F32)
        amx = sb("amx", [P, 8], F32)
        fro = sb("fro", [P, LT + IT], F32)
        amr = sb("amr", [P, 8], F32)
        wexp = sb("wexp", [P, 8], I32)
        wsc = sb("wsc", [P, 8], F32)
        wp = sb("wp", [P, 8], F32)
        coef = sb("coef", [P, 8], F32)
        c_x, c_s, c_r = (coef[:, k:k + 1] for k in range(3))
        st = sb("st", [P, 3, 2, 6], F32)
        mv = sb("mv", [P, 3, 2], F32)
        sd = sb("sd", [P, 3, 4], F32)
        rs = sb("rs", [P, 3, 2], F32)
        LX, L1, LY = range(3)
        st_x = sb("st_x", [P, BB, 2, 6], F32)
        mv_x = sb("mv_x", [P, BB, 2], F32)
        sd_x = sb("sd_x", [P, 4, BB], F32)
        rs_x = sb("rs_x", [P, 2, BB], F32)
        lg = sb("lg", [P, BB, NE], F32)
        top = sb("top", [P, BB, 8], F32)
        rw = sb("rw", [P, BB], F32)
        zeros = sb("zeros", [P, 2], F32)

        psS = ps("psS", [P, T])
        psR = ps("psR", [P, T])
        psP = ps("psP", [P, G, HALF])
        psM = ps("psM", [P, 512])
        up_bank = [psS[:, 0:512], psS[:, 512:1024], psR[:, 0:512], psR[:, 512:1024]]

        const_rdy = sem("const_rdy")
        small_in = sem("small_in")
        g_in = sem("g_in")
        e_in, f2_in, f1_in, gb_in = sem("e_in"), sem("f2_in"), sem("f1_in"), sem("gb_in")
        upraw_in = [sem(f"upraw_in{k}") for k in range(KB)]
        dnraw_in = [sem(f"dnraw_in{k}") for k in range(IT)]
        x_in = [sem(f"x_in{k}") for k in range(2)]
        x_tail_in = [sem(f"x_tail_in{k}") for k in range(2)]
        ctx_in = sem("ctx_in")
        ctx_first_in = [sem(f"ctx_first_in{k}") for k in range(BB)]
        u_in = [sem(f"u_in{k}") for k in range(2)]
        sim_in = [sem(f"sim_in{k}") for k in range(2)]
        fc1_out = [sem(f"fc1_out{k}") for k in range(2)]
        ring_in = [sem(f"ring_in{k}") for k in range(NR)]
        stg_out = [sem(f"stg_out{k}") for k in range(NR)]
        simrow_out, edge_out = sem("simrow_out"), sem("edge_out")
        out_done = sem("out_done")
        tanh_rdy = sem("tanh_rdy")
        amax_rdy, amax_all = sem("amax_rdy"), sem("amax_all")
        scale_rdy = sem("scale_rdy")
        gb_rdy = sem("gb_rdy")
        wxT_done, wx_hi, wx_rdy = sem("wxT_done"), sem("wx_hi"), sem("wx_rdy")
        gate_hi, gate_w_rdy = sem("gate_hi"), sem("gate_w_rdy")
        eT_done, eT_rdy = sem("eT_done"), sem("eT_rdy")
        w2_done, w2_out, w2_rdy = sem("w2_done"), sem("w2_out"), sem("w2_rdy")
        fc1_hi, fc1_rdy, w2_sq, dn_sq = sem("fc1_hi"), sem("fc1_rdy"), sem("w2_sq"), sem("dn_sq")
        sq_rdy, sq_used, norms_read = sem("sq_rdy"), sem("sq_used"), sem("norms_read")
        stg_hi, stg_rdy = sem("stg_hi"), sem("stg_rdy")
        pair_hi, pair_lo, pair_rdy = sem("pair_hi"), sem("pair_lo"), sem("pair_rdy")
        prod1, prod0 = sem("prod1"), sem("prod0")
        prod_used = sem("prod_used")
        part_rdy = sem("part_rdy")
        pads_rdy = sem("pads_rdy")
        sums_done, s0_rdy, nrm_rdy, simo_rdy = sem("sums_done"), sem("s0_rdy"), sem("nrm_rdy"), sem("simo_rdy")
        var_rdy = [sem(f"var_rdy{k}") for k in range(3)]
        std_rdy = [sem(f"std_rdy{k}") for k in range(3)]
        rs_rdy = [sem(f"rs_rdy{k}") for k in range(3)]
        f_hi, f_rdy = sem("f_hi"), sem("f_rdy")
        p_done, comb = sem("p_done"), sem("comb")
        xn_rdy, tr_done, xt_hi, xt_rdy = sem("xn_rdy"), sem("tr_done"), sem("xt_hi"), sem("xt_rdy")
        home_rdy = sem("home_rdy")
        up_done, up_evac = sem("up_done"), sem("up_evac")
        relu_rdy, sq_hid, h_hi, h_rdy = sem("relu_rdy"), sem("sq_hid"), sem("h_hi"), sem("h_rdy")
        l_hi, l_rdy = sem("l_hi"), sem("l_rdy")
        gate_done, rw_rdy = sem("gate_done"), sem("rw_rdy")
        s_done, r_done, s_evac, r_evac = sem("s_done"), sem("r_done"), sem("s_evac"), sem("r_evac")
        y_nrm, y_fin = sem("y_nrm"), sem("y_fin")

        SIM_T = 2
        UP_ORDER = [2, 3, 4, 5, 6, 7, 0, 1]
        UP_SQ = ((), (2, 3, 4), (5, 6, 7), (0, 1))
        SUMS_T = 16
        LNX_T = 18
        DN_ORDER = list(range(0, IT, 2)) + list(range(1, IT, 2))
        DLOAD_T, DSQ_T = NR, 6
        PAIRS_AT = {4: (0, 2), 5: (2, 4), 14: (4, 6), 15: (6, 8), 16: (8, 11), 17: (11, 14),
                    18: (14, 17), 19: (17, 20)}
        SCALE_T = 14
        S_CUTS = (9, 12)

        def pair_chunk(c):
            if c < LT:
                return w2_raw[:, c, :], w2[:, c], W2E
            d = DN_ORDER[c - LT]
            return dn_raw[:, d, :], dn[:, d], WDN

        block = es.enter_context(nc.Block())

        @block.sync
        def _(sp):
            def ahead(value):
                return value if isinstance(value, int) else sp.snap(sp.to_reg(value))

            def load_x(m, j, slot):
                sp.dma_start(work[:, slot, :], x[bass.ds(BB * m + j, 1)].rearrange("o p t -> p (o t)"))\
                    .then_inc(x_in[slot], 16)

            def load_ctx(m, j):
                q = BB * m + j
                if j > 0:
                    sp.wait_ge(prod_used, 2 * q)
                sp.dma_start(scr[0], ctx[bass.ds(q, 1)].rearrange("o p t -> p (o t)"))\
                    .then_inc(ctx_in, 16)

            def store_sims(m):
                sp.wait_ge(simo_rdy, m + 1)
                first = BB * T * m
                sp.dma_start(side_dram[bass.ds(first + 2, BB * T)].rearrange("(c t) -> c t", t=32), simo[:, 0, :])\
                    .then_inc(simrow_out, 16)
                sp.dma_start(self_dram[bass.ds(first, BB * T)].rearrange("(c t) -> c t", t=32), simo[:, 1, :])\
                    .then_inc(simrow_out, 16)

            def unfold_into(j):
                for g in range(G):
                    for k in range(G):
                        p0 = (k - P * g) % G
                        c0 = (P * g + p0) // G
                        num = (P - p0 + G - 1) // G
                        sp.dma_start(U[j % 2][p0:p0 + G * (num - 1) + 1:G, g, :, :],
                                     fp[j][c0:c0 + num, :, k:k + T]).then_inc(u_in[j % 2], 16)

            def sims_into(q, b):
                side = side_dram[bass.ds(q * T + 1, T + 1)].rearrange("(a t) -> a t", a=1)
                same = self_dram[bass.ds(q * T, T)].rearrange("(a t) -> a t", a=1)
                sp.dma_start(sim_side[b][:, 0:T + 1], side.broadcast_to([P, T + 1])).then_inc(sim_in[b], 16)
                sp.dma_start(sim_self[b], same.broadcast_to([P, T])).then_inc(sim_in[b], 16)

            def phase_a_loads(m, j):
                q = BB * m + j
                f_count, pad_count = ahead(q + 1), ahead(m + 1)
                used = ahead(2 * q if j > 0 else UT * m)
                rows, combined, hidden = ahead(32 * (m + 1)), ahead(q), ahead(IT * m)
                sp.wait_ge(f_rdy, f_count)
                sp.wait_ge(pads_rdy, pad_count)
                if j > 0:
                    sp.wait_ge(p_done, used)
                else:
                    sp.wait_ge(up_done, used)
                unfold_into(0)
                sp.wait_ge(simrow_out, rows)
                if j > 0:
                    sp.wait_ge(rs_rdy[L1], combined)
                else:
                    sp.wait_ge(h_rdy, hidden)
                sims_into(q, 0)
                if 1 <= j < BB - 1:
                    sp.wait_ge(home_rdy, BB * m + j)
                    load_x(m, j + 1, (j + 1) % 2)

            def first_unfold(j):
                sp.wait_ge(f_rdy, j + 1)
                sp.wait_ge(pads_rdy, 1)
                if j >= 2:
                    sp.wait_ge(p_done, 2 * (j - 1))
                if j == 1:
                    sp.wait_ge(eT_done, LT)
                unfold_into(j)

            def first_sims(j):
                b = j % 2
                sp.wait_ge(simrow_out, 32)
                sp.wait_ge(edge_out, 16)
                if j >= 2:
                    sp.wait_ge(rs_rdy[L1], j - 1)
                if j == 0:
                    sp.wait_ge(wxT_done, 1)
                    sp.wait_ge(gate_w_rdy, 1)
                sims_into(j, b)

            def up_half(n, phase_a, first=False):
                m = n + 1
                for t in range(UT):
                    if t == 0:
                        sp.wait_ge(p_done, 2 * BB * m)
                    if t == G:
                        sp.wait_ge(rs_rdy[L1], BB * m)
                    if t >= NR:
                        sp.wait_ge(up_done, UT * n + t - NR + 1)
                    if first and t < LT:
                        sp.wait_ge(fc1_out[t % 2], 16 * (t // 2 + 1))
                    elif first:
                        sp.wait_ge(stg_out[t % NR], 16 * ((t - LT) // NR + 1))
                    sp.dma_start(ring_f[:, t % NR, :].bitcast(F16), pair_dram[t])\
                        .then_inc(ring_in[t % NR], 16)
                    if first and DLOAD_T <= t < DLOAD_T + IT // 2:
                        for c in DN_ORDER[2 * (t - DLOAD_T):2 * (t - DLOAD_T) + 2]:
                            sp.wait_ge(stg_rdy, IT // 2 if c % 2 == 0 else IT)
                            sp.dma_start(dn_raw[:, c, :], w_down[P * c:P * c + P, :])\
                                .then_inc(dnraw_in[c], 16)
                    if phase_a:
                        if t == NR - 1:
                            sp.wait_ge(tr_done, 2 * BB * m)
                            load_ctx(m, 0)
                            sp.wait_ge(home_rdy, BB * m - 1)
                            load_x(m, 0, 0)
                            if not first:
                                sp.wait_ge(home_rdy, BB * m)
                                load_x(m, 1, 1)
                        for j in range(1, BB):
                            if t == 4 * j + 5:
                                load_ctx(m, j)
                if phase_a:
                    store_sims(m)
                    if first:
                        sp.wait_ge(pair_rdy, LT + IT)
                        load_x(m, 1, 1)

            sp.dma_start(g_col[:, 0:1], g_xattn.rearrange("(a b) -> a b", a=1).broadcast_to([P, 1]))\
                .then_inc(g_in, 16)
            sp.dma_start(g_col[:, 1:2], g_ffn.rearrange("(a b) -> a b", a=1).broadcast_to([P, 1]))\
                .then_inc(g_in, 16)
            load_x(0, 0, 0)
            load_x(0, 1, 1)
            for j in range(2):
                sp.dma_start(x_tail[:, j, :], x[2 + j]).then_inc(x_tail_in[j], 16)
            sp.dma_start(wx_raw, w_xattn.rearrange("o c k -> o (c k)")).then_inc(small_in, 16)
            sp.dma_start(gate_raw, w_gate.rearrange("(k p) e -> p k e", p=P)).then_inc(small_in, 16)
            sp.dma_start(fc2_raw, w_fc2.rearrange("(m p) h -> p m h", p=P)).then_inc(f2_in, 16)
            sp.wait_ge(const_rdy, 1)
            sp.dma_start(side_dram[0:2].rearrange("(a t) -> a t", a=1), zeros[0:1, :]).then_inc(edge_out, 16)
            first_unfold(0)
            first_unfold(1)
            store_sims(0)
            first_sims(0)
            first_sims(1)
            for j in range(2, BB):
                first_unfold(j)
                first_sims(j)
            sp.wait_ge(p_done, 2 * BB)
            sp.wait_ge(rs_rdy[L1], BB)
            sp.dma_start(gam, ln_gamma.rearrange("(a h) -> a h", a=1).broadcast_to([P, T]))\
                .then_inc(gb_in, 16)
            sp.dma_start(bet, ln_beta.rearrange("(a h) -> a h", a=1).broadcast_to([P, T]))\
                .then_inc(gb_in, 16)
            up_half(0, True, first=True)
            for j in range(BB):
                phase_a_loads(1, j)
            with sp.Fori(1, NB - 1) as n:
                up_half(n, True)
                for j in range(BB):
                    phase_a_loads(n + 1, j)
            up_half(NB - 1, False)
            sp.wait_ge(out_done, 16 * B)

        @block.gpsimd
        def _(pool):
            def products(m, j):
                q = BB * m + j
                pool.wait_ge(ctx_in, 16 * (q - BB + 1))
                if j > 0:
                    pool.wait_ge(prod_used, 2 * q - 1)
                else:
                    pool.wait_ge(u_in[0], UIN * (q - 2))
                pool.tensor_tensor(sides_a[:, 0:T - 1], scr[0][:, 0:T - 1], scr[0][:, 1:T], ALU.mult)
                pool.memset(sides_a[:, T - 1:T], 0.0)
                pool.drain().then_inc(prod1, 1)
                pool.tensor_tensor(scr[0], scr[0], scr[0], ALU.mult).then_inc(prod0, 1)

            def pad(b):
                for c0, c1 in ((0, 1), (T + 1, T + 3), (2 * T + 3, 2 * T + 4)):
                    pool.tensor_tensor(fp_flat[b][:, c0:c1], zeros[:, 0:c1 - c0], zeros[:, 0:c1 - c0], ALU.add)

            def pads(m):
                pool.wait_ge(part_rdy, m + 1)
                pad(0)
                pool.drain().then_inc(pads_rdy, 1)

            def finish(n, j):
                pool.wait_ge(y_nrm, BB * n + j + 1)
                pool.tensor_tensor(y[:, :], y[:, :], gam, ALU.mult)
                pool.drain()
                pool.tensor_tensor(y[:, :], y[:, :], home[:, j, :], ALU.add)
                pool.drain().then_inc(y_fin, 1)

            def keep(m, j):
                pool.wait_ge(rs_rdy[L1], BB * m + j + 1)
                pool.wait_ge(xn_rdy, BB * m + j + 1)
                pool.tensor_tensor(home[:, j, :], work[:, j % 2, :], bet, ALU.add).then_inc(home_rdy, 1)

            def move_his(c0, c1):
                for c in range(c0, c1):
                    pool.wait_ge(pair_lo, c + 1)
                    pool.tensor_scalar(pair_chunk(c)[1][:, HI, :], hi_tmp[:, c % 2, :], 1.0, 1.0, ALU.mult,
                                       ALU.mult).then_inc(pair_rdy, 1)

            pool.memset(zeros[:, :], 0.0)
            pool.memset(ident[:, :], 0.0)
            pool.memset(ones_b[:, :], 1.0)
            pool.memset(fold[:, :], 0.0)
            pool.memset(part[:, :, BB * CH:], 1.0)
            for b in range(2):
                pool.memset(prod_first[b][:, T - 1:T], 0.0)
            pool.drain()
            pool.affine_select(out=ident[:, :], in_=ident[:, :], compare_op=ALU.not_equal, fill=1.0,
                               base=0, pattern=[[-1, P]], channel_multiplier=1)
            for k in range(4):
                pool.affine_select(out=fold[:, :], in_=fold[:, :], compare_op=ALU.not_equal, fill=1.0,
                                   base=-32 * k, pattern=[[-1, 32]], channel_multiplier=1)
                pool.drain()
            for b in range(BB):
                pad(b)
            pool.drain().then_inc(pads_rdy, 1)
            pool.drain().then_inc(const_rdy, 1)
            for j in range(BB):
                pool.wait_ge(ctx_first_in[j], 16)
                if j >= 2:
                    pool.wait_ge(prod_used, 2 * (j - 2) + 1)
                c = ctx_first[:, j, :]
                pool.tensor_tensor(prod_first[j % 2][:, 0:T - 1], c[:, 0:T - 1], c[:, 1:T], ALU.mult)\
                    .then_inc(prod1, 1)
            pool.wait_ge(amax_rdy, 1)
            pool.partition_all_reduce(amr[:, WX:WG + 1], amx[:, WX:WG + 1], P, RMAX).then_inc(amax_all, 1)
            pool.wait_ge(amax_rdy, 2)
            pool.partition_all_reduce(amr[:, WF1:WF1 + 1], amx[:, WF1:WF1 + 1], P, RADD).then_inc(amax_all, 1)
            for j in range(BB):
                if j == 0:
                    for k in range(2):
                        pool.wait_ge(fc1_out[k], 32)
                if j == 2:
                    pool.wait_ge(w2_done, LT)
                pool.wait_ge(xn_rdy, j + 1)
                pool.tensor_scalar(home[:, j, :], x_buf[j], 1.0, 1.0, ALU.mult, ALU.mult)\
                    .then_inc(home_rdy, 1)
            pool.wait_ge(amax_rdy, 3)
            pool.partition_all_reduce(amr[:, W2E:W2E + 1], amx[:, W2E:W2E + 1], P, RADD).then_inc(amax_all, 1)

            def up_half(n, first=False):
                if first:
                    pool.wait_ge(gb_in, 32)
                    pool.tensor_scalar(gam, gam, th[:, 1:2], 1.0, ALU.mult, ALU.mult)
                    pool.tensor_scalar(bet, bet, th[:, 1:2], 1.0, ALU.mult, ALU.mult)
                    pool.drain()
                for j in range(BB):
                    products(n + 1, j)
                    if first and j == 0:
                        move_his(0, LT)
                    if first and j <= 1:
                        for k in range(2 * j, 2 * j + 2):
                            pool.tensor_tensor(home[:, k, :], home[:, k, :], bet, ALU.add)
                if first:
                    pool.wait_ge(amax_rdy, 4)
                    pool.partition_all_reduce(amr[:, WDN:WDN + 1], amx[:, WDN:WDN + 1], P, RADD)\
                        .then_inc(amax_all, 1)
                    move_his(LT, LT + IT)
                pads(n + 1)

            def down_half(n, phase_a):
                for j in range(BB):
                    finish(n, j)
                    if phase_a:
                        keep(n + 1, j)

            up_half(0, first=True)
            down_half(0, True)
            with pool.Fori(1, NB - 1) as n:
                up_half(n)
                down_half(n, True)
            down_half(NB - 1, False)

        @block.scalar
        def _(act):
            def std(k, q):
                act.wait_ge(var_rdy[k], q + 1)
                act.activation(sd[:, k, 1:2], sd[:, k, 0:1], ACT.Sqrt).then_inc(std_rdy[k], 1)

            def norms(m):
                act.wait_ge(s0_rdy, m + 1)
                act.activation(nrm[:, 0:33], sums[:, 0:33], ACT.Sqrt).then_inc(nrm_rdy, 1)

            def f_pairs(m, j):
                first = isinstance(m, int) and m == 0
                q = BB * m + j
                b = j % 2 if first else 0
                act.wait_ge(rs_rdy[LX], q + 1)
                if first:
                    act.wait_ge(pads_rdy, 1)
                    if j >= 2:
                        act.wait_ge(f_rdy, j - 1)
                else:
                    act.wait_ge(part_rdy, m + 1)
                    if j > 0:
                        act.wait_ge(tr_done, 2 * q)
                        act.wait_ge(u_in[0], UIN * (q - 2))
                act.activation(scr[b], x_buf[j] if first else work[:, j % 2, :], ACT.Identity,
                               bias=rs[:, LX, 1:2] if not first else rs_x[:, 1, j:j + 1],
                               scale=rs[:, LX, 0:1] if not first else rs_x[:, 0, j:j + 1])
                act.drain()
                act.activation(fp[j if first else 0][:, 0, 1:T + 1], scr[b], ACT.Copy).then_inc(f_hi, 1)

            def x1_normal(m, j):
                first = isinstance(m, int) and m == 0
                q = BB * m + j
                act.wait_ge(rs_rdy[L1], q + 1)
                act.activation(scr[j % 2 if first else 0], x_buf[j] if first else work[:, j % 2, :],
                               ACT.Identity, bias=rs[:, L1, 1:2], scale=rs[:, L1, 0:1]).then_inc(xn_rdy, 1)

            def xt_his(m, j, h):
                bank = psM[:, :] if isinstance(m, int) and m == 0 else psP[:, h, :]
                act.wait_ge(tr_done, 2 * (BB * m + j) + h + 1)
                act.activation(xT[:, 4 * h:4 * h + 4, 0, P * j:P * j + P],
                               bank.rearrange("p (k t) -> p k t", k=4), ACT.Copy).then_inc(xt_hi, 1)

            def finish(n, j):
                q = BB * n + j
                std(LY, q)
                act.wait_ge(rs_rdy[LY], q + 1)
                act.activation(y[:, :], y[:, :], ACT.Identity, bias=rs[:, LY, 1:2],
                               scale=rs[:, LY, 0:1]).then_inc(y_nrm, 1)
                act.wait_ge(y_fin, q + 1)
                act.dma_start(out[bass.ds(q, 1)].rearrange("o p t -> p (o t)"), y[:, :])\
                    .then_inc(out_done, 16)

            def take_s(n, j, phase_a):
                act.wait_ge(s_done, BB * n + j + 1)
                if not (isinstance(n, int) and BB * n + j == 0):
                    act.wait_ge(out_done, 16 * (BB * n + j))
                act.activation(y[:, :], psS[:, :], ACT.Copy, scale=c_s).then_inc(s_evac, 1)

            def up_half(n, phase_a, first=False):
                m = n + 1
                for t in range(UT):
                    if first and t < NR:
                        for it in range(NR * t, NR * t + NR):
                            tile_hi(it)
                            if it > 0:
                                tile_out(it - 1)
                        if t == NR - 1:
                            tile_out(IT - 1)
                    if first and t == LT + 8:
                        for k in range(NR):
                            act.wait_ge(stg_out[k], 16 * (IT // NR))
                    act.wait_ge(up_done, UT * n + t + 1)
                    bank = up_bank[t % NR]
                    if t < LT:
                        act.activation(lat[:, t, 0, :], bank, ACT.Copy, scale=2.0 ** LAT_SHIFT)\
                            .then_inc(l_hi, 1)
                    else:
                        i = IT * n + t - LT
                        buf = hbuf[:, t % 2, :]
                        if t >= LT + 2:
                            act.wait_ge(h_rdy, i - 1)
                        act.activation(buf, bank, ACT.Relu, scale=2.0 ** HID_SHIFT).then_inc(relu_rdy, 1)
                        act.wait_ge(sq_hid, i + 1)
                        act.activation(hT[:, t - LT, 0, :], buf, ACT.Copy).then_inc(h_hi, 1)
                    if phase_a and t == SUMS_T + 1:
                        norms(m)
                    if phase_a and t == LNX_T:
                        std(LX, BB * m)
                    if first and DSQ_T <= t < DSQ_T + IT // 2:
                        if t == DSQ_T:
                            act.wait_ge(pair_rdy, LT)
                        for c in range(2 * (t - DSQ_T), 2 * (t - DSQ_T) + 2):
                            act.wait_ge(dnraw_in[DN_ORDER[c]], 16)
                            act.activation(hi_tmp[:, 0, :].bitcast(BF16), dn_raw[:, DN_ORDER[c], :], ACT.Square,
                                           accum_out=fro[:, LT + c:LT + c + 1])
                            act.drain().then_inc(dn_sq, 1)
                    if first and t in PAIRS_AT:
                        for c in range(*PAIRS_AT[t]):
                            chunk_hi(c)

            def chunk_hi(c):
                raw, _, k = pair_chunk(c)
                act.wait_ge(scale_rdy, 4 if c < LT else 5)
                if c >= 2:
                    act.wait_ge(pair_rdy, c - 1)
                else:
                    act.wait_ge(home_rdy, BB)
                if c == LT:
                    act.wait_ge(dn_sq, IT)
                act.activation(hi_tmp[:, c % 2, :], raw, ACT.Copy, scale=wsc[:, k:k + 1])\
                    .then_inc(pair_hi, 1)

            def tile_hi(it):
                act.wait_ge(scale_rdy, 3)
                if it >= NR:
                    act.wait_ge(stg_out[it % NR], 16 * (it // NR))
                act.activation(staging[:, it % NR, 0, :, :], up_raw[:, :, P * it:P * it + P], ACT.Copy,
                               scale=wsc[:, WUP:WUP + 1]).then_inc(stg_hi, 1)

            def tile_out(it):
                act.wait_ge(stg_rdy, it + 1)
                act.dma_start(pair_dram[LT + it], staging[:, it % NR].rearrange("p s k i -> p (s k i)"))\
                    .then_inc(stg_out[it % NR], 16)

            def down_half(n, phase_a):
                m = n + 1
                for j in range(BB):
                    if phase_a:
                        f_pairs(m, j)
                    if j > 0:
                        finish(n, j - 1)
                    if phase_a:
                        std(L1, BB * m + j)
                        x1_normal(m, j)
                        if j < BB - 1:
                            std(LX, BB * m + j + 1)
                    take_s(n, j, phase_a)
                    if phase_a:
                        for h in range(2):
                            xt_his(m, j, h)
                finish(n, BB - 1)

            def load_up(k):
                act.dma_start(up_raw[:, k, :], w_up[k * P:(k + 1) * P, :]).then_inc(upraw_in[k], 16)

            def up_squares(k):
                n = UP_ORDER.index(k)
                act.wait_ge(upraw_in[k], 16)
                if n >= 2:
                    act.wait_ge(sq_used, n - 1)
                elif n == 1:
                    act.wait_ge(u_in[0], UIN)
                act.activation(squares[n % 2], up_raw[:, k, :], ACT.Square).then_inc(sq_rdy, 1)

            def w2_evac(l):
                act.wait_ge(w2_done, l + 1)
                if l == 2:
                    act.wait_ge(part_rdy, 1)
                act.activation(w2_raw[:, l, :], (psS if l % 2 == 0 else psR)[:, :], ACT.Copy)\
                    .then_inc(w2_out, 1)

            for j in range(BB):
                act.dma_start(ctx_first[:, j, :], ctx[j]).then_inc(ctx_first_in[j], 16)
            act.dma_start(e_raw, w_expert.rearrange("(l p) m -> p l m", p=P)).then_inc(e_in, 16)
            act.dma_start(fc1_raw, w_fc1.rearrange("(k p) l -> p k l", p=P)).then_inc(f1_in, 16)
            for k in UP_ORDER[0:4]:
                load_up(k)
            act.wait_ge(g_in, 32)
            act.activation(th[:, :], g_col[:, :], ACT.Tanh).then_inc(tanh_rdy, 1)
            act.wait_ge(var_rdy[LX], BB)
            act.activation(sd_x[:, 1, :], sd_x[:, 0, :], ACT.Sqrt).then_inc(std_rdy[LX], BB)
            for j in range(BB):
                act.wait_ge(prod1, j + 1)
                act.activation(ctx_first[:, j, :], ctx_first[:, j, :], ACT.Square).then_inc(prod0, 1)
                if j == 2:
                    act.wait_ge(scale_rdy, 1)
                    act.wait_ge(wxT_done, 1)
                    act.activation(wx[:, :, 0, :], psM[:, 0:G * P].rearrange("p (g o) -> p g o", g=G), ACT.Copy,
                                   scale=wsc[:, WX:WX + 1]).then_inc(wx_hi, 1)
                    act.activation(gate[:, :, 0:NE], gate_raw, ACT.Copy, scale=wsc[:, WG:WG + 1])\
                        .then_inc(gate_hi, 1)
                f_pairs(0, j)
                if j == 1:
                    for k in range(LT):
                        act.wait_ge(eT_done, k + 1)
                        act.activation(ET[:, k, :], up_bank[k], ACT.Copy).then_inc(eT_rdy, 1)
            act.wait_ge(f1_in, 16)
            act.activation(home[:, 0:2, :].bitcast(BF16).rearrange("p b (k l) -> p (b k) l", l=LAT), fc1_raw,
                           ACT.Square, accum_out=amx[:, WF1:WF1 + 1]).then_inc(amax_rdy, 1)
            w2_evac(0)
            w2_evac(1)
            norms(0)
            for t in range(LT):
                act.wait_ge(scale_rdy, 2)
                if t >= 2:
                    act.wait_ge(fc1_out[t % 2], 16 * (t // 2))
                act.activation(fc1_staging[:, t % 2, 0], fc1_raw[:, :, P * t:P * t + P], ACT.Copy,
                               scale=wsc[:, WF1:WF1 + 1]).then_inc(fc1_hi, 1)
                act.wait_ge(fc1_rdy, t + 1)
                act.dma_start(pair_dram[t], fc1_staging[:, t % 2].rearrange("p s k i -> p (s k i)"))\
                    .then_inc(fc1_out[t % 2], 16)
            for k in UP_ORDER[4:6]:
                load_up(k)
            w2_evac(2)
            for j in range(BB):
                for k in UP_SQ[j]:
                    up_squares(k)
                std(L1, j)
                x1_normal(0, j)
                if j >= 1:
                    xt_his(0, j - 1, 1)
                act.wait_ge(part_rdy, 1)
                xt_his(0, j, 0)
                if j == 0:
                    w2_evac(3)
                    for k in UP_ORDER[6:8]:
                        load_up(k)
                    for l in range(LT):
                        act.activation(squares[0][:, 0:T], w2_raw[:, l, :], ACT.Square,
                                       accum_out=fro[:, l:l + 1])
                        act.drain().then_inc(w2_sq, 1)
            xt_his(0, BB - 1, 1)
            act.wait_ge(tr_done, 2 * BB)
            act.wait_ge(rs_rdy[L1], BB)
            for b in range(2):
                act.wait_ge(u_in[b], 2 * UIN)
            act.wait_ge(home_rdy, BB)

            up_half(0, True, first=True)
            down_half(0, True)
            with act.Fori(1, NB - 1) as n:
                up_half(n, True)
                down_half(n, True)
            up_half(NB - 1, False)
            down_half(NB - 1, False)

        @block.vector
        def _(dve):
            def stats(k, src, mvk, sdk):
                for h in range(2):
                    dve.bn_stats(st[:, k, h, :], src[:, HALF * h:HALF * h + HALF])
                dve.drain()
                dve.bn_aggr(mvk, st[:, k, :, :].rearrange("p h s -> p (h s)"))
                dve.drain()
                dve.tensor_scalar(sdk[:, 0:1], mvk[:, 1:2], LN_EPS, None, ALU.add).then_inc(var_rdy[k], 1)

            def scale_bias(k, q, scale, mvk, sdk, rsk):
                dve.wait_ge(std_rdy[k], q + 1)
                dve.reciprocal(sdk[:, 2:3], sdk[:, 1:2])
                dve.drain()
                dve.tensor_scalar(sdk[:, 3:4], sdk[:, 2:3], sdk[:, 2:3], sdk[:, 0:1], ALU.mult, ALU.mult)
                dve.drain()
                dve.tensor_scalar(sdk[:, 3:4], sdk[:, 3:4], -0.5, 1.5, ALU.mult, ALU.add)
                dve.drain()
                dve.scalar_tensor_tensor(out=rsk[:, 0:1], in0=sdk[:, 2:3], scalar=scale,
                                         in1=sdk[:, 3:4], op0=ALU.mult, op1=ALU.mult)
                dve.drain()
                dve.scalar_tensor_tensor(out=rsk[:, 1:2], in0=mvk[:, 0:1], scalar=-1.0,
                                         in1=rsk[:, 0:1], op0=ALU.mult, op1=ALU.mult)
                dve.drain().then_inc(rs_rdy[k], 1)

            def normalise(k, q, src, scale):
                stats(k, src, mv[:, k, :], sd[:, k, :])
                scale_bias(k, q, scale, mv[:, k, :], sd[:, k, :], rs[:, k, :])

            def sum_products(m, j, which):
                first = isinstance(m, int) and m == 0
                q = BB * m + j
                if which == 1:
                    dve.wait_ge(prod1, q + 1)
                    if j == 0 and not (isinstance(m, int) and m <= 1):
                        dve.wait_ge(out_done, 16 * BB * (m - 1))
                    src = prod_first[j % 2] if first else sides_a[:, 0:T]
                else:
                    dve.wait_ge(prod0, q + 1)
                    src = ctx_first[:, j, :] if first else scr[0]
                dve.transpose(y[:, :], src).then_inc(prod_used, 1)
                dve.drain()
                dve.tensor_reduce(part[:, which, CH * j:CH * j + CH],
                                  y[:, :].rearrange("p (c a) -> p c a", a=32), AX.X, ALU.add)
                if which == 0 and j == BB - 1:
                    dve.drain().then_inc(part_rdy, 1)
                else:
                    dve.drain()

            def cosines(m):
                dve.wait_ge(sums_done, m + 1)
                dve.tensor_copy(sums[:, 0:65], psM[:, 0:65])
                dve.drain().then_inc(s0_rdy, 1)
                dve.wait_ge(nrm_rdy, m + 1)
                a, b, c = nrm[:, 0:33], nt[:, 0, 0:33], nt[:, 1, 0:33]
                dve.tensor_scalar(a, a, COS_EPS, None, ALU.max)
                dve.drain()
                dve.reciprocal(b, a)
                dve.drain()
                dve.tensor_tensor(c, sums[:, 0:33], b, ALU.mult)
                dve.drain()
                dve.tensor_tensor(a, a, c, ALU.add)
                dve.drain()
                dve.tensor_scalar(a, a, 0.5, COS_EPS, ALU.mult, ALU.max)
                dve.drain()
                dve.tensor_tensor(nt[:, 0, 0:32], nrm[:, 0:32], nrm[:, 1:33], ALU.mult)
                dve.tensor_tensor(nt[:, 1, 0:32], nrm[:, 0:32], nrm[:, 0:32], ALU.mult)
                dve.drain()
                dve.reciprocal(nt[:, :, 0:32], nt[:, :, 0:32])
                dve.drain()
                if not (isinstance(m, int) and m == 0):
                    dve.wait_ge(simrow_out, 32 * m)
                dve.tensor_tensor(simo[:, 0, :], sums[:, 33:65], nt[:, 0, 0:32], ALU.mult)
                dve.tensor_tensor(simo[:, 1, :], sums[:, 0:32], nt[:, 1, 0:32], ALU.mult)
                dve.drain().then_inc(simo_rdy, 1)

            def f_los(m, j):
                first = isinstance(m, int) and m == 0
                f, pair = (scr[j % 2], fp[j]) if first else (scr[0], fp[0])
                dve.wait_ge(f_hi, BB * m + j + 1)
                dve.tensor_tensor(pair[:, 1, 1:T + 1], f, pair[:, 0, 1:T + 1], ALU.subtract)\
                    .then_inc(f_rdy, 1)

            def combine(m, j):
                first = isinstance(m, int) and m == 0
                q = BB * m + j
                xr = x_buf[j] if first else work[:, j % 2, :]
                b = j % 2 if first else 0
                if first:
                    dve.wait_ge(sim_in[b], 32 * (j // 2 + 1))
                else:
                    dve.wait_ge(sim_in[0], 32 * (q - 1))
                for h in range(2):
                    t0 = HALF * h
                    dve.wait_ge(p_done, 2 * q + h + 1)
                    xh = xr[:, t0:t0 + HALF]
                    left, right = scr[b][:, 0:HALF], scr[b][:, HALF:T]
                    same = sim_self[b][:, t0:t0 + HALF]
                    dve.scalar_tensor_tensor(out=left, in0=psP[:, 0, :], scalar=c_x,
                                             in1=sim_side[b][:, t0:t0 + HALF], op0=ALU.mult, op1=ALU.mult)
                    dve.scalar_tensor_tensor(out=same, in0=psP[:, 1, :], scalar=c_x, in1=same,
                                             op0=ALU.mult, op1=ALU.mult)
                    dve.scalar_tensor_tensor(out=right, in0=psP[:, 2, :], scalar=c_x,
                                             in1=sim_side[b][:, t0 + 1:t0 + HALF + 1], op0=ALU.mult,
                                             op1=ALU.mult)
                    dve.drain().then_inc(comb, 1)
                    dve.tensor_tensor(left, left, same, ALU.add)
                    dve.tensor_tensor(xh, xh, right, ALU.add)
                    dve.drain()
                    dve.tensor_tensor(xh, xh, left, ALU.add)
                    dve.drain()
                normalise(L1, q, xr, 2.0 ** LOG_ACT)

            def x_stats(m, j):
                dve.wait_ge(x_in[j % 2], (2 * m + j // 2) * 16)
                normalise(LX, BB * m + j, work[:, j % 2, :], 2.0 ** LOG_ACT)

            def x_stats_first():
                for j in range(BB):
                    dve.wait_ge(x_in[j] if j < 2 else x_tail_in[j - 2], 16)
                    for h in range(2):
                        dve.bn_stats(st_x[:, j, h, :], x_buf[j][:, HALF * h:HALF * h + HALF])
                dve.drain()
                for j in range(BB):
                    dve.bn_aggr(mv_x[:, j, :], st_x[:, j, :, :].rearrange("p h s -> p (h s)"))
                dve.drain()
                v, s, r, c = (sd_x[:, k, :] for k in range(4))
                dve.tensor_scalar(v, mv_x[:, :, 1], LN_EPS, None, ALU.add)
                dve.drain().then_inc(var_rdy[LX], BB)
                dve.wait_ge(std_rdy[LX], BB)
                dve.reciprocal(r, s)
                dve.drain()
                dve.tensor_tensor(c, r, r, ALU.mult)
                dve.drain()
                dve.tensor_tensor(c, c, v, ALU.mult)
                dve.drain()
                dve.tensor_scalar(c, c, -0.5, 1.5, ALU.mult, ALU.add)
                dve.drain()
                dve.scalar_tensor_tensor(out=rs_x[:, 0, :], in0=r, scalar=2.0 ** LOG_ACT, in1=c,
                                         op0=ALU.mult, op1=ALU.mult)
                dve.drain()
                dve.scalar_tensor_tensor(out=rs_x[:, 1, :], in0=mv_x[:, :, 0], scalar=-1.0,
                                         in1=rs_x[:, 0, :], op0=ALU.mult, op1=ALU.mult)
                dve.drain().then_inc(rs_rdy[LX], BB)

            def xt_los(m, j, halves=(0, 1)):
                for h in halves:
                    bank = psM[:, :] if isinstance(m, int) and m == 0 else psP[:, h, :]
                    dve.wait_ge(xt_hi, 2 * (BB * m + j) + h + 1)
                    dst = xT[:, 4 * h:4 * h + 4, :, P * j:P * j + P]
                    dve.tensor_tensor(dst[:, :, 1, :], bank.rearrange("p (k t) -> p k t", k=4),
                                      dst[:, :, 0, :], ALU.subtract).then_inc(xt_rdy, 1)

            def pow2(lo, hi, src, mult, add):
                dve.tensor_scalar(src, src, 2.0 ** -80, None, ALU.max)
                dve.drain()
                dve.tensor_scalar(wexp[:, lo:hi], src.bitcast(I32), mult, add, ALU.mult, ALU.add)
                dve.drain()
                dve.tensor_scalar(wsc[:, lo:hi].bitcast(I32), wexp[:, lo:hi], -2.0 ** 23,
                                  (254 + LOG_W) * 2.0 ** 23, ALU.mult, ALU.add)
                dve.tensor_scalar(wp[:, lo:hi].bitcast(I32), wexp[:, lo:hi], 2.0 ** 23, None, ALU.mult)
                dve.drain()

            def take_r(n, j):
                q = BB * n + j
                dve.wait_ge(r_done, q + 1)
                dve.wait_ge(s_evac, q + 1)
                dve.scalar_tensor_tensor(out=y[:, :], in0=psR[:, :], scalar=rw[:, j:j + 1], in1=y[:, :],
                                         op0=ALU.mult, op1=ALU.add).then_inc(r_evac, 1)

            def y_stats(n, j):
                dve.drain()
                normalise(LY, BB * n + j, y, 1.0)

            def routing(n):
                dve.wait_ge(gate_done, n + 1)
                lgp = psM[:, 128:128 + BB * 2 * NE].rearrange("p (j s e) -> p j s e", j=BB, s=2)
                dve.tensor_copy(lg[:, :, :], lgp[:, :, 0, :])
                dve.drain()
                dve.tensor_tensor(lg[:, :, :], lg[:, :, :], lgp[:, :, 1, :], ALU.add)
                dve.drain().then_inc(rw_rdy, 1)
                for j in range(BB):
                    dve.max(top[:, j, :], lg[:, j, :])
                dve.drain()
                dve.tensor_tensor(rw[:, :], top[:, :, 0], top[:, :, 1], ALU.add)
                dve.drain()
                dve.tensor_scalar(rw[:, :], rw[:, :], c_r, None, ALU.mult)
                dve.drain()

            def chunk_lo(c):
                raw, pair, k = pair_chunk(c)
                dve.wait_ge(pair_hi, c + 1)
                dve.scalar_tensor_tensor(out=pair[:, LO, :], in0=raw, scalar=wsc[:, k:k + 1],
                                         in1=hi_tmp[:, c % 2, :], op0=ALU.mult, op1=ALU.subtract)\
                    .then_inc(pair_lo, 1)

            def tile_lo(it):
                dve.wait_ge(stg_hi, it + 1)
                dve.scalar_tensor_tensor(out=staging[:, it % NR, 1, :, :], in0=up_raw[:, :, P * it:P * it + P],
                                         scalar=wsc[:, WUP:WUP + 1], in1=staging[:, it % NR, 0, :, :],
                                         op0=ALU.mult, op1=ALU.subtract).then_inc(stg_rdy, 1)

            def norm_scale(k, c0, c1, turn):
                dve.tensor_reduce(amx[:, k:k + 1], fro[:, c0:c1], AX.X, ALU.add)
                dve.drain().then_inc(amax_rdy, 1)
                dve.wait_ge(amax_all, turn)
                pow2(k, k + 1, amr[:, k:k + 1], 2.0 ** -24, 63.5)

            def up_half(n, phase_a, first=False):
                m = n + 1
                for t in range(UT):
                    bank = up_bank[t % NR]
                    if first and t < NR:
                        for it in range(NR * t, NR * t + NR):
                            tile_lo(it)
                    if t < LT:
                        dve.wait_ge(l_hi, LT * n + t + 1)
                        dve.scalar_tensor_tensor(out=lat[:, t, 1, :], in0=bank, scalar=2.0 ** LAT_SHIFT,
                                                 in1=lat[:, t, 0, :], op0=ALU.mult, op1=ALU.subtract)\
                            .then_inc(up_evac, 1)
                    else:
                        i = IT * n + t - LT
                        dve.wait_ge(relu_rdy, i + 1)
                        dve.scalar_tensor_tensor(out=hbuf[:, t % 2, :], in0=bank, scalar=0.0,
                                                 in1=hbuf[:, t % 2, :], op0=ALU.max, op1=ALU.mult)
                        dve.drain().then_inc(up_evac, 1)
                        dve.drain().then_inc(sq_hid, 1)
                    if phase_a and t >= SIM_T and (t - SIM_T) % 4 == 0 and (t - SIM_T) // 4 < BB:
                        sum_products(m, (t - SIM_T) // 4, 1)
                    if phase_a and t >= SIM_T and (t - SIM_T) % 4 == 1 and (t - SIM_T) // 4 < BB:
                        sum_products(m, (t - SIM_T) // 4, 0)
                    if t >= LT:
                        dve.wait_ge(h_hi, i + 1)
                        dve.tensor_tensor(hT[:, t - LT, 1, :], hbuf[:, t % 2, :], hT[:, t - LT, 0, :],
                                          ALU.subtract).then_inc(h_rdy, 1)
                    if phase_a and t == SUMS_T + 1:
                        cosines(m)
                    if phase_a and t == LNX_T:
                        x_stats(m, 0)
                    if first and t == SCALE_T:
                        dve.wait_ge(dn_sq, IT)
                        norm_scale(WDN, LT, LT + IT, 4)
                        dve.tensor_scalar(coef[:, 4:5], wp[:, WUP:WUP + 1], wp[:, WUP:WUP + 1],
                                          wp[:, WDN:WDN + 1], ALU.mult, ALU.mult)
                        dve.drain()
                        dve.tensor_scalar(c_s, coef[:, 4:5], 2.0 ** -17, None, ALU.mult)
                        dve.drain().then_inc(scale_rdy, 1)
                    if first and t in PAIRS_AT:
                        for c in range(*PAIRS_AT[t]):
                            chunk_lo(c)
                routing(n)

            def down_half(n, phase_a):
                m = n + 1
                for j in range(BB):
                    if phase_a:
                        f_los(m, j)
                    if j > 0:
                        y_stats(n, j - 1)
                    if phase_a:
                        combine(m, j)
                        if j < BB - 1:
                            x_stats(m, j + 1)
                    take_r(n, j)
                    if phase_a:
                        xt_los(m, j)
                y_stats(n, BB - 1)

            x_stats_first()
            for j in range(BB):
                sum_products(0, j, 1)
                if j == 0:
                    dve.wait_ge(small_in, 32)
                    dve.tensor_reduce(amx[:, WX:WX + 1], wx_raw, AX.X, ALU.max, apply_absolute_value=True)
                    dve.tensor_reduce(amx[:, WG:WG + 1], gate_raw, AX.XY, ALU.max, apply_absolute_value=True)
                    dve.drain().then_inc(amax_rdy, 1)
                sum_products(0, j, 0)
                if j == 1:
                    dve.wait_ge(amax_all, 1)
                    pow2(WX, WG + 1, amr[:, WX:WG + 1], 2.0 ** -23, 0.0)
                    dve.drain().then_inc(scale_rdy, 1)
                    dve.wait_ge(tanh_rdy, 1)
                    dve.tensor_scalar(c_x, wp[:, WX:WX + 1], th[:, 0:1], 2.0 ** -(LOG_ACT + LOG_W), ALU.mult,
                                      ALU.mult)
                f_los(0, j)
            dve.wait_ge(wx_hi, 1)
            dve.scalar_tensor_tensor(out=wx[:, :, 1, :], in0=psM[:, 0:G * P].rearrange("p (g o) -> p g o", g=G),
                                     scalar=wsc[:, WX:WX + 1], in1=wx[:, :, 0, :], op0=ALU.mult,
                                     op1=ALU.subtract).then_inc(wx_rdy, 1)
            dve.wait_ge(gate_hi, 1)
            dve.scalar_tensor_tensor(out=gate[:, :, NE:2 * NE], in0=gate_raw, scalar=wsc[:, WG:WG + 1],
                                     in1=gate[:, :, 0:NE], op0=ALU.mult, op1=ALU.subtract)\
                .then_inc(gate_w_rdy, 1)
            cosines(0)
            dve.wait_ge(amax_all, 2)
            pow2(WF1, WF1 + 1, amr[:, WF1:WF1 + 1], 2.0 ** -24, 63.5)
            dve.drain().then_inc(scale_rdy, 1)
            for t in range(LT):
                dve.wait_ge(fc1_hi, t + 1)
                dve.scalar_tensor_tensor(out=fc1_staging[:, t % 2, 1], in0=fc1_raw[:, :, P * t:P * t + P],
                                         scalar=wsc[:, WF1:WF1 + 1], in1=fc1_staging[:, t % 2, 0],
                                         op0=ALU.mult, op1=ALU.subtract).then_inc(fc1_rdy, 1)
            for j in range(BB):
                combine(0, j)
                if j >= 1:
                    xt_los(0, j - 1, (1,))
                if j < BB - 1:
                    xt_los(0, j, (0,))
            dve.wait_ge(sq_used, KB)
            dve.tensor_reduce(amx[:, 6:7], psS[:, :], AX.X, ALU.max)
            dve.tensor_reduce(amx[:, 7:8], psR[:, :], AX.X, ALU.max)
            dve.drain().then_inc(norms_read, 1)
            dve.tensor_tensor(amr[:, WUP:WUP + 1], amx[:, 6:7], amx[:, 7:8], ALU.max)
            dve.drain()
            pow2(WUP, WUP + 1, amr[:, WUP:WUP + 1], 2.0 ** -24, 63.5)
            dve.drain().then_inc(scale_rdy, 1)
            xt_los(0, BB - 1)
            dve.wait_ge(w2_sq, LT)
            norm_scale(W2E, 0, LT, 3)
            dve.tensor_scalar(coef[:, 5:6], wp[:, WF1:WF1 + 1], wp[:, W2E:W2E + 1], wp[:, WG:WG + 1],
                              ALU.mult, ALU.mult)
            dve.drain()
            dve.tensor_scalar(c_r, coef[:, 5:6], 2.0 ** -(2 * LOG_ACT + 3 * LOG_W + LAT_SHIFT), None, ALU.mult)
            dve.drain().then_inc(scale_rdy, 1)
            up_half(0, True, first=True)
            down_half(0, True)
            with dve.Fori(1, NB - 1) as n:
                up_half(n, True)
                down_half(n, True)
            up_half(NB - 1, False)
            down_half(NB - 1, False)

        @block.tensor
        def _(pe):
            def quadrant_sums(m):
                pe.wait_ge(part_rdy, m + 1)
                n = BB * CH
                pe.matmul(psM[:, 0:32], part[:, 0, 0:n], fold[:, :], start=True, stop=True)
                pe.matmul(psM[:, 32:33], part[:, 0, 1:n + 1], fold[:, 0:1], start=True, stop=True)
                pe.matmul(psM[:, 33:65], part[:, 1, 0:n], fold[:, :], start=True, stop=True)\
                    .then_inc(sums_done, 1)

            def xattn(m, j, h):
                first = isinstance(m, int) and m == 0
                q = BB * m + j
                b = j % 2 if first else 0
                if h == 1:
                    pe.wait_ge(comb, 2 * q + 1)
                elif first:
                    pe.wait_ge(u_in[b], UIN * (j // 2 + 1))
                    if j > 0:
                        pe.wait_ge(comb, 2 * j)
                else:
                    pe.wait_ge(u_in[0], UIN * (q - 1))
                    pe.wait_ge(xt_rdy, 2 * q)
                t0 = HALF * h
                for g in range(G):
                    for n, (w, v) in enumerate(((0, 0), (0, 1), (1, 0))):
                        mm = pe.matmul(psP[:, g, :], wx[:, g, w, :], U[b][:, g, v, t0:t0 + HALF],
                                       start=(n == 0), stop=(n == 2))
                mm.then_inc(p_done, 1)

            def turn(m, j):
                pe.wait_ge(xn_rdy, BB * m + j + 1)
                for h in range(2):
                    for k in range(4):
                        mm = pe.transpose(psP[:, h, P * k:P * k + P],
                                          scr[0][:, P * (4 * h + k):P * (4 * h + k) + P], ident[:, :])
                    mm.then_inc(tr_done, 1)

            def turn_first(j, h):
                pe.wait_ge(xn_rdy, j + 1)
                if j == 0 and h == 0:
                    pe.wait_ge(s0_rdy, 1)
                else:
                    pe.wait_ge(xt_rdy, 2 * j + h)
                for k in range(4):
                    mm = pe.transpose(psM[:, P * k:P * k + P],
                                      scr[j % 2][:, P * (4 * h + k):P * (4 * h + k) + P], ident[:, :])
                mm.then_inc(tr_done, 1)

            def up_half(n, phase_a):
                m = n + 1
                pe.wait_ge(xt_rdy, 2 * BB * m)
                for t in range(UT):
                    pe.wait_ge(ring_in[t % NR], 16 * (n * (UT // NR) + t // NR + 1))
                    if t >= NR:
                        pe.wait_ge(up_evac, UT * n + t - NR + 1)
                    elif not (isinstance(n, int) and n == 0):
                        pe.wait_ge(s_evac if t < 2 else r_evac, BB * n)
                    for k in range(KB):
                        for a, b in ((0, 0), (0, 1), (1, 0)):
                            mm = pe.matmul(up_bank[t % NR], ring[:, t % NR, a, k, :], xT[:, k, b, :],
                                           start=(k == 0 and a == 0 and b == 0),
                                           stop=(k == KB - 1 and a == 1))
                    mm.then_inc(up_done, 1)
                    if phase_a and t == SUMS_T:
                        if not (isinstance(n, int) and n == 0):
                            pe.wait_ge(rw_rdy, n)
                        quadrant_sums(m)
                if phase_a:
                    pe.wait_ge(simo_rdy, m + 1)
                for j in range(BB):
                    c0 = 128 + 2 * NE * j
                    for k in range(KB):
                        pe.matmul(psM[:, c0:c0 + 2 * NE], xT[:, k, 0, P * j:P * j + P], gate[:, k, :],
                                  start=(k == 0), stop=False, skip_group_check=True)
                        mm = pe.matmul(psM[:, c0:c0 + NE], xT[:, k, 1, P * j:P * j + P], gate[:, k, 0:NE],
                                       start=False, stop=(k == KB - 1), skip_group_check=True)
                mm.then_inc(gate_done, 1)

            def shared(j, i0, i1):
                for i in range(i0, i1):
                    for a, b in ((0, HI), (0, LO), (1, HI)):
                        for h in range(2):
                            mm = pe.matmul(psS[:, HALF * h:HALF * h + HALF], hT[:, i, a, P * j:P * j + P],
                                           dn[:, i, b, HALF * h:HALF * h + HALF],
                                           start=(i == 0 and a == 0 and b == HI),
                                           stop=(i == IT - 1 and a == 1))
                return mm

            def routed(j):
                for l in range(LT):
                    for a, b in ((0, HI), (0, LO), (1, HI)):
                        for h in range(2):
                            mm = pe.matmul(psR[:, HALF * h:HALF * h + HALF], lat[:, l, a, P * j:P * j + P],
                                           w2[:, l, b, HALF * h:HALF * h + HALF],
                                           start=(l == 0 and a == 0 and b == HI),
                                           stop=(l == LT - 1 and a == 1))
                return mm

            def down_half(n, phase_a, first=False):
                m = n + 1
                for j in range(BB):
                    q = BB * n + j
                    if j == 0:
                        pe.wait_ge(up_evac, UT * (n + 1))
                        pe.wait_ge(h_rdy, IT * (n + 1))
                        if first:
                            pe.wait_ge(pair_rdy, LT + IT)
                    else:
                        pe.wait_ge(s_evac, q)
                    shared(j, 0, S_CUTS[0])
                    if phase_a:
                        xattn(m, j, 0)
                    shared(j, *S_CUTS)
                    if phase_a:
                        xattn(m, j, 1)
                    shared(j, S_CUTS[1], IT).then_inc(s_done, 1)
                    if j > 0:
                        pe.wait_ge(r_evac, q)
                    routed(j).then_inc(r_done, 1)
                    if phase_a:
                        turn(m, j)

            pe.wait_ge(const_rdy, 1)
            pe.wait_ge(small_in, 32)
            for g in range(G):
                mm = pe.transpose(psM[:, P * g:P * g + P], wx_raw[:, P * g:P * g + P], ident[:, :])
            mm.then_inc(wxT_done, 1)
            pe.wait_ge(e_in, 16)
            for k in range(LT):
                for l in range(LT):
                    mm = pe.transpose(up_bank[k][:, P * l:P * l + P], e_raw[:, l, P * k:P * k + P], ident[:, :])
                mm.then_inc(eT_done, 1)

            def expert_fc2(l):
                pe.wait_ge(eT_rdy, LT)
                pe.wait_ge(f2_in, 16)
                if l >= 2:
                    pe.wait_ge(w2_out, l - 1)
                acc = psS if l % 2 == 0 else psR
                for k in range(LT):
                    for h in range(2):
                        mm = pe.matmul(acc[:, HALF * h:HALF * h + HALF], ET[:, k, P * l:P * l + P],
                                       fc2_raw[:, k, HALF * h:HALF * h + HALF],
                                       start=(k == 0), stop=(k == LT - 1))
                mm.then_inc(w2_done, 1)

            def column_norms(k):
                n = UP_ORDER.index(k)
                pe.wait_ge(sq_rdy, n + 1)
                if n == 0:
                    pe.wait_ge(w2_out, LT)
                for b in range(4):
                    mm = pe.matmul(up_bank[b], ones_b[:, :], squares[n % 2][:, 512 * b:512 * b + 512],
                                   start=(n == 0), stop=(n == KB - 1), skip_group_check=True)
                mm.then_inc(sq_used, 1)

            expert_fc2(0)
            expert_fc2(1)
            pe.wait_ge(wx_rdy, 1)
            quadrant_sums(0)
            xattn(0, 0, 0)
            expert_fc2(2)
            xattn(0, 0, 1)
            expert_fc2(3)
            for j in range(BB):
                for k in UP_SQ[j]:
                    column_norms(k)
                if j < BB - 1:
                    xattn(0, j + 1, 0)
                turn_first(j, 0)
                if j < BB - 1:
                    xattn(0, j + 1, 1)
                turn_first(j, 1)
            pe.wait_ge(gate_w_rdy, 1)
            pe.wait_ge(norms_read, 1)
            up_half(0, True)
            down_half(0, True, first=True)
            with pe.Fori(1, NB - 1) as n:
                up_half(n, True)
                down_half(n, True)
            up_half(NB - 1, False)
            down_half(NB - 1, False)


_INS = ["x", "ctx_4096", "g_xattn", "g_ffn", "L0_xattn_weight", "L0_ffn_gate_w", "L0_ffn_up_w",
        "L0_ffn_down_w", "L0_ffn_fc1_w", "L0_ffn_fc2_w", "L0_ffn_expert_w", "L0_ffn_ln_gamma",
        "L0_ffn_ln_beta"]


def kernel(**inputs):
    import numpy as np
    import concourse.bacc as bacc
    from concourse.bass_utils import run_bass_kernel_spmd as run

    nc = bacc.Bacc("TRN2", target_bir_lowering=False, num_devices=1)
    arrays, args = {}, []
    for name in _INS:
        a = np.ascontiguousarray(inputs[name])
        arrays[f"in_{name}"] = a
        args.append(nc.dram_tensor(f"in_{name}", a.shape, mybir.dt.from_np(a.dtype), kind="ExternalInput").ap())
    out = nc.dram_tensor("out_rows", tuple(inputs["x"].shape), F32, kind="ExternalOutput").ap()
    flamingo_block(nc, *args, out)
    r = run(nc, [arrays], core_ids=[0])
    return r.results[0]["out_rows"]
```

```python
from contextlib import ExitStack

import concourse.bass as bass
from concourse import mybir

ALU = mybir.AluOpType
ACT = mybir.ActivationFunctionType
AX = mybir.AxisListType
F32 = mybir.dt.float32
F16 = mybir.dt.float16
BF16 = mybir.dt.bfloat16
I32 = mybir.dt.int32
RMAX = bass.bass_isa.ReduceOp.max
RADD = bass.bass_isa.ReduceOp.add

P = 128
LN_EPS = 1e-5
COS_EPS = 1e-8
LOG_ACT = 10
LOG_W = 14
LAT_SHIFT = -15
HID_SHIFT = -45
WX, WG, WF1, WUP, W2E, WDN = range(6)
LO, HI = 0, 1


def flamingo_block(nc, x, ctx, g_xattn, g_ffn, w_xattn, w_gate, w_up, w_down, w_fc1, w_fc2,
                   w_expert, ln_gamma, ln_beta, out):
    B, C, T = x.shape
    INT = w_up.shape[1]
    LAT = w_fc1.shape[1]
    NE = w_gate.shape[1]
    KB = T // P
    IT = INT // P
    LT = LAT // P
    BB = 4
    NB = B // BB
    TOK = BB * C
    UT = LT + IT
    HALF = T // 2
    G = 3
    NR = 4
    CH = T // 32
    UIN = 16 * G * G

    with ExitStack() as es:
        def sb(name, shape, dt):
            return es.enter_context(nc.sbuf_tensor(name, shape, dt))

        def ps(name, shape):
            return es.enter_context(nc.psum_tensor(name, shape, F32))

        def sem(name):
            return es.enter_context(nc.semaphore(name))

        pair_dram = nc.dram_tensor("pair_scratch", (UT, P, 2 * KB * P), F16, kind="Internal").ap()
        side_dram = nc.dram_tensor("side_scratch", (B * T + 2,), F32, kind="Internal").ap()
        self_dram = nc.dram_tensor("self_scratch", (B * T,), F32, kind="Internal").ap()

        big = sb("big", [P, IT * T], F32)
        up_raw = big[:, :].rearrange("p (k i) -> p k i", k=KB)
        dn = big[:, :].bitcast(F16).rearrange("p (c s h) -> p c s h", c=IT, s=2)
        fc2_raw = big[:, 0:LT * T].rearrange("p (m h) -> p m h", m=LT)
        fc1_raw = big[:, (KB - 2) * INT:].rearrange("p (k l) -> p k l", k=KB)
        w2_raw = sb("w2", [P, LT, T], F32)
        w2 = w2_raw[:, :, :].bitcast(F16).rearrange("p l (s h) -> p l s h", s=2)
        gate = sb("gate", [P, KB, 2 * NE], F16)
        wx = sb("wx", [P, G, 2, P], F16)
        xT_f = sb("xT", [P, KB * TOK], F32)
        xT = xT_f[:, :].bitcast(F16).rearrange("p (k s t) -> p k s t", k=KB, s=2)
        fc1_staging = xT_f[:, :].bitcast(F16).rearrange("p (b s k i) -> p b s k i", b=LT, s=2, k=KB)
        ctx_first = xT_f[:, :].rearrange("p (j t) -> p j t", j=BB)
        hid = sb("hid", [P, IT * TOK], F32)
        hT = hid[:, :].bitcast(F16).rearrange("p (i s t) -> p i s t", i=IT, s=2)
        x_tail = hid[:, 0:2 * T].rearrange("p (b t) -> p b t", b=2)
        half_hid = IT * TOK // 2
        staging = hid[:, half_hid:].bitcast(F16).rearrange("p (b s k i) -> p b s k i", b=NR, s=2, k=KB)
        lgb = sb("lgb", [P, LT * TOK + 2 * T], F32)
        lat = lgb[:, 0:LT * TOK].bitcast(F16).rearrange("p (l s t) -> p l s t", l=LT, s=2)
        e_raw = lgb[:, 0:LT * TOK].rearrange("p (l m) -> p l m", l=LT)
        gam = lgb[:, LT * TOK:LT * TOK + T]
        bet = lgb[:, LT * TOK + T:]
        ring_f = sb("ring", [P, NR, T], F32)
        ring = ring_f[:, :, :].bitcast(F16).rearrange("p r (s k i) -> p r s k i", s=2, k=KB)
        wx_raw = ring_f[:, 3, 0:G * P]
        gate_raw = ring_f[:, 3, G * P:G * P + KB * NE].rearrange("p (k e) -> p k e", k=KB)
        home = sb("home", [P, BB, T], F32)
        fc1_junk = home[:, 0:2, :].bitcast(BF16).rearrange("p b (k l) -> p (b k) l", l=LAT)
        ET = home[:, 2:4, :].rearrange("p a (b l) -> p (a b) l", b=2)
        work = sb("work", [P, 2, T], F32)
        hi_tmp = work[:, 1, :].bitcast(F16).rearrange("p (b h) -> p b h", b=2)
        y = sb("y", [P, T], F32)
        scr_a = sb("scr", [P, T], F32)
        sides_a = sb("sides", [P, T + 2], F32)
        side_a = sb("sim_side", [P, T + 2], F32)
        squares = [y[:, :].bitcast(BF16), sides_a[:, 0:T].bitcast(BF16)]
        hbuf = side_a[:, 0:1024].rearrange("p (b t) -> p b t", b=2)

        def as_pairs(buf):
            return buf.bitcast(F16).rearrange("p (s t) -> p s t", s=2)

        spare = [hid[:, 2 * T + (T + 2) * k:2 * T + (T + 2) * (k + 1)] for k in range(5)]
        scr = [scr_a[:, :], spare[3][:, 0:T]]
        fp = [as_pairs(b) for b in (sides_a[:, :], spare[2], spare[0], spare[1])]
        fp_flat = [b.bitcast(F16) for b in (sides_a[:, :], spare[2], spare[0], spare[1])]
        U = [ring_f[:, 0:G, :].bitcast(F16).rearrange("p g (s t) -> p g s t", s=2),
             lgb[:, 0:G * T].bitcast(F16).rearrange("p (g s t) -> p g s t", g=G, s=2)]
        sim_side = [side_a[:, :], spare[4]]
        sim_self = [ring_f[:, 3, :], bet]
        x_buf = [work[:, 0, :], work[:, 1, :], x_tail[:, 0, :], x_tail[:, 1, :]]
        prod_first = [w2_raw[:, 2, :], w2_raw[:, 3, :]]
        ident = sb("ident", [P, P], F32)
        fold = sb("fold", [P, 32], F32)
        ones_b = sb("ones_b", [P, P], BF16)
        pick = sb("pick", [P, 2 * BB * KB - 1], F32)
        NR0 = BB * KB
        first_row = hid[0:NR0, 2 * T + 5 * (T + 2):2 * T + 5 * (T + 2) + 5 * (P + 2)]\
            .rearrange("p (s t) -> p s t", s=5)
        sums_0, nrm_0, nt_0 = first_row[:, 0:2, :], first_row[:, 2, :], first_row[:, 3:5, :]
        part = sb("part", [P, 2, BB * CH + 1], F32)
        sums = sb("sums", [P, 72], F32)
        nrm = sb("nrm", [P, 36], F32)
        nt = sb("nt", [P, 2, 36], F32)
        simo = sb("simo", [P, 2, 32], F32)
        g_col = sb("g_col", [P, 2], F32)
        th = sb("th", [P, 2], F32)
        amx = sb("amx", [P, 8], F32)
        fro = sb("fro", [P, LT + IT], F32)
        amr = sb("amr", [P, 8], F32)
        wexp = sb("wexp", [P, 8], I32)
        wsc = sb("wsc", [P, 8], F32)
        wp = sb("wp", [P, 8], F32)
        coef = sb("coef", [P, 8], F32)
        c_x, c_s, c_r = (coef[:, k:k + 1] for k in range(3))
        st = sb("st", [P, 3, 2, 6], F32)
        mv = sb("mv", [P, 3, 2], F32)
        sd = sb("sd", [P, 3, 4], F32)
        rs = sb("rs", [P, 3, 2], F32)
        LX, L1, LY = range(3)
        st_x = sb("st_x", [P, BB, 2, 6], F32)
        mv_x = sb("mv_x", [P, BB, 2], F32)
        sd_x = sb("sd_x", [P, 4, BB], F32)
        rs_x = sb("rs_x", [P, 2, BB], F32)
        lg = sb("lg", [P, BB, NE], F32)
        top = sb("top", [P, BB, 8], F32)
        rw = sb("rw", [P, BB], F32)
        zeros = sb("zeros", [P, 2], F32)

        psS = ps("psS", [P, T])
        psR = ps("psR", [P, T])
        psP = ps("psP", [P, G, HALF])
        psM = ps("psM", [P, 512])
        up_bank = [psS[:, 0:512], psS[:, 512:1024], psR[:, 0:512], psR[:, 512:1024]]

        def first_turn_bank(j, h):
            return psP[:, 0, :] if j == BB - 1 and h == 1 else psM[:, :]

        const_rdy = sem("const_rdy")
        small_in = sem("small_in")
        g_in = sem("g_in")
        e_in, f2_in, f1_in, gb_in = sem("e_in"), sem("f2_in"), sem("f1_in"), sem("gb_in")
        upraw_in = [sem(f"upraw_in{k}") for k in range(KB)]
        dnraw_in = [sem(f"dnraw_in{k}") for k in range(IT)]
        x_in = [sem(f"x_in{k}") for k in range(2)]
        x_tail_in = [sem(f"x_tail_in{k}") for k in range(2)]
        ctx_in = sem("ctx_in")
        ctx_first_in = [sem(f"ctx_first_in{k}") for k in range(BB)]
        u_in = [sem(f"u_in{k}") for k in range(2)]
        sim_in = [sem(f"sim_in{k}") for k in range(2)]
        fc1_out = [sem(f"fc1_out{k}") for k in range(LT)]
        ring_in = [sem(f"ring_in{k}") for k in range(NR)]
        stg_out = [sem(f"stg_out{k}") for k in range(NR)]
        simrow_out, edge_out = sem("simrow_out"), sem("edge_out")
        out_done = sem("out_done")
        tanh_rdy = sem("tanh_rdy")
        amax_rdy, amax_all = sem("amax_rdy"), sem("amax_all")
        scale_rdy = sem("scale_rdy")
        wxT_done, wx_hi, wx_rdy = sem("wxT_done"), sem("wx_hi"), sem("wx_rdy")
        gate_hi, gate_w_rdy = sem("gate_hi"), sem("gate_w_rdy")
        eT_done, eT_rdy = sem("eT_done"), sem("eT_rdy")
        w2_done, w2_out, w2_rdy = sem("w2_done"), sem("w2_out"), sem("w2_rdy")
        fc1_hi, fc1_rdy, w2_sq, dn_sq = sem("fc1_hi"), sem("fc1_rdy"), sem("w2_sq"), sem("dn_sq")
        sq_rdy, sq_used, norms_read = sem("sq_rdy"), sem("sq_used"), sem("norms_read")
        stg_hi, stg_rdy = sem("stg_hi"), sem("stg_rdy")
        w2_hi, w2_lo = sem("w2_hi"), sem("w2_lo")
        dn_hi = sem("dn_hi")
        dn_rdy = [sem(f"dn_rdy{k}") for k in range(2)]
        prod1, prod0 = sem("prod1"), sem("prod0")
        prod_used = sem("prod_used")
        part_rdy = sem("part_rdy")
        pads_rdy = sem("pads_rdy")
        sums_done, s0_rdy, nrm_rdy, simo_rdy = sem("sums_done"), sem("s0_rdy"), sem("nrm_rdy"), sem("simo_rdy")
        first_col_rdy, next_col_done = sem("first_col_rdy"), sem("next_col_done")
        var_rdy = [sem(f"var_rdy{k}") for k in range(3)]
        std_rdy = [sem(f"std_rdy{k}") for k in range(3)]
        rs_rdy = [sem(f"rs_rdy{k}") for k in range(3)]
        f_hi, f_rdy = sem("f_hi"), sem("f_rdy")
        p_done, comb, left_sum = sem("p_done"), sem("comb"), sem("left_sum")
        xn_rdy, tr_done, xt_hi, xt_rdy = sem("xn_rdy"), sem("tr_done"), sem("xt_hi"), sem("xt_rdy")
        home_rdy = sem("home_rdy")
        up_done, up_evac = sem("up_done"), sem("up_evac")
        relu_rdy, sq_hid, h_hi, h_rdy = sem("relu_rdy"), sem("sq_hid"), sem("h_hi"), sem("h_rdy")
        l_hi = sem("l_hi")
        gate_done, rw_rdy = sem("gate_done"), sem("rw_rdy")
        s_done, r_done, s_evac, r_evac = sem("s_done"), sem("r_done"), sem("s_evac"), sem("r_evac")
        y_nrm, y_fin = sem("y_nrm"), sem("y_fin")
        r_half, nrm_half, fin_half = sem("r_half"), sem("nrm_half"), sem("fin_half")

        SIM_T = 2
        UP_ORDER = [2, 3, 4, 5, 6, 7, 0, 1]
        UP_SQ = ((), (), (4, 5), (0, 1))
        UP_SQ_MID = ((), (2, 3), (6, 7), ())
        W2_WITH = ((2,), (3,), (), ())
        W2_SQ = ((0, 1, 2), (3,), (), ())
        SUMS_T = 16
        LNX_T = 18
        W2_SPLIT = {4: (0, 2), 5: (2, 4)}
        DN_LOAD = {4: (0, 2), 5: (2, 5), 6: (5, 8), 7: (8, 11), 8: (11, 14), 9: (14, 16)}
        DN_SQUARE = {t + 2: c for t, c in DN_LOAD.items()}
        SCALE_T = 12
        DN_SPLIT = {12: (0, 2), 13: (2, 4), 14: (4, 6), 15: (6, 8), 16: (8, 9), 17: (9, 10), 18: (10, 11),
                    19: (11, 12)}
        DN_LATE = range(12, IT)
        SIM_STEP = 3
        S_CUTS = (9, 12)
        S_CUTS_0, S_CUTS_00 = (10, 13), (12, 14)

        def sim_tile(first, j):
            return NR + SIM_STEP * j if first else SIM_T + 4 * j

        def dn_raw(c):
            if c < IT - 2:
                return big[:, (c + 2) * T:(c + 3) * T]
            return lgb[:, LT * TOK + (c - IT + 2) * T:LT * TOK + (c - IT + 3) * T]

        block = es.enter_context(nc.Block())

        @block.sync
        def _(sp):
            def ahead(value):
                return value if isinstance(value, int) else sp.snap(sp.to_reg(value))

            def load_x(m, j, slot):
                sp.dma_start(work[:, slot, :], x[bass.ds(BB * m + j, 1)].rearrange("o p t -> p (o t)"))\
                    .then_inc(x_in[slot], 16)

            def load_ctx(m, j):
                q = BB * m + j
                if j > 0:
                    sp.wait_ge(prod_used, 2 * q)
                sp.dma_start(scr[0], ctx[bass.ds(q, 1)].rearrange("o p t -> p (o t)"))\
                    .then_inc(ctx_in, 16)

            def store_sims(m):
                sp.wait_ge(simo_rdy, m + 1)
                first = BB * T * m
                sp.dma_start(side_dram[bass.ds(first + 2, BB * T)].rearrange("(c t) -> c t", t=32), simo[:, 0, :])\
                    .then_inc(simrow_out, 16)
                sp.dma_start(self_dram[bass.ds(first, BB * T)].rearrange("(c t) -> c t", t=32), simo[:, 1, :])\
                    .then_inc(simrow_out, 16)

            def store_first_sims():
                sp.wait_ge(simo_rdy, 1)
                sp.dma_start(side_dram[2:2 + BB * T].rearrange("(c t) -> c t", t=P), sums_0[:, 1, 0:P])\
                    .then_inc(simrow_out, 16)
                sp.dma_start(self_dram[0:BB * T].rearrange("(c t) -> c t", t=P), sums_0[:, 0, 0:P])\
                    .then_inc(simrow_out, 16)

            def unfold_into(j):
                for g in range(G):
                    for k in range(G):
                        p0 = (k - P * g) % G
                        c0 = (P * g + p0) // G
                        num = (P - p0 + G - 1) // G
                        sp.dma_start(U[j % 2][p0:p0 + G * (num - 1) + 1:G, g, :, :],
                                     fp[j][c0:c0 + num, :, k:k + T]).then_inc(u_in[j % 2], 16)

            def sims_into(q, b):
                side = side_dram[bass.ds(q * T + 1, T + 1)].rearrange("(a t) -> a t", a=1)
                same = self_dram[bass.ds(q * T, T)].rearrange("(a t) -> a t", a=1)
                sp.dma_start(sim_side[b][:, 0:T + 1], side.broadcast_to([P, T + 1])).then_inc(sim_in[b], 16)
                sp.dma_start(sim_self[b], same.broadcast_to([P, T])).then_inc(sim_in[b], 16)

            def phase_a_loads(m, j):
                q = BB * m + j
                f_count, pad_count = ahead(q + 1), ahead(m + 1)
                used = ahead(2 * q if j > 0 else UT * m)
                rows, combined, hidden = ahead(32 * (m + 1)), ahead(q), ahead(IT * m)
                sp.wait_ge(f_rdy, f_count)
                sp.wait_ge(pads_rdy, pad_count)
                if j > 0:
                    sp.wait_ge(p_done, used)
                else:
                    sp.wait_ge(up_done, used)
                unfold_into(0)
                sp.wait_ge(simrow_out, rows)
                if j > 0:
                    sp.wait_ge(var_rdy[L1], combined)
                else:
                    sp.wait_ge(h_rdy, hidden)
                sims_into(q, 0)
                if 1 <= j < BB - 1:
                    sp.wait_ge(home_rdy, BB * m + j)
                    load_x(m, j + 1, (j + 1) % 2)

            def first_unfold(j):
                sp.wait_ge(f_rdy, j + 1)
                sp.wait_ge(pads_rdy, 1)
                if j >= 2:
                    sp.wait_ge(p_done, 2 * (j - 1))
                if j == 1:
                    sp.wait_ge(eT_done, LT)
                unfold_into(j)

            def first_sims(j):
                b = j % 2
                sp.wait_ge(simrow_out, 32)
                sp.wait_ge(edge_out, 16)
                if j >= 2:
                    sp.wait_ge(left_sum, 2 * (j - 1))
                if j == 0:
                    sp.wait_ge(wxT_done, 1)
                    sp.wait_ge(gate_w_rdy, 1)
                sims_into(j, b)

            def up_half(n, phase_a, first=False):
                m = n + 1
                for t in range(UT):
                    if t == 0:
                        sp.wait_ge(p_done, 2 * BB * m)
                    if t == G:
                        sp.wait_ge(rs_rdy[L1], BB * m)
                    if t >= NR:
                        sp.wait_ge(up_done, UT * n + t - NR + 1)
                    if first and t < LT:
                        sp.wait_ge(fc1_out[t], 16)
                    elif first:
                        sp.wait_ge(stg_out[t % NR], 16 * ((t - LT) // NR + 1))
                    sp.dma_start(ring_f[:, t % NR, :].bitcast(F16), pair_dram[t])\
                        .then_inc(ring_in[t % NR], 16)
                    if phase_a:
                        if t == NR - 1:
                            sp.wait_ge(tr_done, 2 * BB * m)
                            load_ctx(m, 0)
                            sp.wait_ge(home_rdy, BB * m - 1)
                            load_x(m, 0, 0)
                            if not first:
                                sp.wait_ge(home_rdy, BB * m)
                                load_x(m, 1, 1)
                        for j in range(1, BB):
                            if t == sim_tile(first, j) + (2 if first else 3):
                                load_ctx(m, j)
                if phase_a:
                    store_sims(m)
                    if first:
                        sp.wait_ge(dn_sq, IT)
                        load_x(m, 1, 1)

            sp.dma_start(g_col[:, 0:1], g_xattn.rearrange("(a b) -> a b", a=1).broadcast_to([P, 1]))\
                .then_inc(g_in, 16)
            sp.dma_start(g_col[:, 1:2], g_ffn.rearrange("(a b) -> a b", a=1).broadcast_to([P, 1]))\
                .then_inc(g_in, 16)
            sp.dma_start(ctx_first[:, 0, :], ctx[0]).then_inc(ctx_first_in[0], 16)
            load_x(0, 0, 0)
            load_x(0, 1, 1)
            for j in range(2):
                sp.dma_start(x_tail[:, j, :], x[2 + j]).then_inc(x_tail_in[j], 16)
            for j in range(1, BB):
                sp.dma_start(ctx_first[:, j, :], ctx[j]).then_inc(ctx_first_in[j], 16)
            sp.dma_start(wx_raw, w_xattn.rearrange("o c k -> o (c k)")).then_inc(small_in, 16)
            sp.dma_start(gate_raw, w_gate.rearrange("(k p) e -> p k e", p=P)).then_inc(small_in, 16)
            sp.dma_start(e_raw, w_expert.rearrange("(l p) m -> p l m", p=P)).then_inc(e_in, 16)
            sp.dma_start(fc2_raw, w_fc2.rearrange("(m p) h -> p m h", p=P)).then_inc(f2_in, 16)
            sp.wait_ge(const_rdy, 1)
            sp.dma_start(side_dram[0:2].rearrange("(a t) -> a t", a=1), zeros[0:1, :]).then_inc(edge_out, 16)
            first_unfold(0)
            sp.dma_start(fc1_raw, w_fc1.rearrange("(k p) l -> p k l", p=P)).then_inc(f1_in, 16)
            store_first_sims()
            first_sims(0)
            first_unfold(1)
            first_sims(1)
            for j in range(2, BB):
                first_unfold(j)
                first_sims(j)
                for k in (UP_ORDER[0:3], UP_ORDER[3:8])[j - 2]:
                    if k == KB - 2:
                        sp.wait_ge(fc1_rdy, LT)
                    if k == 0:
                        sp.wait_ge(w2_done, LT)
                    sp.dma_start(up_raw[:, k, :], w_up[k * P:(k + 1) * P, :]).then_inc(upraw_in[k], 16)
            up_half(0, True, first=True)
            for j in range(BB):
                phase_a_loads(1, j)
                if j == 0:
                    for k in range(2):
                        sp.wait_ge(dn_rdy[k], IT // 2)
                    sp.dma_start(gam, ln_gamma.rearrange("(a h) -> a h", a=1).broadcast_to([P, T]))\
                        .then_inc(gb_in, 16)
                    sp.dma_start(bet, ln_beta.rearrange("(a h) -> a h", a=1).broadcast_to([P, T]))\
                        .then_inc(gb_in, 16)
            with sp.Fori(1, NB - 1) as n:
                up_half(n, True)
                for j in range(BB):
                    phase_a_loads(n + 1, j)
            up_half(NB - 1, False)
            sp.wait_ge(out_done, 16 * (B + 1))

        @block.gpsimd
        def _(pool):
            def products(m, j):
                q = BB * m + j
                pool.wait_ge(ctx_in, 16 * (q - BB + 1))
                if j > 0:
                    pool.wait_ge(prod_used, 2 * q - 1)
                else:
                    pool.wait_ge(u_in[0], UIN * (q - 2))
                pool.tensor_tensor(sides_a[:, 0:T - 1], scr[0][:, 0:T - 1], scr[0][:, 1:T], ALU.mult)
                pool.memset(sides_a[:, T - 1:T], 0.0)
                pool.drain().then_inc(prod1, 1)
                pool.tensor_tensor(scr[0], scr[0], scr[0], ALU.mult).then_inc(prod0, 1)

            def pad(b):
                for c0, c1 in ((0, 1), (T + 1, T + 3), (2 * T + 3, 2 * T + 4)):
                    pool.tensor_tensor(fp_flat[b][:, c0:c1], zeros[:, 0:c1 - c0], zeros[:, 0:c1 - c0], ALU.add)

            def pads(m):
                pool.wait_ge(part_rdy, m + 1)
                pad(0)
                pool.drain().then_inc(pads_rdy, 1)

            def finish(n, j):
                pool.wait_ge(y_nrm, BB * n + j + 1)
                pool.tensor_tensor(y[:, :], y[:, :], gam, ALU.mult)
                pool.drain()
                pool.tensor_tensor(y[:, :], y[:, :], home[:, j, :], ALU.add)
                pool.drain().then_inc(y_fin, 1)

            def keep(m, j):
                pool.wait_ge(rs_rdy[L1], BB * m + j + 1)
                pool.wait_ge(xn_rdy, BB * m + j + 1)
                pool.tensor_tensor(home[:, j, :], work[:, j % 2, :], bet, ALU.add).then_inc(home_rdy, 1)

            def dn_lo(c):
                pool.wait_ge(dn_hi, c + 1)
                pool.tensor_scalar(dn_raw(c), dn_raw(c), wsc[:, WDN:WDN + 1], 1.0, ALU.mult, ALU.mult)
                pool.drain()
                pool.tensor_tensor(dn[:, c, LO, :], dn_raw(c), dn[:, c, HI, :], ALU.subtract)\
                    .then_inc(dn_rdy[1], 1)

            def move_w2():
                for l in range(LT):
                    pool.wait_ge(w2_lo, l + 1)
                    pool.tensor_scalar(w2[:, l, HI, :], hi_tmp[:, l % 2, :], 1.0, 1.0, ALU.mult,
                                       ALU.mult).then_inc(w2_rdy, 1)

            pool.memset(zeros[:, :], 0.0)
            pool.memset(ident[:, :], 0.0)
            pool.memset(ones_b[:, :], 1.0)
            pool.memset(fold[:, :], 0.0)
            pool.memset(part[:, :, BB * CH:], 1.0)
            pool.memset(pick[:, :], 0.0)
            for b in range(2):
                pool.memset(prod_first[b][:, T - 1:T], 0.0)
            pool.drain()
            pool.memset(pick[:, NR0 - 1:NR0], 1.0)
            pool.affine_select(out=ident[:, :], in_=ident[:, :], compare_op=ALU.not_equal, fill=1.0,
                               base=0, pattern=[[-1, P]], channel_multiplier=1)
            for k in range(4):
                pool.affine_select(out=fold[:, :], in_=fold[:, :], compare_op=ALU.not_equal, fill=1.0,
                                   base=-32 * k, pattern=[[-1, 32]], channel_multiplier=1)
                pool.drain()
            for b in range(BB):
                pad(b)
            pool.drain().then_inc(pads_rdy, 1)
            pool.drain().then_inc(const_rdy, 1)
            for j in range(BB):
                pool.wait_ge(ctx_first_in[j], 16)
                if j >= 2:
                    pool.wait_ge(prod_used, 2 * (j - 2) + 1)
                c = ctx_first[:, j, :]
                pool.tensor_tensor(prod_first[j % 2][:, 0:T - 1], c[:, 0:T - 1], c[:, 1:T], ALU.mult)\
                    .then_inc(prod1, 1)
            for j in range(BB):
                pool.wait_ge(f_hi, j + 1)
                pool.tensor_tensor(fp[j][:, 1, 1:T + 1], scr[j % 2], fp[j][:, 0, 1:T + 1], ALU.subtract)\
                    .then_inc(f_rdy, 1)
                if j == 0:
                    pool.wait_ge(amax_rdy, 1)
                    pool.partition_all_reduce(amr[:, WX:WG + 1], amx[:, WX:WG + 1], P, RMAX)\
                        .then_inc(amax_all, 1)
            pool.wait_ge(amax_rdy, 2)
            pool.partition_all_reduce(amr[:, WF1:WF1 + 1], amx[:, WF1:WF1 + 1], P, RADD).then_inc(amax_all, 1)

            def keep_first(j):
                if j == 2:
                    pool.wait_ge(w2_done, LT)
                pool.wait_ge(xn_rdy, j + 1)
                pool.tensor_scalar(home[:, j, :], x_buf[j], 1.0, 1.0, ALU.mult, ALU.mult)\
                    .then_inc(home_rdy, 1)

            for j in range(BB):
                for h in range(2):
                    pool.wait_ge(comb, 2 * j + h + 1)
                    left, same = scr[j % 2][:, 0:HALF], sim_self[j % 2][:, HALF * h:HALF * h + HALF]
                    pool.tensor_tensor(left, left, same, ALU.add).then_inc(left_sum, 1)
                    if j > 0 and h == 0:
                        keep_first(j - 1)
            keep_first(BB - 1)
            pool.wait_ge(amax_rdy, 3)
            pool.partition_all_reduce(amr[:, W2E:W2E + 1], amx[:, W2E:W2E + 1], P, RADD).then_inc(amax_all, 1)

            def up_half(n, first=False):
                for j in range(BB):
                    if first and j == BB - 1:
                        pool.wait_ge(amax_rdy, 4)
                        pool.partition_all_reduce(amr[:, WDN:WDN + 1], amx[:, WDN:WDN + 1], P, RADD)\
                            .then_inc(amax_all, 1)
                    products(n + 1, j)
                    if first and j == 0:
                        move_w2()
                if first:
                    for c in range(1, 4, 2):
                        dn_lo(c)
                pads(n + 1)
                if first:
                    for c in range(5, IT, 2):
                        dn_lo(c)
                    pool.wait_ge(gb_in, 32)
                    pool.tensor_scalar(gam, gam, th[:, 1:2], 1.0, ALU.mult, ALU.mult)
                    pool.tensor_scalar(bet, bet, th[:, 1:2], 1.0, ALU.mult, ALU.mult)
                    pool.drain()
                    for k in range(BB):
                        pool.tensor_tensor(home[:, k, :], home[:, k, :], bet, ALU.add)

            def down_half(n, phase_a):
                for j in range(BB if phase_a else BB - 1):
                    finish(n, j)
                    if phase_a:
                        keep(n + 1, j)

            up_half(0, first=True)
            down_half(0, True)
            with pool.Fori(1, NB - 1) as n:
                up_half(n)
                down_half(n, True)
            down_half(NB - 1, False)

        @block.scalar
        def _(act):
            def std(k, q):
                act.wait_ge(var_rdy[k], q + 1)
                act.activation(sd[:, k, 1:2], sd[:, k, 0:1], ACT.Sqrt).then_inc(std_rdy[k], 1)

            def norms(m):
                act.wait_ge(s0_rdy, m + 1)
                act.activation(nrm[:, 0:33], sums[:, 0:33], ACT.Sqrt).then_inc(nrm_rdy, 1)

            def f_pairs(m, j):
                first = isinstance(m, int) and m == 0
                q = BB * m + j
                b = j % 2 if first else 0
                act.wait_ge(rs_rdy[LX], q + 1)
                if first:
                    act.wait_ge(pads_rdy, 1)
                    if j >= 2:
                        act.wait_ge(f_rdy, j - 1)
                else:
                    act.wait_ge(part_rdy, m + 1)
                    if j > 0:
                        act.wait_ge(tr_done, 2 * q)
                        act.wait_ge(u_in[0], UIN * (q - 2))
                act.activation(scr[b], x_buf[j] if first else work[:, j % 2, :], ACT.Identity,
                               bias=rs[:, LX, 1:2] if not first else rs_x[:, 1, j:j + 1],
                               scale=rs[:, LX, 0:1] if not first else rs_x[:, 0, j:j + 1])
                act.drain()
                act.activation(fp[j if first else 0][:, 0, 1:T + 1], scr[b], ACT.Copy).then_inc(f_hi, 1)

            def x1_normal(m, j):
                first = isinstance(m, int) and m == 0
                q = BB * m + j
                act.wait_ge(rs_rdy[L1], q + 1)
                act.activation(scr[j % 2 if first else 0], x_buf[j] if first else work[:, j % 2, :],
                               ACT.Identity, bias=rs[:, L1, 1:2], scale=rs[:, L1, 0:1]).then_inc(xn_rdy, 1)

            def xt_his(m, j, h):
                bank = first_turn_bank(j, h) if isinstance(m, int) and m == 0 else psP[:, h, :]
                act.wait_ge(tr_done, 2 * (BB * m + j) + h + 1)
                act.activation(xT[:, 4 * h:4 * h + 4, 0, P * j:P * j + P],
                               bank.rearrange("p (k t) -> p k t", k=4), ACT.Copy).then_inc(xt_hi, 1)

            def finish(n, j):
                q = BB * n + j
                std(LY, q)
                act.wait_ge(rs_rdy[LY], q + 1)
                act.activation(y[:, :], y[:, :], ACT.Identity, bias=rs[:, LY, 1:2],
                               scale=rs[:, LY, 0:1]).then_inc(y_nrm, 1)
                act.wait_ge(y_fin, q + 1)
                act.dma_start(out[bass.ds(q, 1)].rearrange("o p t -> p (o t)"), y[:, :])\
                    .then_inc(out_done, 16)

            def take_s(n, j):
                act.wait_ge(s_done, BB * n + j + 1)
                if not (isinstance(n, int) and BB * n + j == 0):
                    act.wait_ge(out_done, 16 * (BB * n + j))
                act.activation(y[:, :], psS[:, :], ACT.Copy, scale=c_s).then_inc(s_evac, 1)

            def up_half(n, phase_a, first=False):
                m = n + 1
                for t in range(UT):
                    if first and t < NR:
                        for it in range(NR * t, NR * t + NR):
                            tile_hi(it)
                            if it > 0:
                                tile_out(it - 1)
                        if t == NR - 1:
                            tile_out(IT - 1)
                    if first and t == LT + 8:
                        for k in range(NR):
                            act.wait_ge(stg_out[k], 16 * (IT // NR))
                    act.wait_ge(up_done, UT * n + t + 1)
                    bank = up_bank[t % NR]
                    if t < LT:
                        act.activation(lat[:, t, 0, :], bank, ACT.Copy, scale=2.0 ** LAT_SHIFT)\
                            .then_inc(l_hi, 1)
                    else:
                        i = IT * n + t - LT
                        buf = hbuf[:, t % 2, :]
                        if t >= LT + 2:
                            act.wait_ge(h_rdy, i - 1)
                        act.activation(buf, bank, ACT.Relu, scale=2.0 ** HID_SHIFT).then_inc(relu_rdy, 1)
                        act.wait_ge(sq_hid, i + 1)
                        act.activation(hT[:, t - LT, 0, :], buf, ACT.Copy).then_inc(h_hi, 1)
                    if phase_a and t == SUMS_T + 1:
                        norms(m)
                    if phase_a and t == LNX_T:
                        std(LX, BB * m)
                    if first:
                        for c in range(*DN_LOAD.get(t, (0, 0))):
                            act.dma_start(dn_raw(c), w_down[P * c:P * c + P, :]).then_inc(dnraw_in[c], 16)
                        for l in range(*W2_SPLIT.get(t, (0, 0))):
                            w2_split_hi(l)
                        for c in range(*DN_SQUARE.get(t, (0, 0))):
                            if c == 0:
                                act.wait_ge(w2_rdy, LT)
                            act.wait_ge(dnraw_in[c], 16)
                            act.activation(hi_tmp[:, 0, :].bitcast(BF16), dn_raw(c), ACT.Square,
                                           accum_out=fro[:, LT + c:LT + c + 1])
                            act.drain().then_inc(dn_sq, 1)
                        for c in range(*DN_SPLIT.get(t, (0, 0))):
                            dn_split_hi(c)

            def w2_split_hi(l):
                act.wait_ge(scale_rdy, 4)
                if l >= 2:
                    act.wait_ge(w2_rdy, l - 1)
                act.activation(hi_tmp[:, l % 2, :], w2_raw[:, l, :], ACT.Copy, scale=wsc[:, W2E:W2E + 1])\
                    .then_inc(w2_hi, 1)

            def dn_split_hi(c):
                act.wait_ge(scale_rdy, 5)
                if c >= 2:
                    act.wait_ge(dn_rdy[c % 2], c // 2)
                act.activation(dn[:, c, HI, :], dn_raw(c), ACT.Copy, scale=wsc[:, WDN:WDN + 1])\
                    .then_inc(dn_hi, 1)

            def tile_hi(it):
                act.wait_ge(scale_rdy, 3)
                if it >= NR:
                    act.wait_ge(stg_out[it % NR], 16 * (it // NR))
                act.activation(staging[:, it % NR, 0, :, :], up_raw[:, :, P * it:P * it + P], ACT.Copy,
                               scale=wsc[:, WUP:WUP + 1]).then_inc(stg_hi, 1)

            def tile_out(it):
                act.wait_ge(stg_rdy, it + 1)
                act.dma_start(pair_dram[LT + it], staging[:, it % NR].rearrange("p s k i -> p (s k i)"))\
                    .then_inc(stg_out[it % NR], 16)

            def down_half(n, phase_a, first=False):
                m = n + 1
                for j in range(BB):
                    if phase_a:
                        f_pairs(m, j)
                    if first and j == 0:
                        for c in DN_LATE:
                            dn_split_hi(c)
                    if j > 0:
                        finish(n, j - 1)
                    if phase_a:
                        std(L1, BB * m + j)
                        x1_normal(m, j)
                        if j < BB - 1:
                            std(LX, BB * m + j + 1)
                    take_s(n, j)
                    if phase_a:
                        for h in range(2):
                            xt_his(m, j, h)
                if phase_a:
                    finish(n, BB - 1)
                else:
                    std(LY, B - 1)
                    act.wait_ge(rs_rdy[LY], B)
                    for h in range(2):
                        yh = y[:, HALF * h:HALF * h + HALF]
                        act.activation(yh, yh, ACT.Identity, bias=rs[:, LY, 1:2], scale=rs[:, LY, 0:1])\
                            .then_inc(nrm_half, 1)
                    for h in range(2):
                        act.wait_ge(fin_half, h + 1)
                        act.dma_start(out[B - 1][:, HALF * h:HALF * h + HALF], y[:, HALF * h:HALF * h + HALF])\
                            .then_inc(out_done, 16)

            def up_squares(k):
                n = UP_ORDER.index(k)
                act.wait_ge(upraw_in[k], 16)
                if n >= 2:
                    act.wait_ge(sq_used, n - 1)
                elif n == 1:
                    act.wait_ge(u_in[0], UIN)
                act.activation(squares[n % 2], up_raw[:, k, :], ACT.Square).then_inc(sq_rdy, 1)

            def w2_evac(l):
                act.wait_ge(w2_done, l + 1)
                if l == 2:
                    act.wait_ge(part_rdy, 1)
                act.activation(w2_raw[:, l, :], (psS if l % 2 == 0 else psR)[:, :], ACT.Copy)\
                    .then_inc(w2_out, 1)

            def w2_squares(l):
                act.drain()
                act.activation(squares[0][:, 0:T], w2_raw[:, l, :], ACT.Square, accum_out=fro[:, l:l + 1])
                act.drain().then_inc(w2_sq, 1)

            act.wait_ge(g_in, 32)
            act.activation(th[:, :], g_col[:, :], ACT.Tanh).then_inc(tanh_rdy, 1)

            def ctx_squares(j):
                act.wait_ge(prod1, j + 1)
                act.activation(ctx_first[:, j, :], ctx_first[:, j, :], ACT.Square).then_inc(prod0, 1)

            ctx_squares(0)
            act.wait_ge(var_rdy[LX], BB)
            act.activation(sd_x[:, 1, :], sd_x[:, 0, :], ACT.Sqrt).then_inc(std_rdy[LX], BB)
            ctx_squares(1)
            f_pairs(0, 0)
            ctx_squares(2)
            ctx_squares(3)
            for j in range(1, BB):
                f_pairs(0, j)
            act.wait_ge(s0_rdy, 1)
            act.activation(nrm_0[:, 0:P + 1], sums_0[:, 0, 0:P + 1], ACT.Sqrt).then_inc(nrm_rdy, 1)
            for k in range(LT):
                act.wait_ge(eT_done, k + 1)
                act.activation(ET[:, k, :], up_bank[k], ACT.Copy).then_inc(eT_rdy, 1)
            act.wait_ge(scale_rdy, 1)
            act.wait_ge(wxT_done, 1)
            act.activation(wx[:, :, 0, :], psM[:, 0:G * P].rearrange("p (g o) -> p g o", g=G), ACT.Copy,
                           scale=wsc[:, WX:WX + 1]).then_inc(wx_hi, 1)
            act.activation(gate[:, :, 0:NE], gate_raw, ACT.Copy, scale=wsc[:, WG:WG + 1]).then_inc(gate_hi, 1)
            act.wait_ge(f1_in, 16)
            act.activation(fc1_junk, fc1_raw, ACT.Square, accum_out=amx[:, WF1:WF1 + 1]).then_inc(amax_rdy, 1)
            w2_evac(0)
            act.wait_ge(scale_rdy, 2)
            act.wait_ge(part_rdy, 1)
            for t in range(LT):
                act.activation(fc1_staging[:, t, 0], fc1_raw[:, :, P * t:P * t + P], ACT.Copy,
                               scale=wsc[:, WF1:WF1 + 1]).then_inc(fc1_hi, 1)
            for t in range(LT):
                act.wait_ge(fc1_rdy, t + 1)
                act.dma_start(pair_dram[t], fc1_staging[:, t].rearrange("p s k i -> p (s k i)"))\
                    .then_inc(fc1_out[t], 16)
            w2_evac(1)
            for j in range(BB):
                for k in UP_SQ[j]:
                    up_squares(k)
                std(L1, j)
                x1_normal(0, j)
                if j == 0:
                    for t in range(LT):
                        act.wait_ge(fc1_out[t], 16)
                for l in W2_WITH[j]:
                    w2_evac(l)
                xt_his(0, j, 0)
                for k in UP_SQ_MID[j]:
                    up_squares(k)
                xt_his(0, j, 1)
                for l in W2_SQ[j]:
                    w2_squares(l)
            act.wait_ge(tr_done, 2 * BB)
            act.wait_ge(rs_rdy[L1], BB)
            for b in range(2):
                act.wait_ge(u_in[b], 2 * UIN)
            act.wait_ge(home_rdy, BB)

            up_half(0, True, first=True)
            down_half(0, True, first=True)
            with act.Fori(1, NB - 1) as n:
                up_half(n, True)
                down_half(n, True)
            up_half(NB - 1, False)
            down_half(NB - 1, False)

        @block.vector
        def _(dve):
            def half_stats(k, src, h):
                dve.bn_stats(st[:, k, h, :], src[:, HALF * h:HALF * h + HALF])

            def stats(k, src, mvk, sdk, halves=(0, 1)):
                for h in halves:
                    half_stats(k, src, h)
                dve.drain()
                dve.bn_aggr(mvk, st[:, k, :, :].rearrange("p h s -> p (h s)"))
                dve.drain()
                dve.tensor_scalar(sdk[:, 0:1], mvk[:, 1:2], LN_EPS, None, ALU.add).then_inc(var_rdy[k], 1)

            def scale_bias(k, q, scale, mvk, sdk, rsk):
                dve.wait_ge(std_rdy[k], q + 1)
                dve.reciprocal(sdk[:, 2:3], sdk[:, 1:2])
                dve.drain()
                dve.tensor_scalar(sdk[:, 3:4], sdk[:, 2:3], sdk[:, 2:3], sdk[:, 0:1], ALU.mult, ALU.mult)
                dve.drain()
                dve.tensor_scalar(sdk[:, 3:4], sdk[:, 3:4], -0.5, 1.5, ALU.mult, ALU.add)
                dve.drain()
                dve.scalar_tensor_tensor(out=rsk[:, 0:1], in0=sdk[:, 2:3], scalar=scale,
                                         in1=sdk[:, 3:4], op0=ALU.mult, op1=ALU.mult)
                dve.drain()
                dve.scalar_tensor_tensor(out=rsk[:, 1:2], in0=mvk[:, 0:1], scalar=-1.0,
                                         in1=rsk[:, 0:1], op0=ALU.mult, op1=ALU.mult)
                dve.drain().then_inc(rs_rdy[k], 1)

            def normalise(k, q, src, scale, halves=(0, 1)):
                stats(k, src, mv[:, k, :], sd[:, k, :], halves)
                scale_bias(k, q, scale, mv[:, k, :], sd[:, k, :], rs[:, k, :])

            def sum_products(m, j, which):
                q = BB * m + j
                if which == 1:
                    dve.wait_ge(prod1, q + 1)
                    if j == 0 and not (isinstance(m, int) and m == 1):
                        dve.wait_ge(out_done, 16 * BB * (m - 1))
                    src = sides_a[:, 0:T]
                else:
                    dve.wait_ge(prod0, q + 1)
                    src = scr[0]
                dve.transpose(y[:, :], src).then_inc(prod_used, 1)
                dve.drain()
                dve.tensor_reduce(part[:, which, CH * j:CH * j + CH],
                                  y[:, :].rearrange("p (c a) -> p c a", a=32), AX.X, ALU.add)
                if which == 0 and j == BB - 1:
                    dve.drain().then_inc(part_rdy, 1)
                else:
                    dve.drain()

            def cosines(m):
                dve.wait_ge(sums_done, m + 1)
                dve.tensor_copy(sums[:, 0:65], psM[:, 0:65])
                dve.drain().then_inc(s0_rdy, 1)
                dve.wait_ge(nrm_rdy, m + 1)
                a, b, c = nrm[:, 0:33], nt[:, 0, 0:33], nt[:, 1, 0:33]
                dve.tensor_scalar(a, a, COS_EPS, None, ALU.max)
                dve.drain()
                dve.reciprocal(b, a)
                dve.drain()
                dve.tensor_tensor(c, sums[:, 0:33], b, ALU.mult)
                dve.drain()
                dve.tensor_tensor(a, a, c, ALU.add)
                dve.drain()
                dve.tensor_scalar(a, a, 0.5, COS_EPS, ALU.mult, ALU.max)
                dve.drain()
                dve.tensor_tensor(nt[:, 0, 0:32], nrm[:, 0:32], nrm[:, 1:33], ALU.mult)
                dve.tensor_tensor(nt[:, 1, 0:32], nrm[:, 0:32], nrm[:, 0:32], ALU.mult)
                dve.drain()
                dve.reciprocal(nt[:, :, 0:32], nt[:, :, 0:32])
                dve.drain()
                dve.wait_ge(simrow_out, 32 * m)
                dve.tensor_tensor(simo[:, 0, :], sums[:, 33:65], nt[:, 0, 0:32], ALU.mult)
                dve.tensor_tensor(simo[:, 1, :], sums[:, 0:32], nt[:, 1, 0:32], ALU.mult)
                dve.drain().then_inc(simo_rdy, 1)

            def first_cosines():
                dve.wait_ge(sums_done, 1)
                for s in range(2):
                    dve.tensor_copy(sums_0[:, s, 0:P], psP[0:NR0, s, 0:P])
                dve.drain().then_inc(first_col_rdy, 1)
                dve.drain().then_inc(part_rdy, 1)
                dve.wait_ge(next_col_done, 1)
                dve.tensor_copy(sums_0[:, 0, P:P + 1], psP[0:NR0, 2, 0:1])
                dve.drain().then_inc(s0_rdy, 1)
                dve.wait_ge(nrm_rdy, 1)
                n = nrm_0[:, 0:P + 1]
                dve.tensor_scalar(n, n, COS_EPS, None, ALU.max)
                dve.drain()
                dve.reciprocal(nt_0[:, 0, 0:P + 1], n)
                dve.drain()
                dve.tensor_tensor(nt_0[:, 1, 0:P + 1], sums_0[:, 0, 0:P + 1], nt_0[:, 0, 0:P + 1], ALU.mult)
                dve.drain()
                dve.tensor_tensor(n, n, nt_0[:, 1, 0:P + 1], ALU.add)
                dve.drain()
                dve.tensor_scalar(n, n, 0.5, COS_EPS, ALU.mult, ALU.max)
                dve.drain()
                dve.tensor_tensor(nt_0[:, 1, 0:P], nrm_0[:, 0:P], nrm_0[:, 1:P + 1], ALU.mult)
                dve.tensor_tensor(nt_0[:, 0, 0:P], nrm_0[:, 0:P], nrm_0[:, 0:P], ALU.mult)
                dve.drain()
                dve.reciprocal(nt_0[:, :, 0:P], nt_0[:, :, 0:P])
                dve.drain()
                dve.tensor_tensor(sums_0[:, :, 0:P], sums_0[:, :, 0:P], nt_0[:, :, 0:P], ALU.mult)
                dve.drain().then_inc(simo_rdy, 1)

            def f_los(m, j):
                dve.wait_ge(f_hi, BB * m + j + 1)
                dve.tensor_tensor(fp[0][:, 1, 1:T + 1], scr[0], fp[0][:, 0, 1:T + 1], ALU.subtract)\
                    .then_inc(f_rdy, 1)

            def fc1_los():
                for t in range(LT):
                    dve.wait_ge(fc1_hi, t + 1)
                    dve.scalar_tensor_tensor(out=fc1_staging[:, t, 1], in0=fc1_raw[:, :, P * t:P * t + P],
                                             scalar=wsc[:, WF1:WF1 + 1], in1=fc1_staging[:, t, 0],
                                             op0=ALU.mult, op1=ALU.subtract).then_inc(fc1_rdy, 1)

            def combine(m, j):
                first = isinstance(m, int) and m == 0
                q = BB * m + j
                xr = x_buf[j] if first else work[:, j % 2, :]
                b = j % 2 if first else 0
                if first:
                    dve.wait_ge(sim_in[b], 32 * (j // 2 + 1))
                else:
                    dve.wait_ge(sim_in[0], 32 * (q - 1))
                for h in range(2):
                    t0 = HALF * h
                    dve.wait_ge(p_done, 2 * q + h + 1)
                    xh = xr[:, t0:t0 + HALF]
                    left, right = scr[b][:, 0:HALF], scr[b][:, HALF:T]
                    same = sim_self[b][:, t0:t0 + HALF]
                    dve.scalar_tensor_tensor(out=left, in0=psP[:, 0, :], scalar=c_x,
                                             in1=sim_side[b][:, t0:t0 + HALF], op0=ALU.mult, op1=ALU.mult)
                    dve.scalar_tensor_tensor(out=same, in0=psP[:, 1, :], scalar=c_x, in1=same,
                                             op0=ALU.mult, op1=ALU.mult)
                    dve.scalar_tensor_tensor(out=right, in0=psP[:, 2, :], scalar=c_x,
                                             in1=sim_side[b][:, t0 + 1:t0 + HALF + 1], op0=ALU.mult,
                                             op1=ALU.mult)
                    dve.drain().then_inc(comb, 1)
                    if not first:
                        dve.tensor_tensor(left, left, same, ALU.add)
                    dve.tensor_tensor(xh, xh, right, ALU.add)
                    if first and j > 0:
                        xt_los(0, j - 1, (h,))
                    dve.drain()
                    if first:
                        dve.wait_ge(left_sum, 2 * j + h + 1)
                    dve.tensor_tensor(xh, xh, left, ALU.add)
                    dve.drain()
                    half_stats(L1, xr, h)
                    if first and j == 0 and h == 0:
                        fc1_los()
                normalise(L1, q, xr, 2.0 ** LOG_ACT, ())

            def x_stats(m, j):
                dve.wait_ge(x_in[j % 2], (2 * m + j // 2) * 16)
                normalise(LX, BB * m + j, work[:, j % 2, :], 2.0 ** LOG_ACT)

            def x_stats_first():
                for j in range(BB):
                    dve.wait_ge(x_in[j] if j < 2 else x_tail_in[j - 2], 16)
                    for h in range(2):
                        dve.bn_stats(st_x[:, j, h, :], x_buf[j][:, HALF * h:HALF * h + HALF])
                dve.drain()
                for j in range(BB):
                    dve.bn_aggr(mv_x[:, j, :], st_x[:, j, :, :].rearrange("p h s -> p (h s)"))
                dve.drain()
                v, s, r, c = (sd_x[:, k, :] for k in range(4))
                dve.tensor_scalar(v, mv_x[:, :, 1], LN_EPS, None, ALU.add)
                dve.drain().then_inc(var_rdy[LX], BB)
                dve.wait_ge(std_rdy[LX], BB)
                dve.reciprocal(r, s)
                dve.drain()
                dve.tensor_tensor(c, r, r, ALU.mult)
                dve.drain()
                dve.tensor_tensor(c, c, v, ALU.mult)
                dve.drain()
                dve.tensor_scalar(c, c, -0.5, 1.5, ALU.mult, ALU.add)
                dve.drain()
                dve.scalar_tensor_tensor(out=rs_x[:, 0, :], in0=r, scalar=2.0 ** LOG_ACT, in1=c,
                                         op0=ALU.mult, op1=ALU.mult)
                dve.drain()
                dve.scalar_tensor_tensor(out=rs_x[:, 1, :], in0=mv_x[:, :, 0], scalar=-1.0,
                                         in1=rs_x[:, 0, :], op0=ALU.mult, op1=ALU.mult)
                dve.drain().then_inc(rs_rdy[LX], BB)

            def xt_los(m, j, halves=(0, 1)):
                for h in halves:
                    bank = first_turn_bank(j, h) if isinstance(m, int) and m == 0 else psP[:, h, :]
                    dve.wait_ge(xt_hi, 2 * (BB * m + j) + h + 1)
                    dst = xT[:, 4 * h:4 * h + 4, :, P * j:P * j + P]
                    dve.tensor_tensor(dst[:, :, 1, :], bank.rearrange("p (k t) -> p k t", k=4),
                                      dst[:, :, 0, :], ALU.subtract).then_inc(xt_rdy, 1)

            def pow2(lo, hi, src, mult, add):
                dve.tensor_scalar(src, src, 2.0 ** -80, None, ALU.max)
                dve.drain()
                dve.tensor_scalar(wexp[:, lo:hi], src.bitcast(I32), mult, add, ALU.mult, ALU.add)
                dve.drain()
                dve.tensor_scalar(wsc[:, lo:hi].bitcast(I32), wexp[:, lo:hi], -2.0 ** 23,
                                  (254 + LOG_W) * 2.0 ** 23, ALU.mult, ALU.add)
                dve.tensor_scalar(wp[:, lo:hi].bitcast(I32), wexp[:, lo:hi], 2.0 ** 23, None, ALU.mult)
                dve.drain()

            def take_r(n, j):
                q = BB * n + j
                dve.wait_ge(r_done, q + 1)
                dve.wait_ge(s_evac, q + 1)
                dve.scalar_tensor_tensor(out=y[:, :], in0=psR[:, :], scalar=rw[:, j:j + 1], in1=y[:, :],
                                         op0=ALU.mult, op1=ALU.add).then_inc(r_evac, 1)

            def y_stats(n, j):
                dve.drain()
                normalise(LY, BB * n + j, y, 1.0)

            def routing(n):
                dve.wait_ge(gate_done, n + 1)
                lgp = psM[:, 128:128 + BB * 2 * NE].rearrange("p (j s e) -> p j s e", j=BB, s=2)
                dve.tensor_copy(lg[:, :, :], lgp[:, :, 0, :])
                dve.drain()
                dve.tensor_tensor(lg[:, :, :], lg[:, :, :], lgp[:, :, 1, :], ALU.add)
                dve.drain().then_inc(rw_rdy, 1)
                for j in range(BB):
                    dve.max(top[:, j, :], lg[:, j, :])
                dve.drain()
                dve.tensor_tensor(rw[:, :], top[:, :, 0], top[:, :, 1], ALU.add)
                dve.drain()
                dve.tensor_scalar(rw[:, :], rw[:, :], c_r, None, ALU.mult)
                dve.drain()

            def w2_split_lo(l):
                dve.wait_ge(w2_hi, l + 1)
                dve.scalar_tensor_tensor(out=w2[:, l, LO, :], in0=w2_raw[:, l, :], scalar=wsc[:, W2E:W2E + 1],
                                         in1=hi_tmp[:, l % 2, :], op0=ALU.mult, op1=ALU.subtract)\
                    .then_inc(w2_lo, 1)

            def dn_lo(c):
                dve.wait_ge(dn_hi, c + 1)
                dve.scalar_tensor_tensor(out=dn[:, c, LO, :], in0=dn_raw(c), scalar=wsc[:, WDN:WDN + 1],
                                         in1=dn[:, c, HI, :], op0=ALU.mult, op1=ALU.subtract)\
                    .then_inc(dn_rdy[0], 1)

            def tile_lo(it):
                dve.wait_ge(stg_hi, it + 1)
                dve.scalar_tensor_tensor(out=staging[:, it % NR, 1, :, :], in0=up_raw[:, :, P * it:P * it + P],
                                         scalar=wsc[:, WUP:WUP + 1], in1=staging[:, it % NR, 0, :, :],
                                         op0=ALU.mult, op1=ALU.subtract).then_inc(stg_rdy, 1)

            def norm_sum(k, c0, c1):
                dve.tensor_reduce(amx[:, k:k + 1], fro[:, c0:c1], AX.X, ALU.add)
                dve.drain().then_inc(amax_rdy, 1)

            def norm_scale(k, turn):
                dve.wait_ge(amax_all, turn)
                pow2(k, k + 1, amr[:, k:k + 1], 2.0 ** -24, 63.5)

            def up_half(n, phase_a, first=False):
                m = n + 1
                for t in range(UT):
                    bank = up_bank[t % NR]
                    if first and t < NR:
                        for it in range(NR * t, NR * t + NR):
                            tile_lo(it)
                    if t < LT:
                        dve.wait_ge(l_hi, LT * n + t + 1)
                        dve.scalar_tensor_tensor(out=lat[:, t, 1, :], in0=bank, scalar=2.0 ** LAT_SHIFT,
                                                 in1=lat[:, t, 0, :], op0=ALU.mult, op1=ALU.subtract)\
                            .then_inc(up_evac, 1)
                    else:
                        i = IT * n + t - LT
                        dve.wait_ge(relu_rdy, i + 1)
                        dve.scalar_tensor_tensor(out=hbuf[:, t % 2, :], in0=bank, scalar=0.0,
                                                 in1=hbuf[:, t % 2, :], op0=ALU.max, op1=ALU.mult)
                        dve.drain().then_inc(up_evac, 1)
                        dve.drain().then_inc(sq_hid, 1)
                    for j in range(BB if phase_a else 0):
                        if t in (sim_tile(first, j), sim_tile(first, j) + 1):
                            sum_products(m, j, 1 if t == sim_tile(first, j) else 0)
                    if t >= LT:
                        dve.wait_ge(h_hi, i + 1)
                        dve.tensor_tensor(hT[:, t - LT, 1, :], hbuf[:, t % 2, :], hT[:, t - LT, 0, :],
                                          ALU.subtract).then_inc(h_rdy, 1)
                    if phase_a and t == SUMS_T + 1:
                        cosines(m)
                    if phase_a and t == LNX_T:
                        x_stats(m, 0)
                    if first and t == SCALE_T - 1:
                        dve.wait_ge(dn_sq, IT)
                        norm_sum(WDN, LT, LT + IT)
                    if first and t == SCALE_T:
                        norm_scale(WDN, 4)
                        dve.tensor_scalar(coef[:, 4:5], wp[:, WUP:WUP + 1], wp[:, WUP:WUP + 1],
                                          wp[:, WDN:WDN + 1], ALU.mult, ALU.mult)
                        dve.drain()
                        dve.tensor_scalar(c_s, coef[:, 4:5], 2.0 ** -17, None, ALU.mult)
                        dve.drain().then_inc(scale_rdy, 1)
                    if first:
                        for l in range(*W2_SPLIT.get(t, (0, 0))):
                            w2_split_lo(l)
                        for c in range(*DN_SPLIT.get(t, (0, 0))):
                            if c % 2 == 0:
                                dn_lo(c)
                routing(n)

            def down_half(n, phase_a, first=False):
                m = n + 1
                for j in range(BB):
                    if phase_a:
                        f_los(m, j)
                    if first and j == 0:
                        for c in DN_LATE:
                            if c % 2 == 0:
                                dn_lo(c)
                    if j > 0:
                        y_stats(n, j - 1)
                    if phase_a:
                        combine(m, j)
                        if j < BB - 1:
                            x_stats(m, j + 1)
                    if phase_a:
                        xt_los(m, j)
                    if phase_a or j < BB - 1:
                        take_r(n, j)
                    else:
                        last_rows()
                if phase_a:
                    y_stats(n, BB - 1)

            def last_rows():
                j = BB - 1
                dve.wait_ge(s_evac, B)
                for h in range(2):
                    yh = y[:, HALF * h:HALF * h + HALF]
                    dve.wait_ge(r_half, h + 1)
                    dve.scalar_tensor_tensor(out=yh, in0=psR[:, HALF * h:HALF * h + HALF],
                                             scalar=rw[:, j:j + 1], in1=yh, op0=ALU.mult, op1=ALU.add)
                    dve.drain()
                    half_stats(LY, y, h)
                normalise(LY, B - 1, y, 1.0, ())
                for h in range(2):
                    cols = slice(HALF * h, HALF * h + HALF)
                    dve.wait_ge(nrm_half, h + 1)
                    dve.tensor_tensor(y[:, cols], y[:, cols], gam[:, cols], ALU.mult)
                    dve.drain()
                    dve.tensor_tensor(y[:, cols], y[:, cols], home[:, j, cols], ALU.add)
                    dve.drain().then_inc(fin_half, 1)

            x_stats_first()
            dve.wait_ge(small_in, 32)
            dve.tensor_reduce(amx[:, WX:WX + 1], wx_raw, AX.X, ALU.max, apply_absolute_value=True)
            dve.tensor_reduce(amx[:, WG:WG + 1], gate_raw, AX.XY, ALU.max, apply_absolute_value=True)
            dve.drain().then_inc(amax_rdy, 1)
            dve.wait_ge(amax_all, 1)
            pow2(WX, WG + 1, amr[:, WX:WG + 1], 2.0 ** -23, 0.0)
            dve.drain().then_inc(scale_rdy, 1)
            dve.wait_ge(tanh_rdy, 1)
            dve.tensor_scalar(c_x, wp[:, WX:WX + 1], th[:, 0:1], 2.0 ** -(LOG_ACT + LOG_W), ALU.mult, ALU.mult)
            first_cosines()
            dve.wait_ge(wx_hi, 1)
            dve.scalar_tensor_tensor(out=wx[:, :, 1, :], in0=psM[:, 0:G * P].rearrange("p (g o) -> p g o", g=G),
                                     scalar=wsc[:, WX:WX + 1], in1=wx[:, :, 0, :], op0=ALU.mult,
                                     op1=ALU.subtract).then_inc(wx_rdy, 1)
            dve.wait_ge(gate_hi, 1)
            dve.scalar_tensor_tensor(out=gate[:, :, NE:2 * NE], in0=gate_raw, scalar=wsc[:, WG:WG + 1],
                                     in1=gate[:, :, 0:NE], op0=ALU.mult, op1=ALU.subtract)\
                .then_inc(gate_w_rdy, 1)
            dve.wait_ge(amax_all, 2)
            pow2(WF1, WF1 + 1, amr[:, WF1:WF1 + 1], 2.0 ** -24, 63.5)
            dve.drain().then_inc(scale_rdy, 1)
            for j in range(BB):
                combine(0, j)
            dve.wait_ge(sq_used, KB)
            dve.tensor_reduce(amx[:, 6:7], psS[:, :], AX.X, ALU.max)
            dve.tensor_reduce(amx[:, 7:8], psR[:, :], AX.X, ALU.max)
            dve.drain().then_inc(norms_read, 1)
            dve.tensor_tensor(amr[:, WUP:WUP + 1], amx[:, 6:7], amx[:, 7:8], ALU.max)
            dve.drain()
            pow2(WUP, WUP + 1, amr[:, WUP:WUP + 1], 2.0 ** -24, 63.5)
            dve.drain().then_inc(scale_rdy, 1)
            xt_los(0, BB - 1)
            dve.wait_ge(w2_sq, LT)
            norm_sum(W2E, 0, LT)
            norm_scale(W2E, 3)
            dve.tensor_scalar(coef[:, 5:6], wp[:, WF1:WF1 + 1], wp[:, W2E:W2E + 1], wp[:, WG:WG + 1],
                              ALU.mult, ALU.mult)
            dve.drain()
            dve.tensor_scalar(c_r, coef[:, 5:6], 2.0 ** -(2 * LOG_ACT + 3 * LOG_W + LAT_SHIFT), None, ALU.mult)
            dve.drain().then_inc(scale_rdy, 1)
            up_half(0, True, first=True)
            down_half(0, True, first=True)
            with dve.Fori(1, NB - 1) as n:
                up_half(n, True)
                down_half(n, True)
            up_half(NB - 1, False)
            down_half(NB - 1, False)

        @block.tensor
        def _(pe):
            def quadrant_sums(m):
                pe.wait_ge(part_rdy, m + 1)
                n = BB * CH
                pe.matmul(psM[:, 0:32], part[:, 0, 0:n], fold[:, :], start=True, stop=True)
                pe.matmul(psM[:, 32:33], part[:, 0, 1:n + 1], fold[:, 0:1], start=True, stop=True)
                pe.matmul(psM[:, 33:65], part[:, 1, 0:n], fold[:, :], start=True, stop=True)\
                    .then_inc(sums_done, 1)

            def first_sums(j):
                for s in (1, 0):
                    pe.wait_ge(prod1 if s == 1 else prod0, j + 1)
                    src = prod_first[j % 2] if s == 1 else ctx_first[:, j, :]
                    for k in range(KB):
                        row = KB * j + k
                        mm = pe.matmul(psP[0:NR0, s, 0:P], pick[:, NR0 - 1 - row:2 * NR0 - 1 - row],
                                       src[:, P * k:P * k + P], start=(row == 0), stop=(row == NR0 - 1),
                                       skip_group_check=True)
                    mm.then_inc(prod_used, 1)

            def xattn(m, j, h):
                first = isinstance(m, int) and m == 0
                q = BB * m + j
                b = j % 2 if first else 0
                if h == 1:
                    pe.wait_ge(comb, 2 * q + 1)
                elif first:
                    pe.wait_ge(u_in[b], UIN * (j // 2 + 1))
                    if j == 0:
                        pe.wait_ge(wx_rdy, 1)
                        pe.wait_ge(s0_rdy, 1)
                    if j > 0:
                        pe.wait_ge(comb, 2 * j)
                else:
                    pe.wait_ge(u_in[0], UIN * (q - 1))
                    pe.wait_ge(xt_rdy, 2 * q)
                t0 = HALF * h
                for g in range(G):
                    for n, (w, v) in enumerate(((0, 0), (0, 1), (1, 0))):
                        mm = pe.matmul(psP[:, g, :], wx[:, g, w, :], U[b][:, g, v, t0:t0 + HALF],
                                       start=(n == 0), stop=(n == 2))
                mm.then_inc(p_done, 1)

            def turn(m, j):
                pe.wait_ge(xn_rdy, BB * m + j + 1)
                for h in range(2):
                    for k in range(4):
                        mm = pe.transpose(psP[:, h, P * k:P * k + P],
                                          scr[0][:, P * (4 * h + k):P * (4 * h + k) + P], ident[:, :])
                    mm.then_inc(tr_done, 1)

            def turn_first(j, h):
                pe.wait_ge(xn_rdy, j + 1)
                if j == BB - 1 and h == 1:
                    pe.wait_ge(comb, 2 * BB)
                elif j > 0 or h > 0:
                    pe.wait_ge(xt_rdy, 2 * j + h)
                for k in range(4):
                    mm = pe.transpose(first_turn_bank(j, h)[:, P * k:P * k + P],
                                      scr[j % 2][:, P * (4 * h + k):P * (4 * h + k) + P], ident[:, :])
                mm.then_inc(tr_done, 1)

            def up_half(n, phase_a):
                m = n + 1
                pe.wait_ge(xt_rdy, 2 * BB * m)
                for t in range(UT):
                    pe.wait_ge(ring_in[t % NR], 16 * (n * (UT // NR) + t // NR + 1))
                    if t >= NR:
                        pe.wait_ge(up_evac, UT * n + t - NR + 1)
                    elif not (isinstance(n, int) and n == 0):
                        pe.wait_ge(s_evac if t < 2 else r_evac, BB * n)
                    for k in range(KB):
                        for a, b in ((0, 0), (0, 1), (1, 0)):
                            mm = pe.matmul(up_bank[t % NR], ring[:, t % NR, a, k, :], xT[:, k, b, :],
                                           start=(k == 0 and a == 0 and b == 0),
                                           stop=(k == KB - 1 and a == 1))
                    mm.then_inc(up_done, 1)
                    if phase_a and t == SUMS_T:
                        if not (isinstance(n, int) and n == 0):
                            pe.wait_ge(rw_rdy, n)
                        quadrant_sums(m)
                if phase_a:
                    pe.wait_ge(simo_rdy, m + 1)
                for j in range(BB):
                    c0 = 128 + 2 * NE * j
                    for k in range(KB):
                        pe.matmul(psM[:, c0:c0 + 2 * NE], xT[:, k, 0, P * j:P * j + P], gate[:, k, :],
                                  start=(k == 0), stop=False, skip_group_check=True)
                        mm = pe.matmul(psM[:, c0:c0 + NE], xT[:, k, 1, P * j:P * j + P], gate[:, k, 0:NE],
                                       start=False, stop=(k == KB - 1), skip_group_check=True)
                mm.then_inc(gate_done, 1)

            def shared(j, i0, i1, first=False):
                for i in range(i0, i1):
                    if first:
                        pe.wait_ge(dn_rdy[i % 2], i // 2 + 1)
                    for a, b in ((0, HI), (0, LO), (1, HI)):
                        for h in range(2):
                            mm = pe.matmul(psS[:, HALF * h:HALF * h + HALF], hT[:, i, a, P * j:P * j + P],
                                           dn[:, i, b, HALF * h:HALF * h + HALF],
                                           start=(i == 0 and a == 0 and b == HI),
                                           stop=(i == IT - 1 and a == 1))
                return mm

            def routed(j, l0, l1, halves=(0, 1)):
                for l in range(l0, l1):
                    for a, b in ((0, HI), (0, LO), (1, HI)):
                        for h in halves:
                            mm = pe.matmul(psR[:, HALF * h:HALF * h + HALF], lat[:, l, a, P * j:P * j + P],
                                           w2[:, l, b, HALF * h:HALF * h + HALF],
                                           start=(l == 0 and a == 0 and b == HI),
                                           stop=(l == LT - 1 and a == 1))
                return mm

            def down_half(n, phase_a, first=False):
                m = n + 1
                for j in range(BB):
                    q = BB * n + j
                    if j == 0:
                        pe.wait_ge(up_evac, UT * (n + 1) - 2)
                        pe.wait_ge(h_rdy, IT * (n + 1) - 2)
                        if first:
                            pe.wait_ge(w2_rdy, LT)
                    else:
                        pe.wait_ge(s_evac, q)
                    cuts = S_CUTS if j > 0 else (S_CUTS_00 if first else S_CUTS_0)
                    shared(j, 0, cuts[0], first and j == 0)
                    if phase_a:
                        xattn(m, j, 0)
                    shared(j, *cuts, first and j == 0)
                    if phase_a:
                        xattn(m, j, 1)
                    if j == 0:
                        pe.wait_ge(h_rdy, IT * (n + 1))
                    shared(j, cuts[1], IT, first and j == 0).then_inc(s_done, 1)
                    if j > 0:
                        pe.wait_ge(r_evac, q)
                    else:
                        pe.wait_ge(up_evac, UT * (n + 1))
                    if not phase_a and j == BB - 1:
                        for h in range(2):
                            routed(j, 0, LT, (h,)).then_inc(r_half, 1)
                        continue
                    routed(j, 0, LT - 1)
                    if phase_a:
                        turn(m, j)
                    routed(j, LT - 1, LT).then_inc(r_done, 1)

            pe.wait_ge(const_rdy, 1)
            for j in range(BB):
                first_sums(j)
            pe.drain().then_inc(sums_done, 1)
            pe.wait_ge(small_in, 32)
            for g in range(G):
                mm = pe.transpose(psM[:, P * g:P * g + P], wx_raw[:, P * g:P * g + P], ident[:, :])
            mm.then_inc(wxT_done, 1)
            pe.wait_ge(first_col_rdy, 1)
            pe.matmul(psP[0:NR0, 2, 0:1], ident[0:NR0, 1:NR0 + 1], sums_0[:, 0, 0:1], start=True, stop=True)\
                .then_inc(next_col_done, 1)
            pe.wait_ge(e_in, 16)
            for k in range(LT):
                for l in range(LT):
                    mm = pe.transpose(up_bank[k][:, P * l:P * l + P], e_raw[:, l, P * k:P * k + P], ident[:, :])
                mm.then_inc(eT_done, 1)

            def expert_fc2(l):
                pe.wait_ge(eT_rdy, LT)
                pe.wait_ge(f2_in, 16)
                if l >= 2:
                    pe.wait_ge(w2_out, l - 1)
                acc = psS if l % 2 == 0 else psR
                for k in range(LT):
                    for h in range(2):
                        mm = pe.matmul(acc[:, HALF * h:HALF * h + HALF], ET[:, k, P * l:P * l + P],
                                       fc2_raw[:, k, HALF * h:HALF * h + HALF],
                                       start=(k == 0), stop=(k == LT - 1))
                mm.then_inc(w2_done, 1)

            def column_norms(k):
                n = UP_ORDER.index(k)
                pe.wait_ge(sq_rdy, n + 1)
                if n == 0:
                    pe.wait_ge(w2_out, LT)
                for b in range(4):
                    mm = pe.matmul(up_bank[b], ones_b[:, :], squares[n % 2][:, 512 * b:512 * b + 512],
                                   start=(n == 0), stop=(n == KB - 1), skip_group_check=True)
                mm.then_inc(sq_used, 1)

            expert_fc2(0)
            xattn(0, 0, 0)
            expert_fc2(1)
            xattn(0, 0, 1)
            expert_fc2(2)
            for j in range(BB):
                if j < BB - 1:
                    xattn(0, j + 1, 0)
                for k in UP_SQ[j]:
                    column_norms(k)
                turn_first(j, 0)
                if j < BB - 1:
                    xattn(0, j + 1, 1)
                for k in UP_SQ_MID[j]:
                    column_norms(k)
                turn_first(j, 1)
                if j == 0:
                    expert_fc2(3)
            pe.wait_ge(gate_w_rdy, 1)
            pe.wait_ge(norms_read, 1)
            up_half(0, True)
            down_half(0, True, first=True)
            with pe.Fori(1, NB - 1) as n:
                up_half(n, True)
                down_half(n, True)
            up_half(NB - 1, False)
            down_half(NB - 1, False)


_INS = ["x", "ctx_4096", "g_xattn", "g_ffn", "L0_xattn_weight", "L0_ffn_gate_w", "L0_ffn_up_w",
        "L0_ffn_down_w", "L0_ffn_fc1_w", "L0_ffn_fc2_w", "L0_ffn_expert_w", "L0_ffn_ln_gamma",
        "L0_ffn_ln_beta"]


def kernel(**inputs):
    import numpy as np
    import concourse.bacc as bacc
    from concourse.bass_utils import run_bass_kernel_spmd as run

    nc = bacc.Bacc("TRN2", target_bir_lowering=False, num_devices=1)
    arrays, args = {}, []
    for name in _INS:
        a = np.ascontiguousarray(inputs[name])
        arrays[f"in_{name}"] = a
        args.append(nc.dram_tensor(f"in_{name}", a.shape, mybir.dt.from_np(a.dtype), kind="ExternalInput").ap())
    out = nc.dram_tensor("out_rows", tuple(inputs["x"].shape), F32, kind="ExternalOutput").ap()
    flamingo_block(nc, *args, out)
    r = run(nc, [arrays], core_ids=[0])
    return r.results[0]["out_rows"]
```
